# Optimizing a Trainium2 kernel written in Bass

```python
import numpy as np
import jax
import jax.numpy as jnp

def _softmax(x, axis=-1):
    return jax.nn.softmax(x, axis=axis)

def _gelu(x):
    return jax.nn.gelu(x, approximate=True)

def _silu(x):
    return jax.nn.silu(x)

def _sigmoid(x):
    return jax.nn.sigmoid(x)

def _layernorm(x, axis=-1, eps=1e-05):
    m = jnp.mean(x, axis=axis, keepdims=True)
    v = jnp.var(x, axis=axis, keepdims=True)
    return (x - m) / jnp.sqrt(v + eps)

def _scatter_add(tgt, idx, src, axis=0):
    return tgt.at[idx].add(src)

def _segment_sum(src, seg, n):
    return jax.ops.segment_sum(src, seg, n)
kernel_name = 'mk_xattn_seq_d4_seqx_r8_592f67'

def setup_inputs(seed: int=0):
    np.random.seed(seed)
    _w = jnp.asarray

    def _rec_inputs():
        import jax
        import jax.numpy as jnp
        _rk = jax.random.key(seed)
        x = -0.0005207 + 1.001 * jax.random.normal(jax.random.fold_in(_rk, 1), (32, 64, 256), jnp.float32)
        _lenS = 64 - jax.random.randint(jax.random.fold_in(_rk, 7), (32,), 0, max(1, 64 // 4) + 1, jnp.int32)
        _lenS2 = 64 - jax.random.randint(jax.random.fold_in(_rk, 8), (32,), 0, max(1, 64 // 4) + 1, jnp.int32)
        _ctx_2048P = jax.random.normal(jax.random.fold_in(_rk, 11), (32, 16, 256), jnp.float32)
        _ctx_2048c = jax.random.dirichlet(jax.random.fold_in(_rk, 511), 0.3 * jnp.ones((16,), jnp.float32), (32, 64))
        _ctx_2048t = jnp.einsum('bsk,bkd->bsd', _ctx_2048c, _ctx_2048P)
        _ctx_2048t = _ctx_2048t * jax.lax.rsqrt(jnp.mean(jnp.square(_ctx_2048t)) + 1e-12) * 0.953939
        ctx_2048 = 2.81802e-05 + 1.00001 * (_ctx_2048t + 0.3 * jax.random.normal(jax.random.fold_in(_rk, 611), (32, 64, 256), jnp.float32))
        _validS = jnp.arange(64)[None, :] < _lenS[:, None]
        _validS2 = jnp.arange(64)[None, :] < _lenS2[:, None]
        _causal = jnp.tril(jnp.ones((64, 64), dtype=bool))
        mask_BxS2_ik0 = jnp.where(jnp.broadcast_to(_validS2[:, :], (32, 64)), 0, 1).astype(jnp.int32)
        mask_BxS2_bf1 = jnp.ones((32, 64), dtype=bool)
        return (x, ctx_2048, mask_BxS2_ik0, mask_BxS2_bf1)
    x, ctx_2048, mask_BxS2_ik0, mask_BxS2_bf1 = _rec_inputs()

    def _L0_xattn_setup():
        import jax, jax.numpy as jnp
        import numpy as np
        B, Q, S1, S2 = (4, 32, 256, 256)
        D, H, K, F = (256, 16, 128, 1024)
        LN_EPS = 1e-05

        def _layer_norm(x, scale, offset):
            mu = jnp.mean(x, axis=-1, keepdims=True)
            var = jnp.var(x, axis=-1, keepdims=True)
            return (x - mu) * jax.lax.rsqrt(var + LN_EPS) * scale + offset

        def _cross_attention(q_in, kv_in, wq, bq, wk, bk, wv, bv, wo, bo, bias_k, bias_v):
            b, q_len, _ = q_in.shape
            t = kv_in.shape[1]
            qh = (q_in @ wq + bq).reshape(b, q_len, H, K)
            kh = (kv_in @ wk + bk).reshape(b, t, H, K)
            vh = (kv_in @ wv + bv).reshape(b, t, H, K)
            kh = jnp.concatenate([kh, jnp.broadcast_to(bias_k, (b, 1, H, K))], axis=1)
            vh = jnp.concatenate([vh, jnp.broadcast_to(bias_v, (b, 1, H, K))], axis=1)
            scale = jnp.sqrt(jnp.asarray(K, q_in.dtype))
            logits = jnp.einsum('bqhk,bthk->bhqt', qh, kh) / scale
            weights = jax.nn.softmax(logits, axis=-1)
            ctx = jnp.einsum('bhqt,bthk->bqhk', weights, vh).reshape(b, q_len, H * K)
            return ctx @ wo + bo

        def _forward(x, xf_1, xf_2, ln1_scale, ln1_offset, wq1, bq1, wk1, bk1, wv1, bv1, wo1, bo1, bias_k1, bias_v1, ln2_scale, ln2_offset, wq2, bq2, wk2, bk2, wv2, bv2, wo2, bo2, bias_k2, bias_v2, ln_mlp_scale, ln_mlp_offset, w_fc1, b_fc1, w_fc2, b_fc2):
            res = x
            h = _layer_norm(x, ln1_scale, ln1_offset)
            x = res + _cross_attention(h, xf_1, wq1, bq1, wk1, bk1, wv1, bv1, wo1, bo1, bias_k1, bias_v1)
            res = x
            h = _layer_norm(x, ln2_scale, ln2_offset)
            x = res + _cross_attention(h, xf_2, wq2, bq2, wk2, bk2, wv2, bv2, wo2, bo2, bias_k2, bias_v2)
            h = _layer_norm(x, ln_mlp_scale, ln_mlp_offset)
            h = jax.nn.gelu(h @ w_fc1 + b_fc1, approximate=False) @ w_fc2 + b_fc2
            return x + h
        key = jax.random.key(seed)
        ks = iter(jax.random.split(key, 64))

        def rn(shape, s=0.02):
            return jax.random.normal(next(ks), shape, jnp.float32) * s
        inp = {'x': rn((B, Q, D), 1.0), 'xf_1': rn((B, S1, D), 1.0), 'xf_2': rn((B, S2, D), 1.0)}
        for i in (1, 2):
            inp[f'ln{i}_scale'] = jnp.ones((D,), jnp.float32)
            inp[f'ln{i}_offset'] = jnp.zeros((D,), jnp.float32)
            inp[f'wq{i}'] = rn((D, H * K))
            inp[f'bq{i}'] = jnp.zeros((H * K,), jnp.float32)
            inp[f'wk{i}'] = rn((D, H * K))
            inp[f'bk{i}'] = jnp.zeros((H * K,), jnp.float32)
            inp[f'wv{i}'] = rn((D, H * K))
            inp[f'bv{i}'] = jnp.zeros((H * K,), jnp.float32)
            inp[f'wo{i}'] = rn((H * K, D))
            inp[f'bo{i}'] = jnp.zeros((D,), jnp.float32)
            inp[f'bias_k{i}'] = rn((1, 1, H, K))
            inp[f'bias_v{i}'] = rn((1, 1, H, K))
        inp['ln_mlp_scale'] = jnp.ones((D,), jnp.float32)
        inp['ln_mlp_offset'] = jnp.zeros((D,), jnp.float32)
        inp['w_fc1'] = rn((D, F))
        inp['b_fc1'] = jnp.zeros((F,), jnp.float32)
        inp['w_fc2'] = rn((F, D))
        inp['b_fc2'] = jnp.zeros((D,), jnp.float32)
        return inp
    _L0_xattn_all = _L0_xattn_setup()
    _L0_xattn_in = {k: v for k, v in _L0_xattn_all.items() if k in ('ln1_scale', 'ln1_offset', 'wq1', 'bq1', 'wk1', 'bk1', 'wv1', 'bv1', 'wo1', 'bo1', 'bias_k1', 'bias_v1', 'ln2_scale', 'ln2_offset', 'wq2', 'bq2', 'wk2', 'bk2', 'wv2', 'bv2', 'wo2', 'bo2', 'bias_k2', 'bias_v2', 'ln_mlp_scale', 'ln_mlp_offset', 'w_fc1', 'b_fc1', 'w_fc2', 'b_fc2')}
    del _L0_xattn_all

    def _L1_xattn_setup():
        import jax, jax.numpy as jnp
        import numpy as np
        B, P, K, H, NH = (4, 256, 32, 256, 16)
        DH = H // NH
        EPS = 1e-06

        def rmsnorm(x, w):
            var = jnp.mean(jnp.square(x), axis=-1, keepdims=True)
            return x * jax.lax.rsqrt(var + EPS) * w
        key = jax.random.key(seed)
        ks = jax.random.split(key, 12)
        s = 0.02
        return {'x': jax.random.normal(ks[0], (B, P, H), jnp.float32), 'latents': jax.random.normal(ks[1], (B, K, H), jnp.float32), 'attention_mask': jax.random.randint(ks[2], (B, P), 0, 2, jnp.int32), 'q_w': s * jax.random.normal(ks[3], (H, H), jnp.float32), 'q_b': jnp.zeros((H,), jnp.float32), 'kv_w': s * jax.random.normal(ks[4], (H, 2 * H), jnp.float32), 'kv_b': jnp.zeros((2 * H,), jnp.float32), 'out_w': s * jax.random.normal(ks[5], (H, H), jnp.float32), 'out_b': jnp.zeros((H,), jnp.float32), 'postnorm_w': jnp.ones((H,), jnp.float32), 'mlp_w1': s * jax.random.normal(ks[6], (H, 4 * H), jnp.float32), 'mlp_b1': jnp.zeros((4 * H,), jnp.float32), 'mlp_w2': s * jax.random.normal(ks[7], (4 * H, H), jnp.float32), 'mlp_b2': jnp.zeros((H,), jnp.float32)}
    _L1_xattn_all = _L1_xattn_setup()
    _L1_xattn_in = {k: v for k, v in _L1_xattn_all.items() if k in ('q_w', 'q_b', 'kv_w', 'kv_b', 'out_w', 'out_b', 'postnorm_w', 'mlp_w1', 'mlp_b1', 'mlp_w2', 'mlp_b2')}
    del _L1_xattn_all

    def _L2_xattn_setup():
        import jax, jax.numpy as jnp
        import numpy as np
        D = 256
        H = 16
        HD = D // H
        INNER = 4 * D
        EPS = 1e-05

        def layer_norm(x, w, b):
            mu = jnp.mean(x, axis=-1, keepdims=True)
            var = jnp.mean(jnp.square(x - mu), axis=-1, keepdims=True)
            return (x - mu) * jax.lax.rsqrt(var + EPS) * w + b
        key = jax.random.key(seed)
        ks = jax.random.split(key, 12)
        B, LQ, LK = (4, 128, 256)
        std = 0.02
        inp = {'hidden_states': jax.random.normal(ks[0], (B, LQ, D), jnp.float32), 'encoder_hidden_states': jax.random.normal(ks[1], (B, LK, D), jnp.float32), 'encoder_attention_mask': jnp.ones((B, LK), dtype=bool), 'ln1_w': jnp.ones((D,), jnp.float32), 'ln1_b': jnp.zeros((D,), jnp.float32), 'q_w': jax.random.normal(ks[2], (D, D), jnp.float32) * std, 'q_b': jnp.zeros((D,), jnp.float32), 'k_w': jax.random.normal(ks[3], (D, D), jnp.float32) * std, 'k_b': jnp.zeros((D,), jnp.float32), 'v_w': jax.random.normal(ks[4], (D, D), jnp.float32) * std, 'v_b': jnp.zeros((D,), jnp.float32), 'cproj_w': jax.random.normal(ks[5], (D, D), jnp.float32) * std, 'cproj_b': jnp.zeros((D,), jnp.float32), 'ln2_w': jnp.ones((D,), jnp.float32), 'ln2_b': jnp.zeros((D,), jnp.float32), 'fc_w': jax.random.normal(ks[6], (D, INNER), jnp.float32) * std, 'fc_b': jnp.zeros((INNER,), jnp.float32), 'proj_w': jax.random.normal(ks[7], (INNER, D), jnp.float32) * std, 'proj_b': jnp.zeros((D,), jnp.float32)}
        return inp
    _L2_xattn_all = _L2_xattn_setup()
    _L2_xattn_in = {k: v for k, v in _L2_xattn_all.items() if k in ('ln1_w', 'ln1_b', 'q_w', 'q_b', 'k_w', 'k_b', 'v_w', 'v_b', 'cproj_w', 'cproj_b', 'ln2_w', 'ln2_b', 'fc_w', 'fc_b', 'proj_w', 'proj_b')}
    del _L2_xattn_all

    def _L3_xattn_setup():
        import jax, jax.numpy as jnp
        import numpy as np
        B, C, CI, T = (8, 64, 32, 256)
        EPS = 1e-05
        key = jax.random.key(seed)
        ks = jax.random.split(key, 8)
        inv_c = 1.0 / np.sqrt(C)
        inv_ci = 1.0 / np.sqrt(CI)
        return {'x_this': jax.random.normal(ks[0], (B, C, T), jnp.float32), 'x_other': jax.random.normal(ks[1], (B, C, T), jnp.float32), 'Wg': jax.random.normal(ks[2], (CI, C), jnp.float32) * inv_c, 'bg': jnp.zeros((CI,), jnp.float32), 'Wtheta': jax.random.normal(ks[3], (CI, C), jnp.float32) * inv_c, 'btheta': jnp.zeros((CI,), jnp.float32), 'Wphi': jax.random.normal(ks[4], (CI, C), jnp.float32) * inv_c, 'bphi': jnp.zeros((CI,), jnp.float32), 'Wz': jax.random.normal(ks[5], (C, CI), jnp.float32) * inv_ci, 'bz': jnp.zeros((C,), jnp.float32), 'gamma': jax.random.normal(ks[6], (C,), jnp.float32), 'beta': jax.random.normal(ks[7], (C,), jnp.float32)}
    _L3_xattn_all = _L3_xattn_setup()
    _L3_xattn_in = {k: v for k, v in _L3_xattn_all.items() if k in ('Wg', 'bg', 'Wtheta', 'btheta', 'Wphi', 'bphi', 'Wz', 'bz', 'gamma', 'beta')}
    del _L3_xattn_all
    return {'x': x, 'ctx_2048': ctx_2048, 'mask_BxS2_ik0': mask_BxS2_ik0, 'mask_BxS2_bf1': mask_BxS2_bf1, 'L0_xattn_ln1_scale': _L0_xattn_in['ln1_scale'], 'L0_xattn_ln1_offset': _L0_xattn_in['ln1_offset'], 'L0_xattn_wq1': _L0_xattn_in['wq1'], 'L0_xattn_bq1': _L0_xattn_in['bq1'], 'L0_xattn_wk1': _L0_xattn_in['wk1'], 'L0_xattn_bk1': _L0_xattn_in['bk1'], 'L0_xattn_wv1': _L0_xattn_in['wv1'], 'L0_xattn_bv1': _L0_xattn_in['bv1'], 'L0_xattn_wo1': _L0_xattn_in['wo1'], 'L0_xattn_bo1': _L0_xattn_in['bo1'], 'L0_xattn_bias_k1': _L0_xattn_in['bias_k1'], 'L0_xattn_bias_v1': _L0_xattn_in['bias_v1'], 'L0_xattn_ln2_scale': _L0_xattn_in['ln2_scale'], 'L0_xattn_ln2_offset': _L0_xattn_in['ln2_offset'], 'L0_xattn_wq2': _L0_xattn_in['wq2'], 'L0_xattn_bq2': _L0_xattn_in['bq2'], 'L0_xattn_wk2': _L0_xattn_in['wk2'], 'L0_xattn_bk2': _L0_xattn_in['bk2'], 'L0_xattn_wv2': _L0_xattn_in['wv2'], 'L0_xattn_bv2': _L0_xattn_in['bv2'], 'L0_xattn_wo2': _L0_xattn_in['wo2'], 'L0_xattn_bo2': _L0_xattn_in['bo2'], 'L0_xattn_bias_k2': _L0_xattn_in['bias_k2'], 'L0_xattn_bias_v2': _L0_xattn_in['bias_v2'], 'L0_xattn_ln_mlp_scale': _L0_xattn_in['ln_mlp_scale'], 'L0_xattn_ln_mlp_offset': _L0_xattn_in['ln_mlp_offset'], 'L0_xattn_w_fc1': _L0_xattn_in['w_fc1'], 'L0_xattn_b_fc1': _L0_xattn_in['b_fc1'], 'L0_xattn_w_fc2': _L0_xattn_in['w_fc2'], 'L0_xattn_b_fc2': _L0_xattn_in['b_fc2'], 'L1_xattn_q_w': _L1_xattn_in['q_w'], 'L1_xattn_q_b': _L1_xattn_in['q_b'], 'L1_xattn_kv_w': _L1_xattn_in['kv_w'], 'L1_xattn_kv_b': _L1_xattn_in['kv_b'], 'L1_xattn_out_w': _L1_xattn_in['out_w'], 'L1_xattn_out_b': _L1_xattn_in['out_b'], 'L1_xattn_postnorm_w': _L1_xattn_in['postnorm_w'], 'L1_xattn_mlp_w1': _L1_xattn_in['mlp_w1'], 'L1_xattn_mlp_b1': _L1_xattn_in['mlp_b1'], 'L1_xattn_mlp_w2': _L1_xattn_in['mlp_w2'], 'L1_xattn_mlp_b2': _L1_xattn_in['mlp_b2'], 'L2_xattn_ln1_w': _L2_xattn_in['ln1_w'], 'L2_xattn_ln1_b': _L2_xattn_in['ln1_b'], 'L2_xattn_q_w': _L2_xattn_in['q_w'], 'L2_xattn_q_b': _L2_xattn_in['q_b'], 'L2_xattn_k_w': _L2_xattn_in['k_w'], 'L2_xattn_k_b': _L2_xattn_in['k_b'], 'L2_xattn_v_w': _L2_xattn_in['v_w'], 'L2_xattn_v_b': _L2_xattn_in['v_b'], 'L2_xattn_cproj_w': _L2_xattn_in['cproj_w'], 'L2_xattn_cproj_b': _L2_xattn_in['cproj_b'], 'L2_xattn_ln2_w': _L2_xattn_in['ln2_w'], 'L2_xattn_ln2_b': _L2_xattn_in['ln2_b'], 'L2_xattn_fc_w': _L2_xattn_in['fc_w'], 'L2_xattn_fc_b': _L2_xattn_in['fc_b'], 'L2_xattn_proj_w': _L2_xattn_in['proj_w'], 'L2_xattn_proj_b': _L2_xattn_in['proj_b'], 'L3_xattn_Wg': _L3_xattn_in['Wg'], 'L3_xattn_bg': _L3_xattn_in['bg'], 'L3_xattn_Wtheta': _L3_xattn_in['Wtheta'], 'L3_xattn_btheta': _L3_xattn_in['btheta'], 'L3_xattn_Wphi': _L3_xattn_in['Wphi'], 'L3_xattn_bphi': _L3_xattn_in['bphi'], 'L3_xattn_Wz': _L3_xattn_in['Wz'], 'L3_xattn_bz': _L3_xattn_in['bz'], 'L3_xattn_gamma': _L3_xattn_in['gamma'], 'L3_xattn_beta': _L3_xattn_in['beta']}

def reference(x, ctx_2048, mask_BxS2_ik0, mask_BxS2_bf1, L0_xattn_ln1_scale, L0_xattn_ln1_offset, L0_xattn_wq1, L0_xattn_bq1, L0_xattn_wk1, L0_xattn_bk1, L0_xattn_wv1, L0_xattn_bv1, L0_xattn_wo1, L0_xattn_bo1, L0_xattn_bias_k1, L0_xattn_bias_v1, L0_xattn_ln2_scale, L0_xattn_ln2_offset, L0_xattn_wq2, L0_xattn_bq2, L0_xattn_wk2, L0_xattn_bk2, L0_xattn_wv2, L0_xattn_bv2, L0_xattn_wo2, L0_xattn_bo2, L0_xattn_bias_k2, L0_xattn_bias_v2, L0_xattn_ln_mlp_scale, L0_xattn_ln_mlp_offset, L0_xattn_w_fc1, L0_xattn_b_fc1, L0_xattn_w_fc2, L0_xattn_b_fc2, L1_xattn_q_w, L1_xattn_q_b, L1_xattn_kv_w, L1_xattn_kv_b, L1_xattn_out_w, L1_xattn_out_b, L1_xattn_postnorm_w, L1_xattn_mlp_w1, L1_xattn_mlp_b1, L1_xattn_mlp_w2, L1_xattn_mlp_b2, L2_xattn_ln1_w, L2_xattn_ln1_b, L2_xattn_q_w, L2_xattn_q_b, L2_xattn_k_w, L2_xattn_k_b, L2_xattn_v_w, L2_xattn_v_b, L2_xattn_cproj_w, L2_xattn_cproj_b, L2_xattn_ln2_w, L2_xattn_ln2_b, L2_xattn_fc_w, L2_xattn_fc_b, L2_xattn_proj_w, L2_xattn_proj_b, L3_xattn_Wg, L3_xattn_bg, L3_xattn_Wtheta, L3_xattn_btheta, L3_xattn_Wphi, L3_xattn_bphi, L3_xattn_Wz, L3_xattn_bz, L3_xattn_gamma, L3_xattn_beta):
    import jax
    import jax.numpy as jnp

    def _L0_xattn_ref(x, xf_1, xf_2, ln1_scale, ln1_offset, wq1, bq1, wk1, bk1, wv1, bv1, wo1, bo1, bias_k1, bias_v1, ln2_scale, ln2_offset, wq2, bq2, wk2, bk2, wv2, bv2, wo2, bo2, bias_k2, bias_v2, ln_mlp_scale, ln_mlp_offset, w_fc1, b_fc1, w_fc2, b_fc2):
        import jax, jax.numpy as jnp
        import numpy as np
        B, Q, S1, S2 = (4, 32, 256, 256)
        D, H, K, F = (256, 16, 128, 1024)
        LN_EPS = 1e-05

        def _layer_norm(x, scale, offset):
            mu = jnp.mean(x, axis=-1, keepdims=True)
            var = jnp.var(x, axis=-1, keepdims=True)
            return (x - mu) * jax.lax.rsqrt(var + LN_EPS) * scale + offset

        def _cross_attention(q_in, kv_in, wq, bq, wk, bk, wv, bv, wo, bo, bias_k, bias_v):
            b, q_len, _ = q_in.shape
            t = kv_in.shape[1]
            qh = (q_in @ wq + bq).reshape(b, q_len, H, K)
            kh = (kv_in @ wk + bk).reshape(b, t, H, K)
            vh = (kv_in @ wv + bv).reshape(b, t, H, K)
            kh = jnp.concatenate([kh, jnp.broadcast_to(bias_k, (b, 1, H, K))], axis=1)
            vh = jnp.concatenate([vh, jnp.broadcast_to(bias_v, (b, 1, H, K))], axis=1)
            scale = jnp.sqrt(jnp.asarray(K, q_in.dtype))
            logits = jnp.einsum('bqhk,bthk->bhqt', qh, kh) / scale
            weights = jax.nn.softmax(logits, axis=-1)
            ctx = jnp.einsum('bhqt,bthk->bqhk', weights, vh).reshape(b, q_len, H * K)
            return ctx @ wo + bo

        def _forward(x, xf_1, xf_2, ln1_scale, ln1_offset, wq1, bq1, wk1, bk1, wv1, bv1, wo1, bo1, bias_k1, bias_v1, ln2_scale, ln2_offset, wq2, bq2, wk2, bk2, wv2, bv2, wo2, bo2, bias_k2, bias_v2, ln_mlp_scale, ln_mlp_offset, w_fc1, b_fc1, w_fc2, b_fc2):
            res = x
            h = _layer_norm(x, ln1_scale, ln1_offset)
            x = res + _cross_attention(h, xf_1, wq1, bq1, wk1, bk1, wv1, bv1, wo1, bo1, bias_k1, bias_v1)
            res = x
            h = _layer_norm(x, ln2_scale, ln2_offset)
            x = res + _cross_attention(h, xf_2, wq2, bq2, wk2, bk2, wv2, bv2, wo2, bo2, bias_k2, bias_v2)
            h = _layer_norm(x, ln_mlp_scale, ln_mlp_offset)
            h = jax.nn.gelu(h @ w_fc1 + b_fc1, approximate=False) @ w_fc2 + b_fc2
            return x + h
        return _forward(x, xf_1, xf_2, ln1_scale, ln1_offset, wq1, bq1, wk1, bk1, wv1, bv1, wo1, bo1, bias_k1, bias_v1, ln2_scale, ln2_offset, wq2, bq2, wk2, bk2, wv2, bv2, wo2, bo2, bias_k2, bias_v2, ln_mlp_scale, ln_mlp_offset, w_fc1, b_fc1, w_fc2, b_fc2)

    def _L1_xattn_ref(x, latents, attention_mask, q_w, q_b, kv_w, kv_b, out_w, out_b, postnorm_w, mlp_w1, mlp_b1, mlp_w2, mlp_b2):
        import jax, jax.numpy as jnp
        import numpy as np
        B, P, K, H, NH = (4, 256, 32, 256, 16)
        DH = H // NH
        EPS = 1e-06

        def rmsnorm(x, w):
            var = jnp.mean(jnp.square(x), axis=-1, keepdims=True)
            return x * jax.lax.rsqrt(var + EPS) * w
        b, p, _ = x.shape
        k_len = latents.shape[1]
        residual = latents
        h = jnp.concatenate([x, latents], axis=1)
        q = (latents @ q_w + q_b).reshape(b, k_len, NH, DH)
        kv = (h @ kv_w + kv_b).reshape(b, p + k_len, NH, DH, 2)
        kmat, v = (kv[..., 0], kv[..., 1])
        attn = jnp.einsum('bkhd,bnhd->bhkn', q, kmat) / DH
        full_mask = jnp.concatenate([attention_mask.astype(bool), jnp.ones((b, k_len), bool)], axis=-1)
        attn = jnp.where(full_mask[:, None, None, :], attn, -jnp.inf)
        attn = jax.nn.softmax(attn.astype(jnp.float32), axis=-1).astype(q.dtype)
        attn_out = jnp.einsum('bhkn,bnhd->bkhd', attn, v).reshape(b, k_len, H)
        attn_out = attn_out @ out_w + out_b + residual
        out = rmsnorm(attn_out, postnorm_w)
        out = jax.nn.gelu(out @ mlp_w1 + mlp_b1) @ mlp_w2 + mlp_b2
        return out + residual

    def _L2_xattn_ref(hidden_states, encoder_hidden_states, encoder_attention_mask, ln1_w, ln1_b, q_w, q_b, k_w, k_b, v_w, v_b, cproj_w, cproj_b, ln2_w, ln2_b, fc_w, fc_b, proj_w, proj_b):
        import jax, jax.numpy as jnp
        import numpy as np
        D = 256
        H = 16
        HD = D // H
        INNER = 4 * D
        EPS = 1e-05

        def layer_norm(x, w, b):
            mu = jnp.mean(x, axis=-1, keepdims=True)
            var = jnp.mean(jnp.square(x - mu), axis=-1, keepdims=True)
            return (x - mu) * jax.lax.rsqrt(var + EPS) * w + b
        B, LQ, _ = hidden_states.shape
        LK = encoder_hidden_states.shape[1]
        residual = hidden_states
        x = layer_norm(hidden_states, ln1_w, ln1_b)
        q = (x @ q_w + q_b).reshape(B, LQ, H, HD).transpose(0, 2, 1, 3)
        k = (encoder_hidden_states @ k_w + k_b).reshape(B, LK, H, HD).transpose(0, 2, 1, 3)
        v = (encoder_hidden_states @ v_w + v_b).reshape(B, LK, H, HD).transpose(0, 2, 1, 3)
        scale = 1.0 / np.sqrt(HD).astype(np.float32)
        scores = jnp.einsum('bhqd,bhkd->bhqk', q, k) * scale
        mask = encoder_attention_mask[:, None, None, :]
        mask_value = jnp.finfo(scores.dtype).min
        scores = jnp.where(mask, scores, mask_value)
        attn = jax.nn.softmax(scores, axis=-1)
        out = jnp.einsum('bhqk,bhkd->bhqd', attn, v)
        out = out.transpose(0, 2, 1, 3).reshape(B, LQ, D)
        out = out @ cproj_w + cproj_b
        hidden = out + residual
        residual = hidden
        y = layer_norm(hidden, ln2_w, ln2_b)
        y = jax.nn.gelu(y @ fc_w + fc_b, approximate=True)
        y = y @ proj_w + proj_b
        return residual + y

    def _L3_xattn_ref(x_this, x_other, Wg, bg, Wtheta, btheta, Wphi, bphi, Wz, bz, gamma, beta):
        import jax, jax.numpy as jnp
        import numpy as np
        B, C, CI, T = (8, 64, 32, 256)
        EPS = 1e-05
        g_x = jnp.einsum('oc,bct->bto', Wg, x_this) + bg
        theta = jnp.einsum('oc,bct->bot', Wtheta, x_this) + btheta[None, :, None]
        phi = jnp.einsum('oc,bct->bot', Wphi, x_other) + bphi[None, :, None]
        f = jnp.einsum('bci,bcj->bij', phi, theta)
        f_div_C = jax.nn.softmax(f, axis=-1)
        y = jnp.einsum('bij,bjo->bio', f_div_C, g_x)
        w_y = jnp.einsum('oc,btc->bot', Wz, y) + bz[None, :, None]
        mean = jnp.mean(w_y, axis=(0, 2), keepdims=True)
        var = jnp.var(w_y, axis=(0, 2), keepdims=True)
        w_y = gamma[None, :, None] * (w_y - mean) * jax.lax.rsqrt(var + EPS) + beta[None, :, None]
        return w_y + x_this
    x = _L0_xattn_ref(x, ctx_2048, ctx_2048, L0_xattn_ln1_scale, L0_xattn_ln1_offset, L0_xattn_wq1, L0_xattn_bq1, L0_xattn_wk1, L0_xattn_bk1, L0_xattn_wv1, L0_xattn_bv1, L0_xattn_wo1, L0_xattn_bo1, L0_xattn_bias_k1, L0_xattn_bias_v1, L0_xattn_ln2_scale, L0_xattn_ln2_offset, L0_xattn_wq2, L0_xattn_bq2, L0_xattn_wk2, L0_xattn_bk2, L0_xattn_wv2, L0_xattn_bv2, L0_xattn_wo2, L0_xattn_bo2, L0_xattn_bias_k2, L0_xattn_bias_v2, L0_xattn_ln_mlp_scale, L0_xattn_ln_mlp_offset, L0_xattn_w_fc1, L0_xattn_b_fc1, L0_xattn_w_fc2, L0_xattn_b_fc2)
    x = _L1_xattn_ref(ctx_2048, x, mask_BxS2_ik0, L1_xattn_q_w, L1_xattn_q_b, L1_xattn_kv_w, L1_xattn_kv_b, L1_xattn_out_w, L1_xattn_out_b, L1_xattn_postnorm_w, L1_xattn_mlp_w1, L1_xattn_mlp_b1, L1_xattn_mlp_w2, L1_xattn_mlp_b2)
    x = _L2_xattn_ref(x, ctx_2048, mask_BxS2_bf1, L2_xattn_ln1_w, L2_xattn_ln1_b, L2_xattn_q_w, L2_xattn_q_b, L2_xattn_k_w, L2_xattn_k_b, L2_xattn_v_w, L2_xattn_v_b, L2_xattn_cproj_w, L2_xattn_cproj_b, L2_xattn_ln2_w, L2_xattn_ln2_b, L2_xattn_fc_w, L2_xattn_fc_b, L2_xattn_proj_w, L2_xattn_proj_b)
    x = _L3_xattn_ref(x, ctx_2048, L3_xattn_Wg, L3_xattn_bg, L3_xattn_Wtheta, L3_xattn_btheta, L3_xattn_Wphi, L3_xattn_bphi, L3_xattn_Wz, L3_xattn_bz, L3_xattn_gamma, L3_xattn_beta)
    return x

_drawn_inputs = setup_inputs


def setup_inputs(seed=0):
    import zlib

    import numpy as np

    out = dict(_drawn_inputs(seed))
    spreads = {'L0_xattn_ln1_scale': (1.0, 0.6),
     'L0_xattn_ln1_offset': (0.0, 0.8),
     'L0_xattn_bq1': (0.0, 0.8),
     'L0_xattn_bk1': (0.0, 2.0),
     'L0_xattn_bv1': (0.0, 0.1),
     'L0_xattn_bo1': (0.0, 0.1),
     'L0_xattn_ln2_scale': (1.0, 0.6),
     'L0_xattn_ln2_offset': (0.0, 0.8),
     'L0_xattn_bq2': (0.0, 0.8),
     'L0_xattn_bk2': (0.0, 2.0),
     'L0_xattn_bv2': (0.0, 0.1),
     'L0_xattn_bo2': (0.0, 0.1),
     'L0_xattn_ln_mlp_scale': (1.0, 0.2),
     'L0_xattn_ln_mlp_offset': (0.0, 0.523),
     'L0_xattn_b_fc1': (0.0, 0.1),
     'L0_xattn_b_fc2': (0.0, 0.1),
     'L1_xattn_q_b': (0.0, 0.8),
     'L1_xattn_kv_b': (0.0, 0.8),
     'L1_xattn_out_b': (0.0, 2.0),
     'L1_xattn_postnorm_w': (1.0, 0.546),
     'L1_xattn_mlp_b1': (0.0, 0.1),
     'L1_xattn_mlp_b2': (0.0, 0.1),
     'L2_xattn_ln1_w': (1.0, 0.6),
     'L2_xattn_ln1_b': (0.0, 0.8),
     'L2_xattn_q_b': (0.0, 0.8),
     'L2_xattn_k_b': (0.0, 2.0),
     'L2_xattn_v_b': (0.0, 0.1),
     'L2_xattn_cproj_b': (0.0, 0.1),
     'L2_xattn_ln2_w': (1.0, 0.2),
     'L2_xattn_ln2_b': (0.0, 0.567),
     'L2_xattn_fc_b': (0.0, 0.1),
     'L2_xattn_proj_b': (0.0, 0.1),
     'L3_xattn_bg': (0.0, 2.0),
     'L3_xattn_btheta': (0.0, 2.0),
     'L3_xattn_bphi': (0.0, 0.1),
     'L3_xattn_bz': (0.0, 2.0)}
    factors = {'L0_xattn_wq1': 6.316,
     'L0_xattn_wk1': 6.054,
     'L0_xattn_bias_k1': 64.0,
     'L0_xattn_bias_v1': 31.367,
     'L0_xattn_wq2': 6.386,
     'L0_xattn_wk2': 6.211,
     'L0_xattn_bias_k2': 64.0,
     'L0_xattn_bias_v2': 55.612,
     'L1_xattn_q_w': 8.0,
     'L1_xattn_kv_w': 8.0,
     'L1_xattn_out_w': 8.0,
     'L2_xattn_q_w': 8.0,
     'L2_xattn_k_w': 8.0}
    for name, (base, spread) in spreads.items():
        noise = np.random.default_rng([zlib.crc32(name.encode()), seed]).standard_normal(out[name].shape)
        drawn = base * np.exp(spread * noise) if base else spread * noise
        out[name] = jnp.asarray(drawn.astype(out[name].dtype))
    for name, factor in factors.items():
        out[name] = (out[name] * factor).astype(out[name].dtype)
    return out
```

```python
import math
from contextlib import ExitStack

import numpy as np

import concourse.bass as bass
from concourse import mybir
from concourse.alu_op_type import AluOpType as ALU

F32 = mybir.dt.float32
F32R = mybir.dt.float32r
I32 = mybir.dt.int32
U8 = mybir.dt.uint8
ACT = mybir.ActivationFunctionType
AX = mybir.AxisListType

P = 128
NB, SEQ, D = 32, 64, 256
TOK = NB * SEQ
TILES = TOK // P
KT = D // P
FF = 4 * D
FT = FF // P
CH = 512
NCH = TOK // CH
TPC = CH // P
BPC = CH // SEQ
H0, DH0 = 16, 128
H1, DH1 = 16, 16
HPT = P // DH1
NHP = H0 // 2
UPP = 2 * NCH
UNITS = NHP * UPP
KEYS0 = SEQ + 1
CI = 32
PACK = 2048
PCOLS = PACK + 8
NPACK = 2 * NHP + 8
NEG = -3.4028234663852886e38

COLS = {}


def _col(name, n):
    COLS[name] = (sum(k for _, k in COLS.values()), n)


for _name, _n in (("ln1", 4), ("ln2", 4), ("lnm", 4), ("l1q", 2), ("l1k", 2), ("rms", 4), ("l2n", 4),
                  ("l2q", 2), ("l2k", 2), ("l2m", 4), ("fb0", FT), ("fb1", FT), ("fb2", FT),
                  ("one", 4), ("bth", 1), ("bph", 1), ("bz", 1), ("gam", 1), ("bet", 1),
                  ("hmask", HPT), ("even", 1), ("odd", 1),
                  ("wth", 2 * CI), ("wph", 2 * CI), ("wg", 2 * CI), ("wz", P), ("ident", P)):
    _col(_name, _n)
NCOL = sum(k for _, k in COLS.values())
ARENA = 11400
PJB = (0, 1, 2, 3)
ROWS = ("bo1", "bo2", "b_fc2", "out_b", "mlp_b2", "cproj_b", "proj_b", "l1v", "l2v", "bg")



class Steps:

    def __init__(self, sem, base):
        self.sem, self.base = sem, base

    def done(self, ins):
        ins.then_inc(self.sem, 1)

    def wait(self, eng, n):
        eng.wait_ge(self.sem, n + (self.base + 1))


class Stage:

    def __init__(self, sem, ahead):
        self.sem, self.total, self.ahead = sem, ahead, ahead

    def phase(self, steps):
        got = Steps(self.sem, self.total)
        self.total += steps
        return got


def build(nc, wpack, ctxT, ctx_tok, x_in, mask1, mask2, cols_in, rows_in, vb_in, out, spill):
    ctx = ExitStack()
    with ctx:
        def sb(name, cols, dt=F32):
            return ctx.enter_context(nc.sbuf_tensor(name, [P, cols], dt))

        def semaphore(name):
            return ctx.enter_context(nc.semaphore(name))

        owned = {e: [] for e in ("pe", "act", "dve", "pool")}

        def stages(owner, ahead, names):
            got = []
            for name in names.split():
                s = Stage(semaphore(name), ahead)
                if ahead:
                    owned[owner].append(s)
                got.append(s)
            return got

        def cut(t, k):
            return t.rearrange("p (k n) -> p k n", k=k)

        def many(t, n):
            return t.rearrange("p (k a) -> p k a", a=1).to_broadcast([P, t.shape[1], n])

        def each(t, k):
            return t.rearrange("p (a n) -> p a n", a=1).to_broadcast([P, k, t.shape[1]])

        x_sb = cut(sb("x_sb", TILES * D)[:, :], TILES)
        cT = [cut(sb(f"cT{i}", KT * TOK, F32R)[:, :], KT) for i in range(2)]
        hT = [cut(sb(f"hT{i}", KT * TOK, F32R)[:, :], KT) for i in range(2)]
        W = [[sb(f"W{b}{i}", PACK, F32R)[:, :] for i in range(2)] for b in range(2)]
        raw = sb("raw", PCOLS)
        hbias = [sb(f"hbias{b}", 8)[:, :] for b in range(2)]
        vraw = sb("vraw", 2 * D)
        vdiff = [sb(f"vdiff{b}", D)[:, :] for b in range(2)]
        cols = sb("cols", NCOL)
        rows = cut(sb("rows", len(ROWS) * D)[:, :], len(ROWS))
        split_arena = sb("split_arena", 4096, F32R)
        norm_arena = sb("norm_arena", KT * CH + TPC * D)
        arena = sb("arena", ARENA)
        small = sb("small", 256)
        ps = ctx.enter_context(nc.psum_tensor("ps", [P, 8, 512], F32))

        def carve(tensor, sizes):
            at, got = 0, []
            for n in sizes:
                got.append(tensor[:, at:at + n])
                at += n
            assert at <= tensor.shape[1], (at, tensor.shape)
            return got

        def col(name, j=0, n=1):
            a = COLS[name][0] + j
            return cols[:, a:a + n]

        def row(name):
            return rows[:, ROWS.index(name), :]

        ident = col("ident", 0, P)

        s_x, s_const, s_ctx, s_raw, s_vb, s_mask, s_spill, s_back, s_out = (
            semaphore("s_" + s) for s in "x const ctx raw vb mask spill back out".split())

        todo = {e: [] for e in ("pe", "act", "dve", "pool", "sp")}

        def on(engine):
            def keep(f):
                todo[engine].append(f)
                return f
            return keep

        def settled(e):
            e.sem_inc(s_turn, 1)

        s_turn = semaphore("s_turn")

        def split3(e, dst, lhs, rhs, start, stop):
            for n, (a, b) in enumerate(((0, 0), (0, 1), (1, 0))):
                last = e.matmul(dst, lhs[a], rhs[b], start=start and n == 0, stop=stop and n == 2,
                                skip_group_check=True)
            return last

        (w_used,) = stages("pe", 2, "w_used")
        w_hi, w_lo = stages("pool", 2, "w_hi w_lo")
        (v_diff,) = stages("pool", 2, "v_diff")
        w_used, w_hi, w_lo, v_diff = (s.phase(NPACK) for s in (w_used, w_hi, w_lo, v_diff))
        NPAIR = 2 * NHP + 2

        def split_pack(e, n, b, pair):
            e.wait_ge(s_raw, n * 16 + 16)
            w_used.wait(e, n - 2)
            settled(e)
            if pair:
                e.tensor_copy(hbias[b], raw[:, PACK:PCOLS])
                e.wait_ge(s_vb, n * 16 + 16)
                v_diff.done(e.tensor_tensor(vdiff[b], vraw[:, 0:D], vraw[:, D:2 * D], ALU.subtract))
            w_hi.done(e.tensor_copy(W[b][0], raw[:, 0:PACK]))
            w_hi.wait(e, n)
            w_lo.done(e.tensor_tensor(W[b][1], raw[:, 0:PACK], W[b][0].bitcast(F32), ALU.subtract))

        @on("sp")
        def _(e):
            e.dma_start(cols[:, :], cols_in[:, :]).then_inc(s_const, 16)
            e.dma_start(x_sb, x_in.rearrange("(t p) d -> p t d", p=P)).then_inc(s_x, 16)
            w_lo.wait(e, -1)
            e.dma_start(raw[:, :], wpack[0, :, :]).then_inc(s_raw, 16)
            e.dma_start(vraw[:, :], vb_in[0, :].partition_broadcast(P)).then_inc(s_vb, 16)
            e.dma_start(ctxraw, ctxT.rearrange("(k p) n -> p k n", p=P)).then_inc(s_ctx, 16)
            e.dma_start(rows.rearrange("p r d -> p (r d)"), rows_in[:].partition_broadcast(P)).then_inc(s_const, 16)
            with e.Fori(1, NPAIR) as n:
                w_lo.wait(e, n - 1)
                e.dma_start(raw[:, :], wpack[bass.ds(n, 1), :, :].rearrange("a p n -> (a p) n")).then_inc(s_raw, 16)
                v_diff.wait(e, n - 1)
                e.dma_start(vraw[:, :], vb_in[bass.ds(n, 1), :].rearrange("a d -> (a d)").partition_broadcast(P)).then_inc(s_vb, 16)
            with e.Fori(NPAIR, NPACK) as n:
                w_lo.wait(e, n - 1)
                e.dma_start(raw[:, :], wpack[bass.ds(n, 1), :, :].rearrange("a p n -> (a p) n")).then_inc(s_raw, 16)

        ctxraw = cut(arena[:, 0:KT * TOK], KT)
        c_hi, c_lo = (s.phase(KT) for s in stages("", 0, "c_hi c_lo"))

        @on("act")
        def _(e):
            e.wait_ge(s_ctx, 16)
            for k in range(KT):
                c_hi.done(e.activation(cT[0][:, k, :], ctxraw[:, k, :], ACT.Copy))

        @on("dve")
        def _(e):
            for k in range(KT):
                c_hi.wait(e, k)
                c_lo.done(e.tensor_tensor(cT[1][:, k, :], ctxraw[:, k, :], cT[0][:, k, :].bitcast(F32), ALU.subtract))

        N = dict(zip("st ag var sq r1 r2 r3 r4 x lo".split(),
                     stages("dve", 2, "n_st n_ag n_var n_sq n_r1 n_r2 n_r3 n_r4 n_x n_lo")))
        N |= zip(["pow"], stages("pool", 2, "n_pow"))
        N |= zip(["T"], stages("pe", 2, "n_T"))
        N |= zip(["ev", "hi"], stages("act", 2, "n_ev n_hi"))
        tn, xn = carve(norm_arena, [KT * CH, TPC * D])
        tn, xn = cut(tn, KT), cut(xn, TPC)
        st6 = cut(small[:, 0:TPC * 6], TPC)
        mv = cut(small[:, 32:32 + TPC * 2], TPC)
        vare, r0, ra, rb, rc, rstd, minus_half = (small[:, 40 + 4 * i:44 + 4 * i] for i in range(7))
        (s_small,) = (s.phase(1) for s in stages("", 0, "s_small"))

        def norm_phase(kind, eps, affine, times=1):
            s = {k: v.phase(times * NCH * (KT if k in ("ev", "hi", "lo") else 1)) for k, v in N.items()
                 if kind != "none" or k in ("x", "T", "ev", "hi", "lo")
                 if kind == "rms" or k != "sq"}

            def dve(e, l):
                with e.Fori(0, NCH) as c:
                    g = l * NCH + c
                    if kind != "none":
                        s["x"].wait(e, g - 1)
                        for j in range(TPC):
                            ins = e.bn_stats(st6[:, j, :], x_sb[:, bass.ds(c * TPC + j, 1), :].rearrange("p a d -> p (a d)"))
                        s["st"].done(ins)
                        s["st"].wait(e, g)
                        settled(e)
                        for j in range(TPC):
                            ins = e.bn_aggr(mv[:, j, :], st6[:, j, :])
                        s["ag"].done(ins)
                        s["ag"].wait(e, g)
                        if kind == "rms":
                            s["sq"].done(e.tensor_tensor(ra, mv[:, :, 0], mv[:, :, 0], ALU.mult))
                            s["sq"].wait(e, g)
                            s["var"].done(e.scalar_tensor_tensor(vare, ra, float(eps), mv[:, :, 1], ALU.add, ALU.add))
                        else:
                            s["var"].done(e.tensor_scalar(vare, mv[:, :, 1], float(eps), None, ALU.add))
                        s["var"].wait(e, g)
                        s["pow"].wait(e, g)
                        s["r1"].done(e.tensor_tensor(ra, r0, r0, ALU.mult))
                        s["r1"].wait(e, g)
                        s["r2"].done(e.tensor_tensor(rb, ra, vare, ALU.mult))
                        s["r2"].wait(e, g)
                        s["r3"].done(e.tensor_scalar(rc, rb, -0.5, 1.5, ALU.mult, ALU.add))
                        s["r3"].wait(e, g)
                        s["r4"].done(e.tensor_tensor(rstd, r0, rc, ALU.mult))
                        s["r4"].wait(e, g)
                    s["T"].wait(e, g - 1)
                    for j in range(TPC):
                        xt = x_sb[:, bass.ds(c * TPC + j, 1), :].rearrange("p a d -> p (a d)")
                        if kind == "layer":
                            ins = e.tensor_scalar(xn[:, j, :], xt, mv[:, j, 0:1], rstd[:, j:j + 1], ALU.subtract, ALU.mult)
                        elif kind == "rms":
                            ins = e.tensor_scalar(xn[:, j, :], xt, rstd[:, j:j + 1], None, ALU.mult)
                        else:
                            ins = e.tensor_copy(xn[:, j, :], xt)
                    s["x"].done(ins)
                    for k in range(KT):
                        s["hi"].wait(e, g * KT + k)
                        s["lo"].done(e.tensor_tensor(hT[1][:, k, bass.ds(c * CH, CH)], tn[:, k, :],
                                                     hT[0][:, k, bass.ds(c * CH, CH)].bitcast(F32), ALU.subtract))

            def pool(e, l):
                if kind != "none":
                    with e.Fori(0, NCH) as c:
                        s["var"].wait(e, l * NCH + c)
                        s["pow"].done(e.tensor_tensor(r0, vare, minus_half, ALU.pow))

            def pe(e, l):
                with e.Fori(0, NCH) as c:
                    g = l * NCH + c
                    s["x"].wait(e, g)
                    s["ev"].wait(e, g * KT - 1)
                    for k in range(KT):
                        for j in range(TPC):
                            ins = e.transpose(ps[:, 6 + k, j * P:(j + 1) * P], xn[:, j, k * P:(k + 1) * P], ident)
                    s["T"].done(ins)

            def act(e, l):
                with e.Fori(0, NCH) as c:
                    g = l * NCH + c
                    s["T"].wait(e, g)
                    s["lo"].wait(e, g * KT - 1)
                    for k in range(KT):
                        s["ev"].done(e.activation(tn[:, k, :], ps[:, 6 + k, :], ACT.Identity,
                                                  bias=affine(l, KT + k), scale=affine(l, k)))
                    for k in range(KT):
                        s["ev"].wait(e, g * KT + k)
                        s["hi"].done(e.activation(hT[0][:, k, bass.ds(c * CH, CH)], tn[:, k, :], ACT.Copy))

            return {"dve": dve, "pool": pool, "pe": pe, "act": act, "x": s["x"], "lo": s["lo"]}

        def static_affine(name):
            return lambda l, j: col(name, j)

        (x_plus,) = stages("", 0, "x_plus")

        def add_row(e, r):
            return e.tensor_tensor(x_sb, x_sb, each(r, TILES), ALU.add)

        got = carve(arena, [CH] * 2 + [BPC * KEYS0] * 2 + [TPC * D] * 2 + [TPC * KEYS0] * 2 + [TPC * P] * 2)
        qs, ks, vs, sm, pts = got[0:2], *([cut(g, k) for g in got[a:a + 2]] for a, k in ((2, BPC), (4, TPC), (6, TPC), (8, TPC)))
        oT = [[split_arena[:, (2 * b + i) * CH:(2 * b + i + 1) * CH] for i in range(2)] for b in range(4)]
        amax, asum, arec = ([small[:, 80 + 16 * i + 8 * b:84 + 16 * i + 8 * b] for b in range(2)] for i in range(3))
        A = {k: s.phase(2 * UNITS) for k, s in zip(
            "kb q k V qe ke ve S mx sub exp sum rec nrm T pt O oh ol wo acc".split(),
            stages("", 0, "a_kb a_q a_k a_V a_qe a_ke a_ve a_S a_mx a_sub a_exp a_sum a_rec a_nrm a_T a_pt a_O a_oh a_ol a_wo a_acc"))}
        (pt_zero,) = (s.phase(1) for s in stages("", 0, "pt_zero"))
        BQ, BK, BV, BS, BT, BO, BW = 0, 1, 2, (3, 4), 5, 6, 7
        norm0 = norm_phase("layer", 1e-5, lambda l, j: cols[:, bass.ds(l * 4 + (COLS["ln1"][0] + j), 1)], times=2)
        x_plus0 = x_plus.phase(2)

        def head_col(u, what):
            return hbias[u // UPP % 2][:, 2 * what + u % 2:2 * what + u % 2 + 1]

        class Step:

            def __init__(self, t, i, l):
                self.t, self.i, self.l = t, i, l

            def live(self, d):
                return self.i is not None or 0 <= self.t + d < UNITS

            def wait(self, e, name, d=0):
                if self.i is None and self.t + d < 0:
                    return
                n = self.l * UNITS + (self.t + d)
                A[name].wait(e, n if self.i is None else self.i * (2 * UPP) + n)

            def wait_pack(self, e, w):
                n = self.l * NHP + w
                w_lo.wait(e, n if self.i is None else self.i * 2 + n)

        def pe_step(e, z):
            t = z.t
            if z.live(0):
                b = t % 2
                z.wait(e, "qe")
                z.wait(e, "ke")
                z.wait(e, "kb")
                z.wait(e, "sub", -2)
                for n in range(BPC):
                    h = n % 2 * SEQ
                    ins = e.matmul(ps[h:h + SEQ, BS[b], n // 2 * KEYS0:(n // 2 + 1) * KEYS0],
                                   qs[b][:, n * SEQ:(n + 1) * SEQ], ks[b][:, n, :], start=True, stop=True)
                A["S"].done(ins)
            if z.live(1):
                u = t + 1
                w, c, hd = u // UPP, u % UPP // 2, u % 2
                if u % UPP == 0:
                    z.wait_pack(e, w)
                for off, src, bank, name, read in ((0, hT, BQ, "q", "qe"), (2 * D, cT, BK, "k", "ke")):
                    z.wait(e, read)
                    for k in range(KT):
                        a = off + k * D + hd * DH0
                        ins = split3(e, ps[:, bank, :], [x[:, a:a + DH0] for x in W[w % 2]],
                                     [x[:, k, c * CH:(c + 1) * CH] for x in src], k == 0, k == KT - 1)
                    A[name].done(ins)
            if z.live(-1):
                b = (t - 1) % 2
                z.wait(e, "nrm", -1)
                z.wait(e, "pt", -2)
                settled(e)
                for n in range(TPC):
                    ins = e.transpose(ps[0:SEQ, BT, n * P:(n + 1) * P], sm[b][:, n, 0:SEQ], ident)
                A["T"].done(ins)
            if z.live(1):
                u = t + 1
                w, c, hf = u // UPP, u % UPP // 2, u % 2
                z.wait(e, "ve")
                for j in range(2):
                    a = (c * TPC + hf * 2 + j) * P
                    for k in range(KT):
                        ins = split3(e, ps[:, BV, j * D:(j + 1) * D], [x[:, k, a:a + P] for x in cT],
                                     [x[:, (4 + k) * D:(5 + k) * D] for x in W[w % 2]],
                                     j == 0 and k == 0, k == KT - 1)
                A["V"].done(ins)
            if z.live(-1):
                u = t - 1
                z.wait(e, "pt", -1)
                z.wait(e, "ve", -1 if u % 2 else 0)
                z.wait(e, "ol", -2)
                for n in range(TPC):
                    ins = e.matmul(ps[:, BO, n * P:(n + 1) * P], vs[u // 2 % 2][:, n, u % 2 * DH0:(u % 2 + 1) * DH0],
                                   pts[u % 2][:, n, :], start=True, stop=True)
                A["O"].done(ins)
            if z.live(-3):
                v = t - 3
                z.wait(e, "ol", -3 if v % 2 else -2)
                z.wait(e, "acc", -4)
                for j in range(2):
                    a = (v % 2 * 2 + j) * P
                    for hd in range(2):
                        ins = split3(e, ps[:, BW, j * D:(j + 1) * D], [x[:, a:a + P] for x in oT[(v // 2 * 2 + hd) % 4]],
                                     [x[:, (6 + hd) * D:(7 + hd) * D] for x in W[v // UPP % 2]],
                                     j == 0 and hd == 0, hd == 1)
                A["wo"].done(ins)
            if z.live(-4) and (t - 4) % UPP == UPP - 1:
                z.wait(e, "wo", -4)
                e.sem_inc(w_used.sem, 1)

        def act_step(e, z):
            t = z.t
            if z.live(0):
                z.wait(e, "sub")
                A["exp"].done(e.activation(sm[t % 2], sm[t % 2], ACT.Exp, scale=1.0 / math.sqrt(DH0)))
            if z.live(1):
                u = t + 1
                b = u % 2
                if u % UPP == 0:
                    z.wait_pack(e, u // UPP)
                z.wait(e, "S", -1)
                z.wait(e, "q", 1)
                A["qe"].done(e.activation(qs[b], ps[:, BQ, :], ACT.Identity, bias=head_col(u, 0)))
                z.wait(e, "k", 1)
                A["ke"].done(e.activation(ks[b][:, :, 0:SEQ], cut(ps[:, BK, :], BPC), ACT.Identity, bias=head_col(u, 1)))
            if z.live(-1):
                u = t - 1
                z.wait(e, "T", -1)
                z.wait(e, "O", -3)
                src = cut(ps[0:SEQ, BT, :], TPC)
                e.activation(pts[u % 2][0:SEQ, :, 0:SEQ], src[:, :, 0:SEQ], ACT.Copy)
                A["pt"].done(e.activation(pts[u % 2][SEQ:P, :, SEQ:P], src[:, :, SEQ:P], ACT.Copy))
                z.wait(e, "O", -1)
                z.wait(e, "wo", -5 if u % 2 else -4)
                A["oh"].done(e.activation(oT[u % 4][0], ps[:, BO, :], ACT.Identity, bias=head_col(u, 3)))

        def dve_step(e, z):
            t = z.t
            if z.live(1):
                u = t + 1
                if u % UPP == 0:
                    z.wait_pack(e, u // UPP)
                z.wait(e, "S", -1)
                A["kb"].done(e.tensor_copy(ks[u % 2][:, :, SEQ:KEYS0], each(head_col(u, 2), BPC)))
            if z.live(0):
                b = t % 2
                s3 = cut(ps[:, BS[b], 0:TPC * KEYS0], TPC)
                z.wait(e, "S")
                A["mx"].done(e.tensor_reduce(amax[b], s3, axis=AX.X, op=ALU.max))
                z.wait(e, "mx")
                z.wait(e, "T", -2)
                A["sub"].done(e.tensor_tensor(sm[b], s3, many(amax[b], KEYS0), ALU.subtract))
            if z.live(-4):
                v = t - 4
                z.wait(e, "wo", -4)
                xs = x_sb[:, v % UPP * 2:v % UPP * 2 + 2, :]
                z.wait(e, "acc", -5)
                A["acc"].done(e.tensor_tensor(xs, cut(ps[:, BW, :], 2), xs, ALU.add))
            if z.live(0):
                b = t % 2
                z.wait(e, "exp")
                A["sum"].done(e.tensor_reduce(asum[b], sm[b], axis=AX.X, op=ALU.add))
                z.wait(e, "sum")
                A["rec"].done(e.reciprocal(arec[b], asum[b]))
                z.wait(e, "rec")
                A["nrm"].done(e.tensor_tensor(sm[b][:, :, 0:SEQ], sm[b][:, :, 0:SEQ], many(arec[b], SEQ), ALU.mult))
            if z.live(1):
                u = t + 1
                hf = u % 2
                z.wait(e, "V", 1)
                z.wait(e, "O", -2 - hf)
                A["ve"].done(e.tensor_tensor(vs[u // 2 % 2][:, 2 * hf:2 * hf + 2, :], cut(ps[:, BV, :], 2),
                                             each(vdiff[u // UPP % 2], 2), ALU.add))
            if z.live(-1):
                u = t - 1
                z.wait(e, "oh", -1)
                A["ol"].done(e.scalar_tensor_tensor(oT[u % 4][1], ps[:, BO, :], head_col(u, 3),
                                                    oT[u % 4][0].bitcast(F32), ALU.add, ALU.subtract))

        def run_units(e, step, l):
            lead, turn, drain = 5, 2 * UPP, 4
            trips = (UNITS - 1 - lead) // turn
            for t in range(-1, lead):
                step(e, Step(t, None, l))
            with e.Fori(0, trips) as i:
                for t in range(lead, lead + turn):
                    step(e, Step(t, i, l))
            for t in range(lead + trips * turn, UNITS + drain):
                step(e, Step(t, None, l))

        @on("dve")
        def _(e):
            s_small.done(e.memset(minus_half, -0.5))
            c_lo.wait(e, KT - 1)
            e.memset(pts[0], 0.0)
            pt_zero.done(e.memset(pts[1], 0.0))
            e.wait_ge(s_x, 16)
            e.wait_ge(s_const, 32)
            with e.Fori(0, 2) as l:
                norm0["dve"](e, l)
                x_plus0.wait(e, l)
                run_units(e, dve_step, l)
                A["acc"].wait(e, l * UNITS + (UNITS - 1))

        @on("act")
        def _(e):
            e.wait_ge(s_const, 32)
            pt_zero.wait(e, 0)
            with e.Fori(0, 2) as l:
                norm0["act"](e, l)
                run_units(e, act_step, l)

        @on("pe")
        def _(e):
            e.wait_ge(s_const, 32)
            with e.Fori(0, 2) as l:
                norm0["pe"](e, l)
                norm0["lo"].wait(e, l * (KT * NCH) + (KT * NCH - 1))
                c_lo.wait(e, KT - 1)
                run_units(e, pe_step, l)

        @on("pool")
        def _(e):
            for n in range(2):
                split_pack(e, n, n, True)
            s_small.wait(e, 0)
            e.wait_ge(s_const, 32)
            with e.Fori(0, 2) as l:
                norm0["pool"](e, l)
                norm0["x"].wait(e, l * NCH + (NCH - 1))
                x_plus0.done(add_row(e, rows[:, bass.ds(l, 1), :].rearrange("p a d -> p (a d)")))
                with e.Fori(0, NHP // 2) as i:
                    for b in range(2):
                        split_pack(e, l * NHP + i * 2 + (2 + b), b, True)

        (m_x,) = stages("", 0, "m_x")
        M = dict(zip("W1 W2".split(), stages("pe", 2, "m_W1 m_W2")))
        M |= zip("gel gh".split(), stages("act", 2, "m_gel m_gh"))
        M |= zip("gl res".split(), stages("dve", 2, "m_gl m_res"))
        gelu, resid = arena[:, 0:2 * CH], cut(arena[:, 2 * CH:2 * CH + TILES * D], TILES)
        gelu = cut(gelu, 2)
        gsp = [[split_arena[:, (2 * b + i) * CH:(2 * b + i + 1) * CH] for i in range(2)] for b in range(2)]

        def mlp(which, func, kind, eps, norm_name, out_row, residual, before):
            norm = norm_phase(kind, eps, static_affine(norm_name))
            s = {k: v.phase(NCH * (1 if k in ("res",) else FT)) for k, v in M.items()}
            xp = x_plus.phase(1)
            pack = (2 * NHP, 2 * NHP + 3, 2 * NHP + 6)[which]
            b1, b2 = pack % 2, (pack + 1) % 2
            w1, w2 = [cut(w, KT) for w in W[b1]], [cut(w, FT) for w in W[b2]]
            base = x_sb if residual is None else residual

            @on("dve")
            def _(e):
                norm["dve"](e, 0)
                xp.wait(e, 0)
                with e.Fori(0, NCH) as c:
                    for f in range(FT):
                        g = c * FT + f
                        s["gh"].wait(e, g)
                        s["W2"].wait(e, g - 2)
                        s["gl"].done(e.tensor_tensor(gsp[f % 2][1], gelu[:, f % 2, :], gsp[f % 2][0].bitcast(F32), ALU.subtract))
                    s["W2"].wait(e, c * FT + (FT - 1))
                    rt = base[:, bass.ds(c * TPC, TPC), :]
                    s["res"].done(e.tensor_tensor(x_sb[:, bass.ds(c * TPC, TPC), :],
                                                  ps[:, 2:4, :].rearrange("p b (t d) -> p (b t) d", d=D), rt, ALU.add))
                s["res"].wait(e, NCH - 1)

            @on("act")
            def _(e):
                before["act"](e)
                norm["act"](e, 0)
                with e.Fori(0, NCH) as c:
                    for f in range(FT):
                        g = c * FT + f
                        s["W1"].wait(e, g)
                        s["gl"].wait(e, g - 2)
                        s["gel"].done(e.activation(gelu[:, f % 2, :], ps[:, f % 2, :], func, bias=col(f"fb{which}", f)))
                        s["gel"].wait(e, g)
                        s["W2"].wait(e, g - 2)
                        s["gh"].done(e.activation(gsp[f % 2][0], gelu[:, f % 2, :], ACT.Copy))

            @on("pool")
            def _(e):
                norm["pool"](e, 0)
                norm["x"].wait(e, NCH - 1)
                before["pool"](e)
                xp.done(e.tensor_tensor(base, base, each(row(out_row), TILES), ALU.add))
                for n in range(pack + 2, min(pack + 4, NPACK)):
                    split_pack(e, n, n % 2, False)

            @on("pe")
            def _(e):
                norm["pe"](e, 0)
                norm["lo"].wait(e, KT * NCH - 1)
                w_lo.wait(e, pack + 1)

                def up(e, c, f):
                    s["gel"].wait(e, c * FT + (f - 2))
                    for k in range(KT):
                        ins = split3(e, ps[:, f % 2, :], [w[:, k, f * P:(f + 1) * P] for w in w1],
                                     [x[:, k, bass.ds(c * CH, CH)] for x in hT], k == 0, k == KT - 1)
                    s["W1"].done(ins)
                    return ins

                with e.Fori(0, NCH) as c:
                    up(e, c, 0)
                    for f in range(FT):
                        if f + 1 < FT:
                            last_up = up(e, c, f + 1)
                        s["gl"].wait(e, c * FT + f)
                        if f == 0:
                            s["res"].wait(e, c - 1)
                        for j in range(TPC):
                            ins = split3(e, ps[:, 2 + j // 2, j % 2 * D:(j % 2 + 1) * D],
                                         [g[:, j * P:(j + 1) * P] for g in gsp[f % 2]],
                                         [w[:, f, :] for w in w2], f == 0 and j % 2 == 0, f == FT - 1)
                        s["W2"].done(ins)
                s["W2"].wait(e, NCH * FT - 1)
                e.sem_inc(w_used.sem, 2)

            return s

        H = dict(zip("pj S T PV out".split(), stages("pe", 2, "h_pj h_S h_T h_PV h_out")))
        H |= zip("c ea exp pt ah".split(), stages("act", 2, "h_c h_ea h_exp h_pt h_ah"))
        H |= zip("ev m mx sub sum rec a1 a2 al res".split(), stages("dve", 2, "h_ev h_m h_mx h_sub h_sum h_rec h_a1 h_a2 h_al h_res"))
        H |= zip("cl qz nrm".split(), stages("pool", 2, "h_cl h_qz h_nrm"))
        (mask_ready,) = stages("", 0, "mask_ready")
        G = H1 // 2

        def narrow(layer, nk, norm_kind, norm_eps, norm_name, qb, kb, vb, out_row, mask, before):
            own = nk > SEQ
            norm = norm_phase(norm_kind, norm_eps, static_affine(norm_name))
            kvc = BPC * nk
            pack = 2 * NHP + 2 + 3 * (layer - 1)
            wb = W[pack % 2]
            NPJ = KT + KT * kvc // CH + BPC // 2
            per = {"pj": NPJ, "ea": KT + KT * kvc // CH, "ev": BPC // 2, "c": 1, "cl": 1, "ah": 1, "al": 1, "out": 2, "res": 2}
            s = {k: v.phase(NCH * per.get(k, BPC)) for k, v in H.items()}
            xp = x_plus.phase(1)
            mask_ok = mask_ready.phase(1)
            vt = BPC if own else BPC // 2
            mraw, _, qT, v_sb, pt, aT, tmp, maskb, *qz = carve(
                arena, [2 * G * P, 0, KT * CH, vt * D, G * P, KT * CH, KT * SEQ, NB * SEQ] + [KT * HPT * SEQ] * 2)
            tt = [cut(mraw[:, b * G * P:b * G * P + G * nk], G) for b in range(2)]
            (kT,) = carve(norm_arena, [KT * kvc])
            kT = cut(kT, KT)
            qT, v_sb, pt, aT, tmp = cut(qT, KT), cut(v_sb, vt), cut(pt, G), cut(aT, KT), cut(tmp, KT)
            mx, sm_, rc_ = ([small[:, 128 + 16 * i + 8 * b:136 + 16 * i + 8 * b] for b in range(2)] for i in range(3))
            kv = [cut(split_arena[:, 2048 * i:2048 * i + KT * kvc], KT) for i in range(2)]
            asp = [cut(split_arena[:, 2048 * i + 1024 * (0 if own else 1):2048 * i + 1024 * (0 if own else 1) + KT * CH], KT) for i in range(2)]
            kpb = CH // nk

            def kv_parts(i, c):
                for k in range(KT):
                    dst = cut(kv[i][:, k, :], BPC)
                    yield dst[:, :, 0:SEQ], cut(cT[i][:, k, bass.ds(c * CH, CH)], BPC)
                    if own:
                        yield dst[:, :, SEQ:nk], cut(hT[i][:, k, bass.ds(c * CH, CH)], BPC)

            @on("dve")
            def _(e):
                norm["dve"](e, 0)
                e.wait_ge(s_mask, 16 * layer)
                src = mraw.bitcast(I32) if own else mraw.bitcast(U8)[:, 0:NB * SEQ]
                mask_ok.done(e.tensor_scalar(maskb, src, 0.0, NEG, ALU.is_equal, ALU.mult))
                mask_ok.wait(e, 0)
                xp.wait(e, 0)
                with e.Fori(0, NCH) as c:
                    for i in range(BPC // 2):
                        s["pj"].wait(e, c * NPJ + (NPJ - BPC // 2 + i))
                        s["PV"].wait(e, c * BPC - 1)
                        if own:
                            dst, src = v_sb[:, 2 * i:2 * i + 2, :], cut(ps[:, PJB[(NPJ - BPC // 2 + i) % 4], :], 2)
                            ins = e.tensor_tensor(dst, src, each(row(vb), 2), ALU.add)
                        else:
                            ins = e.tensor_tensor(v_sb[:, i, :], ps[:, PJB[(NPJ - BPC // 2 + i) % 4], 0:D], row(vb), ALU.add)
                        s["ev"].done(ins)
                    for u in range(BPC + 1):
                        g = c * BPC + u
                        if u < BPC:
                            b = u % 2
                            sps = ps[:, 2 * b:2 * b + (2 if own else 1), :].rearrange("p b (t n) -> p (b t) n", n=nk)
                            mk = maskb[:, bass.ds(g * SEQ, SEQ)]
                            s["S"].wait(e, g)
                            s["T"].wait(e, g - 2)
                            ins = e.tensor_tensor(tt[b][:, :, 0:SEQ], sps[:, :, 0:SEQ], each(mk, G), ALU.add)
                            if own:
                                ins = e.tensor_copy(tt[b][:, :, SEQ:nk], sps[:, :, SEQ:nk])
                            s["m"].done(ins)
                            s["m"].wait(e, g)
                            s["mx"].done(e.tensor_reduce(mx[b], tt[b], axis=AX.X, op=ALU.max))
                            s["mx"].wait(e, g)
                            s["sub"].done(e.tensor_tensor(tt[b], tt[b], many(mx[b], nk), ALU.subtract))
                        if u >= 1:
                            h = g - 1
                            s["PV"].wait(e, h)
                            xv = cut(ps[:, 6 + (u - 1) % 2, 0:KT * P], KT)
                            s["a2"].wait(e, h - 1)
                            s["a1"].done(e.tensor_scalar(tmp, xv[:, :, SEQ:P], col("odd"), None, ALU.mult))
                            s["a1"].wait(e, h)
                            if u == 1:
                                s["al"].wait(e, c - 1)
                            s["a2"].done(e.scalar_tensor_tensor(aT[:, :, (u - 1) * SEQ:u * SEQ], xv[:, :, 0:SEQ],
                                                                col("even"), tmp, ALU.mult, ALU.add))
                        if u < BPC:
                            s["exp"].wait(e, g)
                            s["sum"].done(e.tensor_reduce(sm_[b], tt[b], axis=AX.X, op=ALU.add))
                            s["sum"].wait(e, g)
                            s["nrm"].wait(e, g - 2)
                            s["rec"].done(e.reciprocal(rc_[b], sm_[b]))
                    s["ah"].wait(e, c)
                    s["al"].done(e.tensor_tensor(asp[1], aT, asp[0].bitcast(F32), ALU.subtract))
                    for i in range(2):
                        s["out"].wait(e, c * 2 + i)
                        xs = x_sb[:, bass.ds(c * TPC + 2 * i, 2), :]
                        s["res"].done(e.tensor_tensor(xs, cut(ps[:, i, :], 2), xs, ALU.add))
                s["res"].wait(e, NCH * 2 - 1)

            @on("act")
            def _(e):
                before["act"](e)
                raw_mask = mraw.bitcast(I32) if own else mraw.bitcast(U8)[:, 0:NB * SEQ]
                e.dma_start(raw_mask, mask.rearrange("b s -> (b s)").partition_broadcast(P)).then_inc(s_mask, 16)
                norm["act"](e, 0)
                norm["lo"].wait(e, KT * NCH - 1)
                with e.Fori(0, NCH) as c:
                    s["out"].wait(e, c * 2 - 1)
                    s["pj"].wait(e, c * NPJ - 1)
                    for dst, src in kv_parts(0, c):
                        ins = e.activation(dst, src.bitcast(F32), ACT.Copy)
                    s["c"].done(ins)
                    for i in range(NPJ - BPC // 2):
                        s["pj"].wait(e, c * NPJ + i)
                        bank = ps[:, PJB[i % 4], :]
                        if i == 0:
                            s["qz"].wait(e, c * BPC - 1)
                        if i == KT:
                            s["S"].wait(e, c * BPC - 1)
                        if i < KT:
                            s["ea"].done(e.activation(qT[:, i, :], bank, ACT.Identity, bias=col(qb, i)))
                        else:
                            k, a = (i - KT) // (kvc // CH), (i - KT) % (kvc // CH)
                            s["ea"].done(e.activation(kT[:, k, a * CH:(a + 1) * CH], bank, ACT.Identity, bias=col(kb, k)))
                    for u in range(BPC + 1):
                        g = c * BPC + u
                        if u < BPC:
                            s["sub"].wait(e, g)
                            s["exp"].done(e.activation(tt[u % 2], tt[u % 2], ACT.Exp, scale=1.0 / (DH1 if own else math.sqrt(DH1))))
                        if u >= 1:
                            h, b = g - 1, (u - 1) % 2
                            s["T"].wait(e, h)
                            s["PV"].wait(e, h - 1)
                            at = 0 if own else b * SEQ
                            src = ps[0:nk, 4:6, :].rearrange("p b (t n) -> p (b t) n", n=P)
                            s["pt"].done(e.activation(pt[at:at + nk, :, :], src, ACT.Copy))
                    s["a2"].wait(e, c * BPC + (BPC - 1))
                    s["pj"].wait(e, c * NPJ + (NPJ - 1))
                    s["ah"].done(e.activation(asp[0], aT, ACT.Copy))

            @on("pool")
            def _(e):
                norm["pool"](e, 0)
                norm["x"].wait(e, NCH - 1)
                before["pool"](e)
                xp.done(e.tensor_tensor(x_sb, x_sb, each(row(out_row), TILES), ALU.add))
                norm["lo"].wait(e, KT * NCH - 1)
                with e.Fori(0, NCH) as c:
                    s["out"].wait(e, c * 2 - 1)
                    s["pj"].wait(e, c * NPJ - 1)
                    settled(e)
                    for dst, src in kv_parts(1, c):
                        ins = e.tensor_copy(dst, src)
                    s["cl"].done(ins)
                    for u in range(BPC + 1):
                        g = c * BPC + u
                        if u < BPC:
                            if u == 0:
                                s["ea"].wait(e, c * (NPJ - BPC // 2) + (KT - 1))
                            s["S"].wait(e, g - 2)
                            for k in range(KT):
                                ins = e.tensor_tensor(
                                    cut(qz[u % 2][:, k * HPT * SEQ:(k + 1) * HPT * SEQ], HPT),
                                    each(qT[:, k, u * SEQ:(u + 1) * SEQ], HPT), many(col("hmask", 0, HPT), SEQ), ALU.mult)
                            s["qz"].done(ins)
                        if u >= 1:
                            h, b = g - 1, (u - 1) % 2
                            s["rec"].wait(e, h)
                            s["nrm"].done(e.tensor_tensor(tt[b], tt[b], many(rc_[b], nk), ALU.mult))
                if pack + 2 < NPACK:
                    split_pack(e, pack + 2, pack % 2, False)

            @on("pe")
            def _(e):
                norm["pe"](e, 0)
                norm["lo"].wait(e, KT * NCH - 1)
                w_lo.wait(e, pack)
                with e.Fori(0, NCH) as c:
                    s["c"].wait(e, c)
                    s["cl"].wait(e, c)
                    s["sub"].wait(e, c * BPC - 1)
                    s["res"].wait(e, c * 2 - 1)
                    for i in range(NPJ):
                        if i >= 4:
                            if i - 4 < NPJ - BPC // 2:
                                s["ea"].wait(e, c * (NPJ - BPC // 2) + (i - 4))
                            else:
                                s["ev"].wait(e, c * (BPC // 2) + (i - 4 - NPJ + BPC // 2))
                        bank = ps[:, PJB[i % 4], :]
                        if i < NPJ - BPC // 2:
                            for k in range(KT):
                                if i < KT:
                                    a = k * D + i * P
                                    rhs = [x[:, k, bass.ds(c * CH, CH)] for x in hT]
                                else:
                                    m, q = (i - KT) // (kvc // CH), (i - KT) % (kvc // CH)
                                    a = 2 * D + k * D + m * P
                                    rhs = [x[:, k, q * CH:(q + 1) * CH] for x in kv]
                                ins = split3(e, bank, [w[:, a:a + P] for w in wb], rhs, k == 0, k == KT - 1)
                        else:
                            j = i - (NPJ - BPC // 2)
                            for m in range(2 if own else 1):
                                a = ((2 * j + m) if own else j) * P
                                for k in range(KT):
                                    ins = split3(e, bank[:, m * D:(m + 1) * D], [x[:, k, a:a + P] for x in kv],
                                                 [w[:, (4 + k) * D:(5 + k) * D] for w in wb], m == 0 and k == 0, k == KT - 1)
                        s["pj"].done(ins)
                    s["ea"].wait(e, (c + 1) * (NPJ - BPC // 2) - 1)
                    s["ev"].wait(e, (c + 1) * (BPC // 2) - 1)
                    for u in range(BPC + 1):
                        g = c * BPC + u
                        if u < BPC:
                            s["qz"].wait(e, g)
                            s["sub"].wait(e, g - 2)
                            s["m"].wait(e, g - 2)
                            for n in range(G):
                                k, a = n * 2 // HPT, n * 2 % HPT * SEQ
                                ins = e.matmul(ps[:, 2 * (u % 2) + n * nk // 512, n * nk % 512:n * nk % 512 + nk],
                                               qz[u % 2][:, k * HPT * SEQ + a:k * HPT * SEQ + a + P],
                                               kT[:, k, u * nk:(u + 1) * nk], start=True, stop=True)
                            s["S"].done(ins)
                        if u >= 1:
                            h, b = g - 1, (u - 1) % 2
                            s["nrm"].wait(e, h)
                            s["pt"].wait(e, h - 1)
                            settled(e)
                            for n in range(G):
                                ins = e.transpose(ps[0:nk, 4 + n // 4, n % 4 * P:(n % 4 + 1) * P], tt[b][:, n, :], ident)
                            s["T"].done(ins)
                            s["pt"].wait(e, h)
                            s["a2"].wait(e, h - 2)
                            at = 0 if own else b * SEQ
                            settled(e)
                            for n in range(G):
                                k, r = n * 2 // HPT, n % 4 * 2 * DH1
                                ins = e.matmul(ps[r:r + 2 * DH1, 6 + b, k * P:(k + 1) * P],
                                               v_sb[at:at + nk, u - 1 if own else (u - 1) // 2, n * 2 * DH1:(n + 1) * 2 * DH1],
                                               pt[at:at + nk, n, :], start=True, stop=True)
                            s["PV"].done(ins)
                    s["al"].wait(e, c)
                    for i in range(2):
                        for j in range(2):
                            a = (2 * i + j) * P
                            for k in range(KT):
                                ins = split3(e, ps[:, i, j * D:(j + 1) * D], [x[:, k, a:a + P] for x in asp],
                                             [w[:, (6 + k) * D:(7 + k) * D] for w in wb], j == 0 and k == 0, k == KT - 1)
                        s["out"].done(ins)
                s["out"].wait(e, 2 * NCH - 1)
                e.sem_inc(w_used.sem, 1)

            return s


        def nothing(e):
            return None

        def after(steps, n):
            return lambda e: steps.wait(e, n)

        mlp0 = mlp(0, ACT.Gelu, "layer", 1e-5, "lnm", "b_fc2", None, {"act": nothing, "pool": nothing})

        def spill_tokens(e):
            mlp0["res"].wait(e, NCH - 1)
            e.dma_start(spill.rearrange("(t p) d -> p t d", p=P), x_sb).then_inc(s_spill, 16)

        narrow1 = narrow(1, 2 * SEQ, "none", 0.0, "one", "l1q", "l1k", "l1v", "out_b", mask1,
                         {"act": spill_tokens, "pool": lambda e: e.wait_ge(s_spill, 16)})

        def fetch_tokens(e):
            narrow1["res"].wait(e, 2 * NCH - 1)
            e.dma_start(resid, spill.rearrange("(t p) d -> p t d", p=P)).then_inc(s_back, 16)

        mlp1 = mlp(1, ACT.Gelu_apprx_tanh, "rms", 1e-6, "rms", "mlp_b2", resid,
                   {"act": fetch_tokens, "pool": lambda e: e.wait_ge(s_back, 16)})
        narrow2 = narrow(2, SEQ, "layer", 1e-5, "l2n", "l2q", "l2k", "l2v", "cproj_b", mask2,
                         {"act": after(mlp1["res"], NCH - 1), "pool": nothing})
        mlp2 = mlp(2, ACT.Gelu_apprx_tanh, "layer", 1e-5, "l2m", "proj_b", None, {"act": nothing, "pool": nothing})

        Z = {k: v.phase(TILES) for k, v in zip(
            "F pj T Y wy".split(), stages("pe", 2, "z_F z_pj z_T z_Y z_wy"))}
        Z |= {k: v.phase(TILES) for k, v in zip("exp pe pt ye".split(), stages("act", 2, "z_exp z_pe z_pt z_ye"))}
        Z |= {k: v.phase(TILES) for k, v in zip("mx sub sum rec ge we st".split(),
                                                 stages("dve", 2, "z_mx z_sub z_sum z_rec z_ge z_we z_st"))}
        Z |= {k: v.phase(TILES) for k, v in zip("xc nrm".split(), stages("pool", 2, "z_xc z_nrm"))}
        (z_c,) = (s.phase(16) for s in stages("", 0, "z_c"))
        (z_o,) = (s.phase(NCH) for s in stages("", 0, "z_o"))
        (z_p,) = (s.phase(1) for s in stages("", 0, "z_p"))
        s_ct = [semaphore(f"s_ct{b}") for b in range(2)]
        got = carve(arena, [D] * 8 + [2 * 2 * CI] * 2 + [4 * D] * 2 + [4 * D] + [D] * 2 + [TILES * D])
        xc, cx, th, ph = got[0:2], got[2:4], got[4:6], got[6:8]
        gx = [cut(g, 2) for g in got[8:10]]
        ff = [cut(g, 4) for g in got[10:12]]
        fT, yT, wy = got[12], got[13:15], cut(got[15], TILES)
        bst = cut(norm_arena[:, 0:2 * TILES * 6], 2 * TILES)
        zmx, zsum, zrec = ([small[:, 192 + 8 * i + 4 * b:196 + 8 * i + 4 * b] for b in range(2)] for i in range(3))
        zs = [small[:, 216 + i:217 + i] for i in range(12)]

        class Tile:
            def __init__(self, t, i):
                self.t, self.i = t, i

            def live(self, d):
                return self.i is not None or 0 <= self.t + d < TILES

            def n(self, d=0):
                return self.t + d if self.i is None else self.i * 2 + (self.t + d)

            def wait(self, e, name, d=0):
                Z[name].wait(e, self.n(d))

        def z_pe(e, z):
            t = z.t
            if z.live(0):
                b = t % 2
                z.wait(e, "pe")
                z.wait(e, "sub", -1)
                for q in range(4):
                    r = q // 2 * CI
                    ins = e.matmul(ps[:, 2 + q // 2, q % 2 * D:(q % 2 + 1) * D], ph[b][r:r + CI, q % 2 * P:(q % 2 + 1) * P],
                                   th[b][r:r + CI, :], start=True, stop=True)
                Z["F"].done(ins)
            if z.live(1):
                b = (t + 1) % 2
                z.wait(e, "xc", 1)
                e.wait_ge(s_ct[b], 16 * ((t + 1) // 2 + 1) if z.i is None else z.i * 16 + 16 * ((t + 1) // 2 + 1))
                z.wait(e, "pe")
                z.wait(e, "ge")
                e.matmul(ps[0:2 * CI, 0, 0:D], col("wth", 0, 2 * CI), xc[b], start=True, stop=True)
                e.matmul(ps[0:2 * CI, 0, D:2 * D], col("wph", 0, 2 * CI), cx[b], start=True, stop=True)
                for q in range(2):
                    ins = e.matmul(ps[:, 1, q * 2 * CI:(q + 1) * 2 * CI], xc[b][:, q * P:(q + 1) * P],
                                   col("wg", 0, 2 * CI), start=True, stop=True)
                Z["pj"].done(ins)
            if z.live(-1):
                b = (t - 1) % 2
                z.wait(e, "nrm", -1)
                z.wait(e, "pt", -2)
                for a in range(2):
                    for jh in range(2):
                        for ih in range(2):
                            at = (2 * jh + ih) * P
                            ins = e.transpose(ps[:, 4 + a, at:at + P], ff[b][:, 2 * a + ih, jh * P:(jh + 1) * P], ident)
                Z["T"].done(ins)
                z.wait(e, "pt", -1)
                z.wait(e, "ye", -2)
                for a in range(2):
                    for jh in range(2):
                        ins = e.matmul(ps[a * CI:(a + 1) * CI, 6, 0:D], gx[b][:, jh, a * CI:(a + 1) * CI],
                                       fT[:, (2 * a + jh) * D:(2 * a + jh + 1) * D], start=jh == 0, stop=jh == 1)
                Z["Y"].done(ins)
                z.wait(e, "ye", -1)
                z.wait(e, "we", -2)
                Z["wy"].done(e.matmul(ps[:, 7, 0:D], col("wz", 0, P)[0:2 * CI, :], yT[b][0:2 * CI, :], start=True, stop=True))

        def z_act(e, z):
            t = z.t
            if z.live(0):
                z.wait(e, "sub")
                Z["exp"].done(e.activation(ff[t % 2], ff[t % 2], ACT.Exp))
            if z.live(1):
                b = (t + 1) % 2
                z.wait(e, "pj", 1)
                z.wait(e, "F", -1)
                e.activation(th[b][0:2 * CI, :], ps[0:2 * CI, 0, 0:D], ACT.Identity, bias=col("bth")[0:2 * CI, :])
                Z["pe"].done(e.activation(ph[b][0:2 * CI, :], ps[0:2 * CI, 0, D:2 * D], ACT.Identity, bias=col("bph")[0:2 * CI, :]))
            if z.live(-1):
                z.wait(e, "T", -1)
                z.wait(e, "Y", -2)
                Z["pt"].done(e.activation(cut(fT, 2), ps[:, 4:6, :], ACT.Copy))
                z.wait(e, "Y", -1)
                z.wait(e, "wy", -3)
                Z["ye"].done(e.activation(yT[(t - 1) % 2][0:2 * CI, :], ps[0:2 * CI, 6, 0:D], ACT.Copy))

        def z_dve(e, z):
            t = z.t
            if z.live(0):
                b = t % 2
                f4 = ps[:, 2:4, :].rearrange("p b (q n) -> p (b q) n", n=D)
                z.wait(e, "F")
                Z["mx"].done(e.tensor_reduce(zmx[b], f4, axis=AX.X, op=ALU.max))
                z.wait(e, "mx")
                z.wait(e, "T", -2)
                Z["sub"].done(e.tensor_tensor(ff[b], f4, many(zmx[b], D), ALU.subtract))
            if z.live(1):
                b = (t + 1) % 2
                z.wait(e, "pj", 1)
                z.wait(e, "Y", -1)
                Z["ge"].done(e.tensor_tensor(gx[b], cut(ps[:, 1, 0:4 * CI], 2), each(row("bg")[:, 0:2 * CI], 2), ALU.add))
            if z.live(0):
                b = t % 2
                z.wait(e, "exp")
                Z["sum"].done(e.tensor_reduce(zsum[b], ff[b], axis=AX.X, op=ALU.add))
                z.wait(e, "sum")
                z.wait(e, "nrm", -2)
                Z["rec"].done(e.reciprocal(zrec[b], zsum[b]))
            if z.live(-1):
                z.wait(e, "wy", -1)
                dst = wy[:, bass.ds(z.n(-1), 1), :].rearrange("p a d -> p (a d)")
                Z["we"].done(e.tensor_scalar(dst, ps[:, 7, 0:D], col("bz"), None, ALU.add))
                z.wait(e, "we", -1)
                Z["st"].done(e.bn_stats(bst[:, bass.ds(z.n(-1), 1), :].rearrange("p a d -> p (a d)"), dst))

        def z_pool(e, z):
            t = z.t
            if z.live(1):
                b = (t + 1) % 2
                z.wait(e, "pj", -1)
                settled(e)
                Z["xc"].done(e.tensor_copy(xc[b], x_sb[:, bass.ds(z.n(1), 1), :].rearrange("p a d -> p (a d)")))
            if z.live(0):
                b = t % 2
                z.wait(e, "rec")
                Z["nrm"].done(e.tensor_tensor(ff[b], ff[b], many(zrec[b], D), ALU.mult))

        def run_tiles(e, step):
            lead, drain = 3, 2
            trips = (TILES - 1 - lead) // 2
            for t in range(-1, lead):
                step(e, Tile(t, None))
            with e.Fori(0, trips) as i:
                for t in range(lead, lead + 2):
                    step(e, Tile(t, i))
            for t in range(lead + 2 * trips, TILES + drain - 1):
                step(e, Tile(t, None))

        @on("sp")
        def _(e):
            mlp2["res"].wait(e, NCH - 1)
            with e.Fori(0, TILES // 2) as i:
                for b in range(2):
                    Z["pj"].wait(e, i * 2 + (b - 2))
                    e.dma_start(cx[b], ctx_tok[bass.ds(i * 2 + b, 1), :, :].rearrange("a p d -> (a p) d")).then_inc(s_ct[b], 16)

        @on("pe")
        def _(e):
            run_tiles(e, z_pe)

        @on("act")
        def _(e):
            mlp2["res"].wait(e, NCH - 1)
            run_tiles(e, z_act)

        @on("pool")
        def _(e):
            mlp2["res"].wait(e, NCH - 1)
            run_tiles(e, z_pool)
            z_c.wait(e, 2)
            z_p.done(e.tensor_tensor(zs[3][0:SEQ, :], zs[2][0:SEQ, :], minus_half[0:SEQ, 0:1], ALU.pow))

        @on("dve")
        def _(e):
            run_tiles(e, z_dve)
            lower = slice(0, SEQ)
            count = [0]

            def then(ins):
                z_c.done(ins)
                z_c.wait(e, count[0])
                count[0] += 1

            Z["st"].wait(e, TILES - 1)
            then(e.tensor_copy(bst[lower, TILES:2 * TILES, :], bst[SEQ:P, 0:TILES, :]))
            then(e.bn_aggr(zs2, bst[lower, :, :].rearrange("p t s -> p (t s)")))
            then(e.tensor_scalar(zs[2][lower, :], zs2[:, 1:2], 1e-5, None, ALU.add))
            z_p.wait(e, 0)
            then(e.tensor_tensor(zs[4][lower, :], zs[3][lower, :], zs[3][lower, :], ALU.mult))
            then(e.tensor_tensor(zs[5][lower, :], zs[4][lower, :], zs[2][lower, :], ALU.mult))
            then(e.tensor_scalar(zs[6][lower, :], zs[5][lower, :], -0.5, 1.5, ALU.mult, ALU.add))
            then(e.tensor_tensor(zs[7][lower, :], zs[3][lower, :], zs[6][lower, :], ALU.mult))
            e.tensor_copy(zs[8][lower, :], zs2[:, 0:1])
            e.tensor_copy(zs[8][SEQ:P, :], zs2[:, 0:1])
            e.tensor_copy(zs[9][lower, :], zs[7][lower, :])
            then(e.tensor_copy(zs[9][SEQ:P, :], zs[7][lower, :]))
            then(e.tensor_tensor(zs[10], zs[9], col("gam"), ALU.mult))
            for c in range(NCH):
                w = wy[:, c * TPC:(c + 1) * TPC, :]
                then(e.tensor_scalar(w, w, zs[8], zs[10], ALU.subtract, ALU.mult))
                z_o.done(e.scalar_tensor_tensor(x_sb[:, c * TPC:(c + 1) * TPC, :], w, col("bet"),
                                                x_sb[:, c * TPC:(c + 1) * TPC, :], ALU.add, ALU.add))

        zs2 = small[0:SEQ, 232:234]

        @on("sp")
        def _(e):
            to = out.rearrange("(t p) d -> p t d", p=P)
            for c in range(NCH):
                z_o.wait(e, c)
                e.dma_start(to[:, c * TPC:(c + 1) * TPC, :], x_sb[:, c * TPC:(c + 1) * TPC, :]).then_inc(s_out, 16)
            e.wait_ge(s_out, 16 * NCH)
            e.wait_ge(s_spill, 16)

        block = ctx.enter_context(nc.Block())

        def program(name):
            def run(e):
                for s in owned.get(name, ()):
                    e.sem_inc(s.sem, s.ahead)
                for f in todo[name]:
                    f(e)
            return run

        block.sync(program("sp"))
        block.scalar(program("act"))
        block.vector(program("dve"))
        block.gpsimd(program("pool"))
        block.tensor(program("pe"))


def kernel(**inputs):
    import concourse.bacc as bacc
    from concourse.bass_utils import run_bass_kernel_spmd

    v = {k: np.asarray(a) for k, a in inputs.items()}
    f0, f1, f2, f3 = (f"L{i}_xattn_" for i in range(4))

    def rows_on_partitions(w):
        return w.reshape(-1, P, w.shape[1]).transpose(1, 0, 2).reshape(P, -1)

    packs, pairs = [], []
    zero8 = np.zeros((P, 8), np.float32)
    for a in (1, 2):
        g = {n: v[f"{f0}{n}{a}"] for n in ("wq", "wk", "wv", "wo", "bq", "bk", "bv", "bias_k", "bias_v")}
        for w in range(NHP):
            c = slice(w * 2 * DH0, (w + 1) * 2 * DH0)
            bias = [g[n].reshape(-1)[c].reshape(2, DH0).T for n in ("bq", "bk", "bias_k", "bias_v")]
            packs.append([rows_on_partitions(g["wq"][:, c]), rows_on_partitions(g["wk"][:, c]),
                          rows_on_partitions(g["wv"][:, c]), rows_on_partitions(g["wo"][c, :]), *bias])
            pairs.append([g["bv"][c], g["bias_v"].reshape(-1)[c]])
    kv = v[f1 + "kv_w"].reshape(D, D, 2)
    kvb = v[f1 + "kv_b"].reshape(D, 2)
    packs += [[rows_on_partitions(v[f0 + "w_fc1"]), zero8], [rows_on_partitions(v[f0 + "w_fc2"]), zero8],
              [*(rows_on_partitions(w) for w in (v[f1 + "q_w"], kv[:, :, 0], kv[:, :, 1], v[f1 + "out_w"])), zero8],
              [rows_on_partitions(v[f1 + "mlp_w1"]), zero8], [rows_on_partitions(v[f1 + "mlp_w2"]), zero8],
              [*(rows_on_partitions(v[f2 + n]) for n in ("q_w", "k_w", "v_w", "cproj_w")), zero8],
              [rows_on_partitions(v[f2 + "fc_w"]), zero8], [rows_on_partitions(v[f2 + "proj_w"]), zero8]]
    wpack = np.stack([np.concatenate(p, axis=1) for p in packs])
    pairs += [[np.zeros(2 * DH0, np.float32)] * 2] * 2
    vb = np.stack([np.concatenate(p) for p in pairs])

    consts = np.zeros((P, NCOL), np.float32)

    def put(name, *vectors):
        blocks = [a.reshape(-1, P).T if a.ndim == 1 else a for a in vectors]
        block = np.concatenate(blocks, axis=1)
        consts[:block.shape[0], COLS[name][0]:COLS[name][0] + block.shape[1]] = block

    one, nil = np.ones(D, np.float32), np.zeros(D, np.float32)
    put("ln1", v[f0 + "ln1_scale"], v[f0 + "ln1_offset"])
    put("ln2", v[f0 + "ln2_scale"], v[f0 + "ln2_offset"])
    put("lnm", v[f0 + "ln_mlp_scale"], v[f0 + "ln_mlp_offset"])
    put("l1q", v[f1 + "q_b"])
    put("l1k", kvb[:, 0])
    put("rms", v[f1 + "postnorm_w"], nil)
    put("l2n", v[f2 + "ln1_w"], v[f2 + "ln1_b"])
    put("l2q", v[f2 + "q_b"])
    put("l2k", v[f2 + "k_b"])
    put("l2m", v[f2 + "ln2_w"], v[f2 + "ln2_b"])
    put("fb0", v[f0 + "b_fc1"])
    put("fb1", v[f1 + "mlp_b1"])
    put("fb2", v[f2 + "fc_b"])
    put("one", one, nil)
    for name, w in (("bth", "btheta"), ("bph", "bphi"), ("bz", "bz"), ("gam", "gamma"), ("bet", "beta")):
        put(name, np.tile(v[f3 + w], 2)[:, None])
    p = np.arange(P)
    put("hmask", (p[:, None] // DH1 == np.arange(HPT)).astype(np.float32))
    put("even", (p // DH1 % 2 == 0).astype(np.float32)[:, None])
    put("odd", (p // DH1 % 2 == 1).astype(np.float32)[:, None])
    put("ident", np.eye(P, dtype=np.float32))

    def twice(w):
        z = np.zeros((2 * w.shape[0], 2 * w.shape[1]), np.float32)
        z[:w.shape[0], :w.shape[1]] = z[w.shape[0]:, w.shape[1]:] = w
        return z

    put("wth", twice(v[f3 + "Wtheta"].T))
    put("wph", twice(v[f3 + "Wphi"].T))
    put("wg", twice(v[f3 + "Wg"].T))
    put("wz", twice(v[f3 + "Wz"].T))

    bg = np.concatenate([v[f3 + "bg"], v[f3 + "bg"], np.zeros(D - 2 * CI, np.float32)])
    rows = np.concatenate([v[f0 + "bo1"], v[f0 + "bo2"], v[f0 + "b_fc2"], v[f1 + "out_b"], v[f1 + "mlp_b2"],
                           v[f2 + "cproj_b"], v[f2 + "proj_b"], kvb[:, 1], v[f2 + "v_b"], bg])
    ctx_tok = v["ctx_2048"].reshape(TILES, P, D)
    arrays = {
        "wpack": wpack, "ctxT": v["ctx_2048"].reshape(TOK, D).T, "ctx_tok": ctx_tok, "x_in": v["x"].reshape(TOK, D),
        "mask1": v["mask_BxS2_ik0"], "mask2": v["mask_BxS2_bf1"].view(np.uint8), "cols_in": consts,
        "rows_in": rows, "vb_in": vb,
    }
    arrays = {k: np.ascontiguousarray(a) for k, a in arrays.items()}
    nc = bacc.Bacc("TRN2", target_bir_lowering=False, num_devices=1)
    aps = {k: nc.dram_tensor(k, a.shape, mybir.dt.from_np(a.dtype), kind="ExternalInput").ap() for k, a in arrays.items()}
    out = nc.dram_tensor("out", (TOK, D), F32, kind="ExternalOutput").ap()
    spill = nc.dram_tensor("spill", (TOK, D), F32, kind="Internal").ap()
    build(nc, **aps, out=out, spill=spill)
    got = run_bass_kernel_spmd(nc, [arrays], core_ids=[0])
    return got.results[0]["out"].reshape(NB, SEQ, D)
```

```python
import math
from contextlib import ExitStack

import numpy as np

import concourse.bass as bass
from concourse import mybir
from concourse.alu_op_type import AluOpType as ALU

F32 = mybir.dt.float32
F32R = mybir.dt.float32r
I32 = mybir.dt.int32
U8 = mybir.dt.uint8
BF16 = mybir.dt.bfloat16
ACT = mybir.ActivationFunctionType
AX = mybir.AxisListType

P = 128
NB, SEQ, D = 32, 64, 256
TOK = NB * SEQ
TILES = TOK // P
KT = D // P
FF = 4 * D
FT = FF // P
CH = 512
NCH = TOK // CH
TPC = CH // P
BPC = CH // SEQ
H0, DH0 = 16, 128
H1, DH1 = 16, 16
HPT = P // DH1
NHP = H0 // 2
UPP = 2 * NCH
UNITS = NHP * UPP
KEYS0 = SEQ + 1
CI = 32
PACK = 2048
PCOLS = PACK + 8
NPACK = 2 * NHP + 8
NEG = -3.3895313892515355e38

COLS = {}


def _col(name, n):
    COLS[name] = (sum(k for _, k in COLS.values()), n)


for _name, _n in (("ln1", 4), ("ln2", 4), ("lnm", 4), ("l1q", 2), ("l1k", 2), ("rms", 4), ("l2n", 4),
                  ("l2q", 2), ("l2k", 2), ("l2m", 4), ("fb0", FT), ("fb1", FT), ("fb2", FT),
                  ("one", 4), ("bth", 1), ("bph", 1), ("bz", 1), ("gam", 1), ("bet", 1),
                  ("hmask", HPT), ("even", 1), ("odd", 1),
                  ("wth", 2 * CI), ("wph", 2 * CI), ("wg", 2 * CI), ("wz", P), ("ident", P)):
    _col(_name, _n)
NCOL = sum(k for _, k in COLS.values())
ARENA = 12432
PJB = (0, 1, 2, 3)
ROWS = ("bo1", "bo2", "b_fc2", "out_b", "mlp_b2", "cproj_b", "proj_b", "l1v", "l2v", "bg")



class Steps:

    def __init__(self, sem, base):
        self.sem, self.base = sem, base

    def done(self, ins):
        ins.then_inc(self.sem, 1)

    def wait(self, eng, n):
        eng.wait_ge(self.sem, n + (self.base + 1))


class Stage:

    def __init__(self, sem, ahead):
        self.sem, self.total, self.ahead = sem, ahead, ahead

    def phase(self, steps):
        got = Steps(self.sem, self.total)
        self.total += steps
        return got


def build(nc, wpack, ctxT, ctx_tok, x_in, mask1, mask2, cols_in, rows_in, vb_in, out, spill):
    ctx = ExitStack()
    with ctx:
        def sb(name, cols, dt=F32):
            return ctx.enter_context(nc.sbuf_tensor(name, [P, cols], dt))

        def semaphore(name):
            return ctx.enter_context(nc.semaphore(name))

        owned = {e: [] for e in ("pe", "act", "dve", "pool")}

        def stages(owner, ahead, names):
            got = []
            for name in names.split():
                s = Stage(semaphore(name), ahead)
                if ahead:
                    owned[owner].append(s)
                got.append(s)
            return got

        def cut(t, k):
            return t.rearrange("p (k n) -> p k n", k=k)

        def many(t, n):
            return t.rearrange("p (k a) -> p k a", a=1).to_broadcast([P, t.shape[1], n])

        def each(t, k):
            return t.rearrange("p (a n) -> p a n", a=1).to_broadcast([P, k, t.shape[1]])

        x_sb = cut(sb("x_sb", TILES * D)[:, :], TILES)
        cT = [cut(sb(f"cT{i}", KT * TOK, F32R)[:, :], KT) for i in range(2)]
        hT = [cut(sb(f"hT{i}", KT * TOK, F32R)[:, :], KT) for i in range(2)]
        W = [[sb(f"W{b}{i}", PACK, F32R)[:, :] for i in range(2)] for b in range(2)]
        raw = sb("raw", PCOLS)
        hbias = [sb(f"hbias{b}", 8)[:, :] for b in range(2)]
        cols = sb("cols", NCOL)
        rows = cut(sb("rows", len(ROWS) * D)[:, :], len(ROWS))
        split_arena = sb("split_arena", 4096, F32R)
        norm_arena = sb("norm_arena", KT * CH + TPC * D)
        arena = sb("arena", ARENA)
        small = sb("small", 256)
        ps = ctx.enter_context(nc.psum_tensor("ps", [P, 8, 512], F32))

        def carve(tensor, sizes):
            at, got = 0, []
            for n in sizes:
                got.append(tensor[:, at:at + n])
                at += n
            assert at <= tensor.shape[1], (at, tensor.shape)
            return got

        def col(name, j=0, n=1):
            a = COLS[name][0] + j
            return cols[:, a:a + n]

        def row(name):
            return rows[:, ROWS.index(name), :]

        ident = col("ident", 0, P)

        s_cols, s_rows, s_ctx, s_raw, s_vb, s_mask, s_spill, s_back, s_out = (
            semaphore("s_" + s) for s in "cols rows ctx raw vb mask spill back out".split())
        s_x = [semaphore(f"s_x{c}") for c in range(NCH)]

        todo = {e: [] for e in ("pe", "act", "dve", "pool", "sp")}

        def on(engine):
            def keep(f):
                todo[engine].append(f)
                return f
            return keep

        def settled(e):
            e.sem_inc(s_turn, 1)

        s_turn = semaphore("s_turn")

        def split3(e, dst, lhs, rhs, start, stop):
            for n, (a, b) in enumerate(((0, 0), (0, 1), (1, 0))):
                last = e.matmul(dst, lhs[a], rhs[b], start=start and n == 0, stop=stop and n == 2,
                                skip_group_check=True)
            return last

        (w_used,) = stages("pe", 2, "w_used")
        (w_lo,) = stages("pool", 2, "w_lo")
        (v_diff,) = stages("pool", 2, "v_diff")
        w_used, w_lo, v_diff = (s.phase(NPACK) for s in (w_used, w_lo, v_diff))
        NPAIR = 2 * NHP + 2

        F_PIECES = 4
        (p_hi,) = (s.phase(NPACK) for s in stages("", 0, "p_hi"))
        (f_hi,) = (s.phase(NPACK * F_PIECES) for s in stages("", 0, "f_hi"))
        vraw = arena[:, ARENA - 4 * D:ARENA - 2 * D]
        vdiff = [arena[:, ARENA - (2 - b) * D:ARENA - (1 - b) * D] for b in range(2)]

        def pair_bias(e, n, b):
            e.wait_ge(s_vb, n * 16 + 16)
            w_used.wait(e, n - 2)
            v_diff.done(e.tensor_tensor(vdiff[b], vraw[:, 0:D], vraw[:, D:2 * D], ALU.subtract))

        def split_pool(e, n, b, nth, pair):
            if pair:
                pair_bias(e, n, b)
            e.wait_ge(s_raw, n * 16 + 16)
            w_used.wait(e, n - 2)
            settled(e)
            if pair:
                e.tensor_copy(hbias[b], raw[:, PACK:PCOLS])
            p_hi.done(e.tensor_copy(W[b][0], raw[:, 0:PACK]))
            p_hi.wait(e, nth)
            w_lo.done(e.tensor_tensor(W[b][1], raw[:, 0:PACK], W[b][0].bitcast(F32), ALU.subtract))

        def split_act(e, n, b, nth, pair):
            e.wait_ge(s_raw, n * 16 + 16)
            w_used.wait(e, n - 2)
            if pair:
                e.activation(hbias[b], raw[:, PACK:PCOLS], ACT.Copy)
            for k in range(F_PIECES):
                a = slice(k * PACK // F_PIECES, (k + 1) * PACK // F_PIECES)
                f_hi.done(e.activation(W[b][0][:, a], raw[:, a], ACT.Copy))

        def split_dve(e, n, b, nth, pair=False):
            if pair:
                pair_bias(e, n, b)
            w_lo.wait(e, n - 1)
            for k in range(F_PIECES):
                a = slice(k * PACK // F_PIECES, (k + 1) * PACK // F_PIECES)
                f_hi.wait(e, nth * F_PIECES + k)
                ins = e.tensor_tensor(W[b][1][:, a], raw[:, a], W[b][0][:, a].bitcast(F32), ALU.subtract)
            w_lo.done(ins)

        @on("sp")
        def _(e):
            e.dma_start(cols[:, :], cols_in[:, :]).then_inc(s_cols, 16)
            x_tiles = x_in.rearrange("(t p) d -> p t d", p=P)
            for c in range(NCH):
                tiles = slice(c * TPC, (c + 1) * TPC)
                e.dma_start(x_sb[:, tiles, :], x_tiles[:, tiles, :]).then_inc(s_x[c], 16)
                if c == 0:
                    w_lo.wait(e, -1)
                    e.dma_start(raw[:, :], wpack[0, :, :]).then_inc(s_raw, 16)
            e.dma_start(ctxraw, ctxT.rearrange("(k p) n -> p k n", p=P)).then_inc(s_ctx, 16)
            e.dma_start(vraw, vb_in[0, :].partition_broadcast(P)).then_inc(s_vb, 16)
            e.dma_start(rows.rearrange("p r d -> p (r d)"), rows_in[:].partition_broadcast(P)).then_inc(s_rows, 16)
            with e.Fori(1, NPAIR) as n:
                w_lo.wait(e, n - 1)
                e.dma_start(raw[:, :], wpack[bass.ds(n, 1), :, :].rearrange("a p n -> (a p) n")).then_inc(s_raw, 16)
                v_diff.wait(e, n - 1)
                e.dma_start(vraw, vb_in[bass.ds(n, 1), :].rearrange("a d -> (a d)").partition_broadcast(P)).then_inc(s_vb, 16)
            with e.Fori(NPAIR, NPACK) as n:
                w_lo.wait(e, n - 1)
                e.dma_start(raw[:, :], wpack[bass.ds(n, 1), :, :].rearrange("a p n -> (a p) n")).then_inc(s_raw, 16)

        ctxraw = cut(arena[:, 0:KT * TOK], KT)
        c_hi, c_lo = (s.phase(KT) for s in stages("", 0, "c_hi c_lo"))

        def context_act(e):
            e.wait_ge(s_ctx, 16)
            for k in range(KT):
                c_hi.done(e.activation(cT[0][:, k, :], ctxraw[:, k, :], ACT.Copy))

        def context_dve(e):
            for k in range(KT):
                c_hi.wait(e, k)
                c_lo.done(e.tensor_tensor(cT[1][:, k, :], ctxraw[:, k, :], cT[0][:, k, :].bitcast(F32), ALU.subtract))

        N = dict(zip("st ag var sq r1 r2 r3 r4 x lo".split(),
                     stages("dve", 2, "n_st n_ag n_var n_sq n_r1 n_r2 n_r3 n_r4 n_x n_lo")))
        N |= zip(["pow"], stages("pool", 2, "n_pow"))
        N |= zip(["T"], stages("pe", 2, "n_T"))
        N |= zip(["ev", "hi"], stages("act", 2, "n_ev n_hi"))
        tn, xn = carve(norm_arena, [KT * CH, TPC * D])
        tn, xn = cut(tn, KT), cut(xn, TPC)
        st6 = cut(small[:, 0:TPC * 6], TPC)
        mv = cut(small[:, 32:32 + TPC * 2], TPC)
        vare, r0, ra, rb, rc, rstd, minus_half = (small[:, 40 + 4 * i:44 + 4 * i] for i in range(7))
        (s_small,) = (s.phase(1) for s in stages("", 0, "s_small"))

        (x_plus,) = stages("pool", 2, "x_plus")

        class Norm:

            def __init__(self, kind, eps, affine, times=1, row=None):
                self.kind, self.eps, self.affine = kind, float(eps), affine
                names = "x T ev hi lo".split()
                if kind != "none":
                    names += "st ag var pow r1 r2 r3 r4".split()
                if kind == "rms":
                    names.append("sq")
                self.s = {k: N[k].phase(times * NCH * (KT if k in ("ev", "hi", "lo") else 1)) for k in names}
                self.row = row
                self.x_plus = x_plus.phase(times * NCH) if row is not None or times > 1 else None

            def split(self, e, c, l=0):
                self.s["lo"].wait(e, l * (NCH * KT) + c * KT + (KT - 1))

            def dve(self, e, c, l=0):
                s, kind, g = self.s, self.kind, l * NCH + c
                if kind != "none":
                    s["x"].wait(e, g - 1)
                    settled(e)
                    for j in range(TPC):
                        ins = e.bn_stats(st6[:, j, :], x_sb[:, bass.ds(c * TPC + j, 1), :].rearrange("p a d -> p (a d)"))
                    s["st"].done(ins)
                    s["st"].wait(e, g)
                    settled(e)
                    for j in range(TPC):
                        ins = e.bn_aggr(mv[:, j, :], st6[:, j, :])
                    s["ag"].done(ins)
                    s["ag"].wait(e, g)
                    if kind == "rms":
                        s["sq"].done(e.tensor_tensor(ra, mv[:, :, 0], mv[:, :, 0], ALU.mult))
                        s["sq"].wait(e, g)
                        s["var"].done(e.scalar_tensor_tensor(vare, ra, self.eps, mv[:, :, 1], ALU.add, ALU.add))
                    else:
                        s["var"].done(e.tensor_scalar(vare, mv[:, :, 1], self.eps, None, ALU.add))
                    s["var"].wait(e, g)
                    s["pow"].wait(e, g)
                    s["r1"].done(e.tensor_tensor(ra, r0, r0, ALU.mult))
                    s["r1"].wait(e, g)
                    s["r2"].done(e.tensor_tensor(rb, ra, vare, ALU.mult))
                    s["r2"].wait(e, g)
                    s["r3"].done(e.tensor_scalar(rc, rb, -0.5, 1.5, ALU.mult, ALU.add))
                    s["r3"].wait(e, g)
                    s["r4"].done(e.tensor_tensor(rstd, r0, rc, ALU.mult))
                    s["r4"].wait(e, g)
                s["T"].wait(e, g - 1)
                settled(e)
                for j in range(TPC):
                    xt = x_sb[:, bass.ds(c * TPC + j, 1), :].rearrange("p a d -> p (a d)")
                    if kind == "layer":
                        ins = e.tensor_scalar(xn[:, j, :], xt, mv[:, j, 0:1], rstd[:, j:j + 1], ALU.subtract, ALU.mult)
                    elif kind == "rms":
                        ins = e.tensor_scalar(xn[:, j, :], xt, rstd[:, j:j + 1], None, ALU.mult)
                    else:
                        ins = e.tensor_copy(xn[:, j, :], xt)
                s["x"].done(ins)

            def dve_lo(self, e, c, l=0):
                for k in range(KT):
                    self.s["hi"].wait(e, (l * NCH + c) * KT + k)
                    self.s["lo"].done(e.tensor_tensor(hT[1][:, k, bass.ds(c * CH, CH)], tn[:, k, :],
                                                      hT[0][:, k, bass.ds(c * CH, CH)].bitcast(F32), ALU.subtract))

            def pool(self, e, c, row=None, l=0):
                g = l * NCH + c
                if self.kind != "none":
                    self.s["var"].wait(e, g)
                    self.s["pow"].done(e.tensor_tensor(r0, vare, minus_half, ALU.pow))
                if row is not None:
                    self.s["x"].wait(e, g)
                    settled(e)
                    xs = x_sb[:, bass.ds(c * TPC, TPC), :]
                    self.x_plus.done(e.tensor_tensor(xs, xs, each(row, TPC), ALU.add))

            def pe(self, e, c, banks, l=0):
                g = l * NCH + c
                self.s["x"].wait(e, g)
                self.s["ev"].wait(e, g * KT - 1)
                for k in range(KT):
                    for j in range(TPC):
                        ins = e.transpose(ps[:, banks[k], j * P:(j + 1) * P], xn[:, j, k * P:(k + 1) * P], ident)
                self.s["T"].done(ins)

            def act(self, e, c, banks, l=0):
                s, g = self.s, l * NCH + c
                s["T"].wait(e, g)
                s["lo"].wait(e, g * KT - 1)
                settled(e)
                for k in range(KT):
                    s["ev"].done(e.activation(tn[:, k, :], ps[:, banks[k], :], ACT.Identity,
                                              bias=self.affine(l, KT + k), scale=self.affine(l, k)))
                for k in range(KT):
                    s["ev"].wait(e, g * KT + k)
                    s["hi"].done(e.activation(hT[0][:, k, bass.ds(c * CH, CH)], tn[:, k, :], ACT.Copy))

        def static_affine(name):
            return lambda l, j: col(name, j)

        got = carve(arena, [CH] * 2 + [BPC * KEYS0] * 2 + [TPC * D] * 2 + [TPC * KEYS0] * 2 + [TPC * P] * 2)
        qs, ks, vs, sm, pts = got[0:2], *([cut(g, k) for g in got[a:a + 2]] for a, k in ((2, BPC), (4, TPC), (6, TPC), (8, TPC)))
        oT = [[split_arena[:, (2 * b + i) * CH:(2 * b + i + 1) * CH] for i in range(2)] for b in range(4)]
        amax, asum, arec = ([small[:, 80 + 16 * i + 8 * b:84 + 16 * i + 8 * b] for b in range(2)] for i in range(3))
        A = {k: s.phase(2 * UNITS) for k, s in zip(
            "kb q k V qe ke ve S mx sub exp sum rec nrm T pt O oh ol wo acc".split(),
            stages("", 0, "a_kb a_q a_k a_V a_qe a_ke a_ve a_S a_mx a_sub a_exp a_sum a_rec a_nrm a_T a_pt a_O a_oh a_ol a_wo a_acc"))}
        (pt_zero,) = (s.phase(1) for s in stages("", 0, "pt_zero"))
        BQ, BK, BV, BS, BT, BO, BW = 0, 1, 2, (3, 4), 5, 6, 7
        norm0 = Norm("layer", 1e-5, lambda l, j: cols[:, bass.ds(l * 2 * KT + (COLS["ln1"][0] + j), 1)], times=3)
        NB0 = {c: BS if c == NCH - 1 else (BQ, BK) for c in range(NCH)}

        def head_col(u, what):
            return hbias[u // UPP % 2][:, 2 * what + u % 2:2 * what + u % 2 + 1]

        class Step:

            def __init__(self, t, i, l):
                self.t, self.i, self.l = t, i, l

            def live(self, d):
                return self.i is not None or 0 <= self.t + d < UNITS

            def wait(self, e, name, d=0):
                if self.i is None and self.t + d < 0:
                    return
                n = self.l * UNITS + (self.t + d)
                A[name].wait(e, n if self.i is None else self.i * (2 * UPP) + n)

            def wait_pack(self, e, w):
                n = self.l * NHP + w
                w_lo.wait(e, n if self.i is None else self.i * 2 + n)

        def pe_step(e, z):
            t = z.t
            if z.live(0):
                b = t % 2
                z.wait(e, "qe")
                z.wait(e, "ke")
                z.wait(e, "kb")
                z.wait(e, "sub", -2)
                if z.i is None and t == 0:
                    norm0.split(e, NCH - 1, z.l)
                for n in range(BPC):
                    h = n % 2 * SEQ
                    ins = e.matmul(ps[h:h + SEQ, BS[b], n // 2 * KEYS0:(n // 2 + 1) * KEYS0],
                                   qs[b][:, n * SEQ:(n + 1) * SEQ], ks[b][:, n, :], start=True, stop=True)
                A["S"].done(ins)
            if z.live(1):
                u = t + 1
                w, c, hd = u // UPP, u % UPP // 2, u % 2
                if u % UPP == 0:
                    z.wait_pack(e, w)
                if z.i is None and u in (0, 2, 4):
                    norm0.split(e, NCH - 1 if u == 4 else u // 2, z.l)
                if z.i is None and u == 0:
                    c_lo.wait(e, KT - 1)
                    norm0.s["ev"].wait(e, (z.l * NCH + (NCH - 1)) * KT - 1)
                for off, src, bank, name, read in ((0, hT, BQ, "q", "qe"), (2 * D, cT, BK, "k", "ke")):
                    z.wait(e, read)
                    for k in range(KT):
                        a = off + k * D + hd * DH0
                        ins = split3(e, ps[:, bank, :], [x[:, a:a + DH0] for x in W[w % 2]],
                                     [x[:, k, c * CH:(c + 1) * CH] for x in src], k == 0, k == KT - 1)
                    A[name].done(ins)
            if z.live(-1):
                b = (t - 1) % 2
                z.wait(e, "nrm", -1)
                z.wait(e, "pt", -2)
                settled(e)
                for n in range(TPC):
                    ins = e.transpose(ps[0:SEQ, BT, n * P:(n + 1) * P], sm[b][:, n, 0:SEQ], ident)
                A["T"].done(ins)
            if z.live(1):
                u = t + 1
                w, c, hf = u // UPP, u % UPP // 2, u % 2
                z.wait(e, "ve")
                for j in range(2):
                    a = (c * TPC + hf * 2 + j) * P
                    for k in range(KT):
                        ins = split3(e, ps[:, BV, j * D:(j + 1) * D], [x[:, k, a:a + P] for x in cT],
                                     [x[:, (4 + k) * D:(5 + k) * D] for x in W[w % 2]],
                                     j == 0 and k == 0, k == KT - 1)
                A["V"].done(ins)
            if z.live(-1):
                u = t - 1
                z.wait(e, "pt", -1)
                z.wait(e, "ve", -1 if u % 2 else 0)
                z.wait(e, "ol", -2)
                for n in range(TPC):
                    ins = e.matmul(ps[:, BO, n * P:(n + 1) * P], vs[u // 2 % 2][:, n, u % 2 * DH0:(u % 2 + 1) * DH0],
                                   pts[u % 2][:, n, :], start=True, stop=True)
                A["O"].done(ins)
            if z.live(-3):
                v = t - 3
                z.wait(e, "ol", -3 if v % 2 else -2)
                z.wait(e, "acc", -4)
                for j in range(2):
                    a = (v % 2 * 2 + j) * P
                    for hd in range(2):
                        ins = split3(e, ps[:, BW, j * D:(j + 1) * D], [x[:, a:a + P] for x in oT[(v // 2 * 2 + hd) % 4]],
                                     [x[:, (6 + hd) * D:(7 + hd) * D] for x in W[v // UPP % 2]],
                                     j == 0 and hd == 0, hd == 1)
                A["wo"].done(ins)
            if z.live(-4) and (t - 4) % UPP == UPP - 1:
                z.wait(e, "wo", -4)
                e.sem_inc(w_used.sem, 1)

        def act_step(e, z):
            t = z.t
            if z.live(0):
                z.wait(e, "sub")
                A["exp"].done(e.activation(sm[t % 2], sm[t % 2], ACT.Exp, scale=1.0 / math.sqrt(DH0)))
            if z.live(1):
                u = t + 1
                b = u % 2
                if u % UPP == 0:
                    z.wait_pack(e, u // UPP)
                z.wait(e, "S", -1)
                z.wait(e, "q", 1)
                A["qe"].done(e.activation(qs[b], ps[:, BQ, :], ACT.Identity, bias=head_col(u, 0)))
                z.wait(e, "k", 1)
                A["ke"].done(e.activation(ks[b][:, :, 0:SEQ], cut(ps[:, BK, :], BPC), ACT.Identity, bias=head_col(u, 1)))
            if z.live(-1):
                u = t - 1
                z.wait(e, "T", -1)
                z.wait(e, "O", -3)
                src = cut(ps[0:SEQ, BT, :], TPC)
                e.activation(pts[u % 2][0:SEQ, :, 0:SEQ], src[:, :, 0:SEQ], ACT.Copy)
                A["pt"].done(e.activation(pts[u % 2][SEQ:P, :, SEQ:P], src[:, :, SEQ:P], ACT.Copy))
                z.wait(e, "O", -1)
                z.wait(e, "wo", -5 if u % 2 else -4)
                A["oh"].done(e.activation(oT[u % 4][0], ps[:, BO, :], ACT.Identity, bias=head_col(u, 3)))

        def dve_step(e, z):
            t = z.t
            if z.live(1):
                u = t + 1
                if u % UPP == 0:
                    z.wait_pack(e, u // UPP)
                z.wait(e, "S", -1)
                A["kb"].done(e.tensor_copy(ks[u % 2][:, :, SEQ:KEYS0], each(head_col(u, 2), BPC)))
            if z.live(0):
                b = t % 2
                s3 = cut(ps[:, BS[b], 0:TPC * KEYS0], TPC)
                z.wait(e, "S")
                A["mx"].done(e.tensor_reduce(amax[b], s3, axis=AX.X, op=ALU.max))
                z.wait(e, "mx")
                z.wait(e, "T", -2)
                A["sub"].done(e.tensor_tensor(sm[b], s3, many(amax[b], KEYS0), ALU.subtract))
            if z.live(-4):
                v = t - 4
                z.wait(e, "wo", -4)
                if z.i is None and v == 0:
                    norm0.x_plus.wait(e, z.l * NCH + (NCH - 1))
                xs = x_sb[:, v % UPP * 2:v % UPP * 2 + 2, :]
                z.wait(e, "acc", -5)
                A["acc"].done(e.tensor_tensor(xs, cut(ps[:, BW, :], 2), xs, ALU.add))
            if z.live(0):
                b = t % 2
                z.wait(e, "exp")
                A["sum"].done(e.tensor_reduce(asum[b], sm[b], axis=AX.X, op=ALU.add))
                z.wait(e, "sum")
                A["rec"].done(e.reciprocal(arec[b], asum[b]))
                z.wait(e, "rec")
                A["nrm"].done(e.tensor_tensor(sm[b][:, :, 0:SEQ], sm[b][:, :, 0:SEQ], many(arec[b], SEQ), ALU.mult))
            if z.live(1):
                u = t + 1
                hf = u % 2
                z.wait(e, "V", 1)
                z.wait(e, "O", -2 - hf)
                A["ve"].done(e.tensor_tensor(vs[u // 2 % 2][:, 2 * hf:2 * hf + 2, :], cut(ps[:, BV, :], 2),
                                             each(vdiff[u // UPP % 2], 2), ALU.add))
            if z.live(-1):
                u = t - 1
                z.wait(e, "oh", -1)
                A["ol"].done(e.scalar_tensor_tensor(oT[u % 4][1], ps[:, BO, :], head_col(u, 3),
                                                    oT[u % 4][0].bitcast(F32), ALU.add, ALU.subtract))

        def run_units(e, step, l, tail=None):
            lead, turn, drain = 5, 2 * UPP, 4
            trips = (UNITS - 1 - lead) // turn
            for t in range(-1, lead):
                step(e, Step(t, None, l))
            with e.Fori(0, trips) as i:
                for t in range(lead, lead + turn):
                    step(e, Step(t, i, l))
            for t in range(lead + trips * turn, UNITS + drain):
                step(e, Step(t, None, l))
                tail(e, t - (UNITS - UPP))

        @on("dve")
        def _(e):
            s_small.done(e.memset(minus_half, -0.5))
            s_small.wait(e, 0)
            e.wait_ge(s_cols, 16)
            for c in range(NCH):
                e.wait_ge(s_x[c], 16)
                norm0.dve(e, c)
                norm0.dve_lo(e, c)
                if c == 0:
                    split_dve(e, 0, 0, 0, True)
            context_dve(e)
            c_lo.wait(e, KT - 1)
            e.memset(pts[0], 0.0)
            pt_zero.done(e.memset(pts[1], 0.0))
            with e.Fori(0, 2) as l:
                def tail(e, k):
                    c = (k - 5) // 2
                    if k >= 5 and k % 2:
                        A["acc"].wait(e, l * UNITS + (UNITS - UPP + 2 * c + 1))
                        norm0.dve(e, c, l + 1)
                    elif k >= 8:
                        norm0.dve_lo(e, c - 1, l + 1)

                run_units(e, dve_step, l, tail)
                norm0.dve_lo(e, NCH - 2, l + 1)
                norm0.dve_lo(e, NCH - 1, l + 1)
                split_dve(e, l * NHP + (NHP + 1), 1, l + 1, True)

        @on("act")
        def _(e):
            e.wait_ge(s_cols, 16)
            for c in range(NCH):
                norm0.act(e, c, NB0[c])
                if c == 0:
                    split_act(e, 0, 0, 0, True)
            context_act(e)
            pt_zero.wait(e, 0)
            with e.Fori(0, 2) as l:
                def tail(e, k):
                    if k >= 7 and k % 2:
                        norm0.act(e, (k - 7) // 2, NB0[0], l + 1)

                run_units(e, act_step, l, tail)
                norm0.act(e, NCH - 1, NB0[NCH - 1], l + 1)
                split_act(e, l * NHP + (NHP + 1), 1, l + 1, True)

        @on("pe")
        def _(e):
            e.wait_ge(s_cols, 16)
            for c in range(NCH):
                norm0.pe(e, c, NB0[c])
            with e.Fori(0, 2) as l:
                def tail(e, k):
                    if k >= 7 and k % 2:
                        norm0.pe(e, (k - 7) // 2, NB0[0], l + 1)

                run_units(e, pe_step, l, tail)
                norm0.pe(e, NCH - 1, NB0[NCH - 1], l + 1)

        @on("pool")
        def _(e):
            def out_row(l):
                return rows[:, bass.ds(l, 1), :].rearrange("p a d -> p (a d)")

            s_small.wait(e, 0)
            for c in range(NCH):
                norm0.pool(e, c)
            split_pool(e, 1, 1, 0, True)
            e.wait_ge(s_rows, 16)
            for c in range(NCH):
                norm0.s["x"].wait(e, c)
                xs = x_sb[:, c * TPC:(c + 1) * TPC, :]
                norm0.x_plus.done(e.tensor_tensor(xs, xs, each(row("bo1"), TPC), ALU.add))
            with e.Fori(0, 2) as l:
                with e.Fori(0, NHP // 2 - 1) as i:
                    for b in range(2):
                        split_pool(e, l * NHP + i * 2 + (2 + b), b, l * (NHP - 1) + i * 2 + (1 + b), True)
                split_pool(e, l * NHP + NHP, 0, l * (NHP - 1) + (NHP - 1), True)
                for c in range(NCH):
                    norm0.pool(e, c, out_row(l + 1), l + 1)

        FAST = iter(range(3, NPACK))
        POOLED = iter(range(2 * NHP - 1, NPACK))

        def by_chunks(chunk):
            def run(e):
                chunk(e, 0, True, False)
                with e.Fori(1, NCH - 1) as c:
                    chunk(e, c, False, False)
                chunk(e, NCH - 1, False, True)
            return run

        M = dict(zip("W1 W2".split(), stages("pe", 2, "m_W1 m_W2")))
        M |= zip("gel gh".split(), stages("act", 2, "m_gel m_gh"))
        M |= zip("gl res".split(), stages("dve", 2, "m_gl m_res"))
        gelu, resid = arena[:, 0:2 * CH], cut(arena[:, 2 * CH:2 * CH + TILES * D], TILES)
        gelu = cut(gelu, 2)
        gsp = [[split_arena[:, (2 * b + i) * CH:(2 * b + i + 1) * CH] for i in range(2)] for b in range(2)]

        (r_plus,) = stages("pool", 2, "r_plus")

        def mlp(which, func, norm, nxt, out_row, residual, before, seam):
            s = {k: v.phase(NCH * (1 if k == "res" else FT)) for k, v in M.items()}
            xr, x0 = (r_plus.phase(NCH), 0) if residual is not None else (norm.x_plus, 2 * NCH if which == 0 else 0)
            l = 2 if which == 0 else 0
            pack = (2 * NHP, 2 * NHP + 3, 2 * NHP + 6)[which]
            w1, w2 = [cut(w, KT) for w in W[pack % 2]], [cut(w, FT) for w in W[(pack + 1) % 2]]
            base = x_sb if residual is None else residual
            nth = None if seam is None else next(FAST)
            banks = (6, 7)

            def behind(c, first):
                if first:
                    return (None if which == 0 else norm), NCH - 1
                return nxt, c - 1

            @by_chunks
            def dve(e, c, first, last):
                for f in range(FT):
                    g = c * FT + f
                    s["gh"].wait(e, g)
                    s["W2"].wait(e, g - 2)
                    s["gl"].done(e.tensor_tensor(gsp[f % 2][1], gelu[:, f % 2, :], gsp[f % 2][0].bitcast(F32), ALU.subtract))
                    if f == 4:
                        n, m = behind(c, first)
                        if n is not None:
                            n.dve_lo(e, m)
                s["W2"].wait(e, c * FT + (FT - 1))
                xr.wait(e, c + x0)
                rt = base[:, bass.ds(c * TPC, TPC), :]
                s["res"].done(e.tensor_tensor(x_sb[:, bass.ds(c * TPC, TPC), :],
                                              ps[:, 2:4, :].rearrange("p b (t d) -> p (b t) d", d=D), rt, ALU.add))
                s["res"].wait(e, c)
                if nxt is not None:
                    nxt.dve(e, c)
                if last and seam is not None:
                    split_dve(e, seam, seam % 2, nth)

            @by_chunks
            def act(e, c, first, last):
                for f in range(FT):
                    g = c * FT + f
                    s["W1"].wait(e, g)
                    s["gl"].wait(e, g - 2)
                    s["gel"].done(e.activation(gelu[:, f % 2, :], ps[:, f % 2, :], func, bias=col(f"fb{which}", f)))
                    s["gel"].wait(e, g)
                    s["W2"].wait(e, g - 2)
                    s["gh"].done(e.activation(gsp[f % 2][0], gelu[:, f % 2, :], ACT.Copy))
                    if f == 3:
                        n, m = behind(c, first)
                        if n is not None:
                            n.act(e, m, banks)
                if last and seam is not None:
                    split_act(e, seam, seam % 2, nth, False)

            @by_chunks
            def pool(e, c, first, last):
                if residual is not None:
                    rt = base[:, bass.ds(c * TPC, TPC), :]
                    settled(e)
                    xr.done(e.tensor_tensor(rt, rt, each(row(out_row), TPC), ALU.add))
                if nxt is not None:
                    nxt.pool(e, c, nxt.row)

            def up(e, c, f):
                s["gel"].wait(e, c * FT + (f - 2))
                for k in range(KT):
                    ins = split3(e, ps[:, f % 2, :], [w[:, k, f * P:(f + 1) * P] for w in w1],
                                 [x[:, k, bass.ds(c * CH, CH)] for x in hT], k == 0, k == KT - 1)
                s["W1"].done(ins)

            @by_chunks
            def pe(e, c, first, last):
                if first:
                    before["pe"](e)
                    norm.split(e, 0, l)
                    w_lo.wait(e, pack)
                    up(e, 0, 0)
                for f in range(FT):
                    if f + 1 < FT:
                        up(e, c, f + 1)
                    elif not last:
                        norm.split(e, c + 1, l)
                        up(e, c + 1, 0)
                    if first and f == 0:
                        w_lo.wait(e, pack + 1)
                    s["gl"].wait(e, c * FT + f)
                    if f == 0:
                        s["res"].wait(e, c - 1)
                    for j in range(TPC):
                        ins = split3(e, ps[:, 2 + j // 2, j % 2 * D:(j % 2 + 1) * D],
                                     [g[:, j * P:(j + 1) * P] for g in gsp[f % 2]],
                                     [w[:, f, :] for w in w2], f == 0 and j % 2 == 0, f == FT - 1)
                    s["W2"].done(ins)
                    if f == 3:
                        n, m = behind(c, first)
                        if n is not None:
                            n.pe(e, m, banks)
                    if last and f == FT - 2:
                        s["W1"].wait(e, NCH * FT - 1)
                        e.sem_inc(w_used.sem, 1)

            todo["dve"].append(dve)
            todo["act"] += [before["act"], act]
            todo["pool"] += [before["pool"], pool]
            todo["pe"].append(pe)

            @on("pe")
            def _(e):
                s["W2"].wait(e, NCH * FT - 1)
                e.sem_inc(w_used.sem, 1)

            return s

        H = dict(zip("pj S T PV out".split(), stages("pe", 2, "h_pj h_S h_T h_PV h_out")))
        H |= zip("c ea exp pt ah".split(), stages("act", 2, "h_c h_ea h_exp h_pt h_ah"))
        H |= zip("cl ev m mx neg rec a1 a2 al res".split(),
                 stages("dve", 2, "h_cl h_ev h_m h_mx h_neg h_rec h_a1 h_a2 h_al h_res"))
        H |= zip(["nrm"], stages("pool", 2, "h_nrm"))
        (mask_ready,) = stages("", 0, "mask_ready")
        G = H1 // 2
        PW = 2 * DH1

        def narrow(layer, nk, norm, nxt, qb, kb, vb, out_row, mask, before):
            own = nk > SEQ
            nsrc = nk // SEQ
            pack = 2 * NHP + 2 + 3 * (layer - 1)
            wb = W[pack % 2]
            nth_pack, nth_pool = next(FAST), next(POOLED)
            scale = 1.0 / (DH1 if own else math.sqrt(DH1))
            NQK, NV = KT + KT * nsrc, BPC // 2
            NPJ = NQK + NV
            EARLY = NQK if own else NQK + 2
            bank_of = ([0, 1, 2, 3] * 2)[:EARLY] + ([0, 1, 2, 3] if own else [2, 3])
            OUT = (2, 3)
            banks = (4, 5)
            per = {"pj": NPJ, "ea": NQK, "ev": NV, "c": 1, "cl": 1, "ah": 1, "al": 1, "out": 2, "res": 2}
            s = {k: v.phase(NCH * per.get(k, BPC)) for k, v in H.items()}
            xr = r_plus.phase(NCH) if out_row else norm.x_plus
            mask_ok = mask_ready.phase(1)
            NT = 3
            vt = BPC if own else BPC // 2
            mraw, qz, v_sb, pt, aT, tmp, maskb, kT = carve(
                arena, [NT * G * P, KT * BPC * P, vt * D, G * P, KT * CH, KT * SEQ, NB * SEQ // 2, KT * BPC * nk])
            maskb = maskb.bitcast(BF16)
            tt = [cut(mraw[:, b * G * P:b * G * P + G * nk], G) for b in range(NT)]
            qz = qz.rearrange("p (k u h n) -> p k u h n", k=KT, u=BPC, h=2)
            kT = kT.rearrange("p (k u n) -> p k u n", k=KT, u=BPC)
            v_sb, pt, aT, tmp = cut(v_sb, vt), cut(pt, G), cut(aT, KT), cut(tmp, KT)
            mx, neg, sums, recs = ([small[:, 128 + 16 * i + 8 * b:136 + 16 * i + 8 * b] for b in range(2)] for i in range(4))
            qzb = cut(small[:, 72:72 + 2 * KT], 2)
            kv = [cut(split_arena[:, 2048 * i:2048 * i + KT * BPC * nk], KT) for i in range(2)]
            at = 2048 - KT * CH if not own else 0
            asp = [cut(split_arena[:, 2048 * i + at:2048 * i + at + KT * CH], KT) for i in range(2)]

            def kv_parts(i, c):
                for k in range(KT):
                    dst = cut(kv[i][:, k, :], BPC)
                    yield dst[:, :, 0:SEQ], cut(cT[i][:, k, bass.ds(c * CH, CH)], BPC)
                    if own:
                        yield dst[:, :, SEQ:nk], cut(hT[i][:, k, bass.ds(c * CH, CH)], BPC)

            def kv_free(e, c):
                s["pj"].wait(e, c * NPJ - 1)
                if own:
                    s["out"].wait(e, c * 2 - 1)
                norm.split(e, c)

            def kv_act(e, c):
                kv_free(e, c)
                settled(e)
                for dst, src in kv_parts(0, c):
                    ins = e.activation(dst, src.bitcast(F32), ACT.Copy)
                s["c"].done(ins)

            def kv_dve(e, c):
                kv_free(e, c)
                settled(e)
                for dst, src in kv_parts(1, c):
                    ins = e.tensor_copy(dst, src.bitcast(F32))
                s["cl"].done(ins)

            def behind(c, first):
                return (norm, NCH - 1) if first else (nxt, c - 1)

            def project(e, c, i):
                bank = ps[:, bank_of[i], :]
                if i < 4:
                    s["m"].wait(e, c * BPC - 1)
                    if i == 0:
                        norm.split(e, c)
                elif bank_of[i] in OUT:
                    s["ea"].wait(e, c * NQK + (NQK - 1))
                    s["res"].wait(e, c * 2 - (1 if bank_of[i] == OUT[1] else 2))
                elif i - 4 < NQK and i < EARLY:
                    s["ea"].wait(e, c * NQK + (i - 4))
                else:
                    s["ea"].wait(e, c * NQK + (NQK - 1))
                if i < NQK:
                    m, src = (i, 0) if i < KT else ((i - KT) // nsrc, (i - KT) % nsrc)
                    w0 = 0 if i < KT else 2 * D
                    rhs = hT if i < KT or src else cT
                    for k in range(KT):
                        ins = split3(e, bank, [w[:, w0 + k * D + m * P:w0 + k * D + (m + 1) * P] for w in wb],
                                     [x[:, k, bass.ds(c * CH, CH)] for x in rhs], k == 0, k == KT - 1)
                else:
                    j = i - NQK
                    if j == 0:
                        s["c"].wait(e, c)
                        s["cl"].wait(e, c)
                    for m in range(nsrc):
                        a = (nsrc * j + m) * P
                        for k in range(KT):
                            ins = split3(e, bank[:, m * D:(m + 1) * D], [x[:, k, a:a + P] for x in kv],
                                         [w[:, (4 + k) * D:(5 + k) * D] for w in wb], m == 0 and k == 0, k == KT - 1)
                s["pj"].done(ins)

            def output(e, c):
                s["al"].wait(e, c)
                s["ea"].wait(e, c * NQK + (NQK - 1))
                for i in range(2):
                    for j in range(2):
                        a = (2 * i + j) * P
                        for k in range(KT):
                            ins = split3(e, ps[:, OUT[i], j * D:(j + 1) * D], [x[:, k, a:a + P] for x in asp],
                                         [w[:, (6 + k) * D:(7 + k) * D] for w in wb], j == 0 and k == 0, k == KT - 1)
                    s["out"].done(ins)

            @by_chunks
            def pe(e, c, first, last):
                if first:
                    before["pe"](e)
                    w_lo.wait(e, pack)
                    for i in range(4):
                        project(e, c, i)
                for i in range(4, EARLY):
                    project(e, c, i)
                if not first:
                    s["ea"].wait(e, c * NQK + 3)
                    output(e, c - 1)
                for i in range(EARLY, NPJ):
                    project(e, c, i)
                s["ea"].wait(e, c * NQK + (NQK - 1))
                s["ev"].wait(e, c * NV + (NV - 1))
                if first:
                    norm.s["ev"].wait(e, (NCH - 1) * KT - 1)
                for u in range(BPC + 2):
                    g = c * BPC + u
                    h, b = g - 2, u % 2
                    if u >= 2:
                        s["nrm"].wait(e, h)
                        s["pt"].wait(e, h - 1)
                        if u == 5:
                            n, m = behind(c, first)
                            n.s["ev"].wait(e, m * KT + (KT - 1))
                        settled(e)
                        for n in range(G):
                            ins = e.transpose(ps[0:nk, banks[n // 4], n % 4 * P:(n % 4 + 1) * P], tt[(u - 2) % NT][:, n, :], ident)
                        s["T"].done(ins)
                    if u < BPC:
                        s["m"].wait(e, g - 1)
                        for k in range(KT):
                            for j in range(G // KT):
                                r = j * PW
                                ins = e.matmul(ps[:, j, k * nk:(k + 1) * nk],
                                               qz[r:r + PW, k, u, :, :].rearrange("p h n -> p (h n)"),
                                               kT[r:r + PW, k, u, :], start=True, stop=True)
                        s["S"].done(ins)
                    elif not last:
                        for i in range(2):
                            project(e, c + 1, 2 * (u - BPC) + i)
                    if u >= 2:
                        s["pt"].wait(e, h)
                        s["a2"].wait(e, h - 2)
                        at = 0 if own else b * SEQ
                        settled(e)
                        for n in range(G):
                            j, k = n // KT, n % KT
                            v0 = k * P + j * PW
                            ins = e.matmul(ps[j * PW:(j + 1) * PW, 6 + b, k * P:(k + 1) * P],
                                           v_sb[at:at + nk, (u - 2) // (1 if own else 2), v0:v0 + PW],
                                           pt[at:at + nk, n, :], start=True, stop=True)
                        s["PV"].done(ins)
                    if u == 4:
                        n, m = behind(c, first)
                        s["pt"].wait(e, h)
                        n.pe(e, m, banks)
                if last:
                    output(e, c)
                    s["out"].wait(e, 2 * NCH - 1)
                    e.sem_inc(w_used.sem, 1)

            def evacuate(e, c, i):
                bank = ps[:, bank_of[i], :]
                s["pj"].wait(e, c * NPJ + i)
                if i < KT:
                    for h, part in enumerate(("even", "odd")):
                        ins = e.activation(qz[:, i, :, h, :], cut(bank, BPC), ACT.Identity,
                                           bias=qzb[:, h, i:i + 1], scale=col(part))
                else:
                    m, src = (i - KT) // nsrc, (i - KT) % nsrc
                    ins = e.activation(kT[:, m, :, src * SEQ:(src + 1) * SEQ], cut(bank, BPC), ACT.Identity, bias=col(kb, m))
                s["ea"].done(ins)

            @by_chunks
            def act(e, c, first, last):
                if first:
                    before["act"](e)
                    raw_mask = mraw[:, 0:NB * SEQ].bitcast(I32) if own else mraw.bitcast(U8)[:, 0:NB * SEQ]
                    e.dma_start(raw_mask, mask.rearrange("b s -> (b s)").partition_broadcast(P)).then_inc(s_mask, 16)
                    mask_ok.wait(e, 0)
                    kv_act(e, c)
                    for i in range(4):
                        evacuate(e, c, i)
                else:
                    s["a2"].wait(e, c * BPC - 1)
                    s["pj"].wait(e, (c - 1) * NPJ + (NPJ - 1))
                    s["out"].wait(e, (c - 1) * 2 - 1)
                    s["ah"].done(e.activation(asp[0], aT, ACT.Copy))
                for i in range(4, NQK):
                    evacuate(e, c, i)
                if own and not first:
                    kv_act(e, c)
                for u in range(BPC + 2):
                    g = c * BPC + u
                    if u >= 2:
                        h, b = g - 2, u % 2
                        s["T"].wait(e, h)
                        s["PV"].wait(e, h - 1)
                        at = 0 if own else b * SEQ
                        src = ps[0:nk, banks[0]:banks[1] + 1, :].rearrange("p b (t n) -> p (b t) n", n=P)
                        s["pt"].done(e.activation(pt[at:at + nk, :, :], src, ACT.Copy))
                    if u == 4:
                        n, m = behind(c, first)
                        n.act(e, m, banks)
                    if u < BPC:
                        s["neg"].wait(e, g)
                        s["rec"].wait(e, g - 2)
                        for n in range(G):
                            t = tt[u % NT][:, n, :]
                            ins = e.activation(t, t, ACT.Exp, scale=scale, bias=neg[u % 2][:, n:n + 1],
                                               accum_out=sums[u % 2][:, n:n + 1])
                        s["exp"].done(ins)
                    elif not last:
                        if u == BPC and not own:
                            kv_act(e, c + 1)
                        for i in range(2):
                            evacuate(e, c + 1, 2 * (u - BPC) + i)
                if last:
                    s["a2"].wait(e, (c + 1) * BPC - 1)
                    s["pj"].wait(e, c * NPJ + (NPJ - 1))
                    s["out"].wait(e, c * 2 - 1)
                    s["ah"].done(e.activation(asp[0], aT, ACT.Copy))
                    if pack + 2 < NPACK:
                        split_act(e, pack + 2, pack % 2, nth_pack, False)

            def split_output(e, c):
                s["ah"].wait(e, c)
                s["al"].done(e.tensor_tensor(asp[1], aT, asp[0].bitcast(F32), ALU.subtract))

            def residual(e, c):
                xr.wait(e, c)
                for i in range(2):
                    s["out"].wait(e, c * 2 + i)
                    xs = x_sb[:, bass.ds(c * TPC + 2 * i, 2), :]
                    s["res"].done(e.tensor_tensor(xs, cut(ps[:, OUT[i], :], 2), xs, ALU.add))

            @by_chunks
            def dve(e, c, first, last):
                if first:
                    for h, part in enumerate(("even", "odd")):
                        e.tensor_scalar(qzb[:, h, :], col(qb, 0, KT), col(part), None, ALU.mult)
                    e.wait_ge(s_mask, 16 * layer)
                    src = mraw[:, 0:NB * SEQ].bitcast(I32) if own else mraw.bitcast(U8)[:, 0:NB * SEQ]
                    mask_ok.done(e.tensor_scalar(maskb, src, 0.0, NEG, ALU.is_equal, ALU.mult))
                    kv_dve(e, c)
                else:
                    split_output(e, c - 1)
                    if own:
                        kv_dve(e, c)
                    residual(e, c - 1)
                for i in range(NV):
                    j = NQK + i
                    s["pj"].wait(e, c * NPJ + j)
                    s["PV"].wait(e, c * BPC - 1)
                    bank = ps[:, bank_of[j], :]
                    if own:
                        ins = e.tensor_tensor(v_sb[:, 2 * i:2 * i + 2, :], cut(bank, 2), each(row(vb), 2), ALU.add)
                    else:
                        ins = e.tensor_tensor(v_sb[:, i, :], bank[:, 0:D], row(vb), ALU.add)
                    s["ev"].done(ins)
                for u in range(BPC + 3):
                    g = c * BPC + u
                    if u < BPC:
                        b = u % 2
                        t = tt[u % NT]
                        sps = ps[:, 0:G // KT, 0:KT * nk].rearrange("p b (t n) -> p b t n", n=nk)
                        t4 = t.rearrange("p (b t) n -> p b t n", t=KT)
                        mk = each(maskb[:, bass.ds(g * SEQ, SEQ)], G).rearrange("p (b t) n -> p b t n", t=KT)
                        s["S"].wait(e, g)
                        s["T"].wait(e, g - NT)
                        if first and u == 0:
                            mask_ok.wait(e, 0)
                        ins = e.tensor_tensor(t4[:, :, :, 0:SEQ], sps[:, :, :, 0:SEQ], mk, ALU.add)
                        if own:
                            ins = e.tensor_copy(t4[:, :, :, SEQ:nk], sps[:, :, :, SEQ:nk])
                        s["m"].done(ins)
                        s["m"].wait(e, g)
                        s["mx"].done(e.tensor_reduce(mx[b], t, axis=AX.X, op=ALU.max))
                        s["mx"].wait(e, g)
                        s["exp"].wait(e, g - 2)
                        s["neg"].done(e.tensor_scalar(neg[b], mx[b], -scale, None, ALU.mult))
                    if 1 <= u <= BPC:
                        s["exp"].wait(e, g - 1)
                        s["nrm"].wait(e, g - 3)
                        s["rec"].done(e.reciprocal(recs[(u - 1) % 2], sums[(u - 1) % 2]))
                    if u >= 3:
                        h = g - 3
                        s["PV"].wait(e, h)
                        xv = cut(ps[:, 6 + (u - 3) % 2, 0:KT * P], KT)
                        s["a2"].wait(e, h - 1)
                        s["a1"].done(e.tensor_scalar(tmp, xv[:, :, SEQ:P], col("odd"), None, ALU.mult))
                        s["a1"].wait(e, h)
                        if u == 3:
                            s["al"].wait(e, c - 1)
                        s["a2"].done(e.scalar_tensor_tensor(aT[:, :, (u - 3) * SEQ:(u - 2) * SEQ], xv[:, :, 0:SEQ],
                                                            col("even"), tmp, ALU.mult, ALU.add))
                    if u == 1 and not first:
                        nxt.dve(e, c - 1)
                    if u == 5:
                        n, m = behind(c, first)
                        n.dve_lo(e, m)
                    if u == BPC and not own and not last:
                        kv_dve(e, c + 1)
                if last:
                    split_output(e, c)
                    residual(e, c)
                    s["res"].wait(e, NCH * 2 - 1)
                    nxt.dve(e, c)
                    if pack + 2 < NPACK:
                        split_dve(e, pack + 2, pack % 2, nth_pack)

            @by_chunks
            def pool(e, c, first, last):
                if first:
                    before["pool"](e)
                    if out_row:
                        for j in range(NCH):
                            norm.s["x"].wait(e, j)
                            xs = x_sb[:, j * TPC:(j + 1) * TPC, :]
                            xr.done(e.tensor_tensor(xs, xs, each(row(out_row), TPC), ALU.add))
                    split_pool(e, pack + 1, (pack + 1) % 2, nth_pool, False)
                for u in range(1, BPC + 1):
                    h = c * BPC + (u - 1)
                    s["rec"].wait(e, h)
                    t = tt[(u - 1) % NT]
                    s["nrm"].done(e.tensor_tensor(t, t, many(recs[(u - 1) % 2], nk), ALU.mult))
                    if u == 1 and not first:
                        nxt.pool(e, c - 1, nxt.row)
                if last:
                    nxt.pool(e, c, nxt.row)

            for name, part in (("pe", pe), ("act", act), ("dve", dve), ("pool", pool)):
                todo[name].append(part)
            return s


        def nothing(e):
            return None

        def after(steps, n):
            return lambda e: steps.wait(e, n)

        def last_of(steps, n=NCH - 1):
            return {e: after(steps, n) for e in ("pe", "act")} | {"pool": nothing}

        norm1 = Norm("none", 0.0, static_affine("one"))
        mlp0 = mlp(0, ACT.Gelu, norm0, norm1, "b_fc2", None,
                   {"pe": after(norm0.s["ev"], (3 * NCH - 1) * KT - 1), "act": nothing, "pool": nothing}, 2 * NHP + 2)

        def spill_tokens(e):
            mlp0["res"].wait(e, NCH - 1)
            e.dma_start(spill.rearrange("(t p) d -> p t d", p=P), x_sb).then_inc(s_spill, 16)

        rms1 = Norm("rms", 1e-6, static_affine("rms"))
        narrow1 = narrow(1, 2 * SEQ, norm1, rms1, "l1q", "l1k", "l1v", "out_b", mask1,
                         last_of(mlp0["res"]) | {"act": spill_tokens, "pool": lambda e: e.wait_ge(s_spill, 16)})

        def fetch_tokens(e):
            narrow1["res"].wait(e, 2 * NCH - 1)
            e.dma_start(resid, spill.rearrange("(t p) d -> p t d", p=P)).then_inc(s_back, 16)

        norm2 = Norm("layer", 1e-5, static_affine("l2n"), row=row("cproj_b"))
        mlp1 = mlp(1, ACT.Gelu_apprx_tanh, rms1, norm2, "mlp_b2", resid,
                   last_of(narrow1["res"], 2 * NCH - 1) | {"act": fetch_tokens, "pool": lambda e: e.wait_ge(s_back, 16)},
                   2 * NHP + 5)
        norm2m = Norm("layer", 1e-5, static_affine("l2m"), row=row("proj_b"))
        narrow2 = narrow(2, SEQ, norm2, norm2m, "l2q", "l2k", "l2v", None, mask2, last_of(mlp1["res"]))
        mlp2 = mlp(2, ACT.Gelu_apprx_tanh, norm2m, None, None, None, last_of(narrow2["res"], 2 * NCH - 1), None)

        Z = {k: v.phase(TILES) for k, v in zip(
            "F pj T Y wy".split(), stages("pe", 2, "z_F z_pj z_T z_Y z_wy"))}
        Z |= {k: v.phase(TILES) for k, v in zip("exp pe pt ye".split(), stages("act", 2, "z_exp z_pe z_pt z_ye"))}
        Z |= {k: v.phase(TILES) for k, v in zip("mx sub sum rec ge we st".split(),
                                                 stages("dve", 2, "z_mx z_sub z_sum z_rec z_ge z_we z_st"))}
        Z |= {k: v.phase(TILES) for k, v in zip("xc nrm".split(), stages("pool", 2, "z_xc z_nrm"))}
        (z_c,) = (s.phase(16) for s in stages("", 0, "z_c"))
        (z_o,) = (s.phase(NCH) for s in stages("", 0, "z_o"))
        (z_p,) = (s.phase(1) for s in stages("", 0, "z_p"))
        s_ct = [semaphore(f"s_ct{b}") for b in range(2)]
        got = carve(arena, [D] * 8 + [2 * 2 * CI] * 2 + [4 * D] * 2 + [4 * D] + [D] * 2 + [TILES * D])
        xc, cx, th, ph = got[0:2], got[2:4], got[4:6], got[6:8]
        gx = [cut(g, 2) for g in got[8:10]]
        ff = [cut(g, 4) for g in got[10:12]]
        fT, yT, wy = got[12], got[13:15], cut(got[15], TILES)
        bst = cut(norm_arena[:, 0:2 * TILES * 6], 2 * TILES)
        zmx, zsum, zrec = ([small[:, 192 + 8 * i + 4 * b:196 + 8 * i + 4 * b] for b in range(2)] for i in range(3))
        zs = [small[:, 216 + i:217 + i] for i in range(12)]

        class Tile:
            def __init__(self, t, i):
                self.t, self.i = t, i

            def live(self, d):
                return self.i is not None or 0 <= self.t + d < TILES

            def n(self, d=0):
                return self.t + d if self.i is None else self.i * 2 + (self.t + d)

            def wait(self, e, name, d=0):
                Z[name].wait(e, self.n(d))

        def z_pe(e, z):
            t = z.t
            if z.live(0):
                b = t % 2
                z.wait(e, "pe")
                z.wait(e, "sub", -1)
                for q in range(4):
                    r = q // 2 * CI
                    ins = e.matmul(ps[:, 2 + q // 2, q % 2 * D:(q % 2 + 1) * D], ph[b][r:r + CI, q % 2 * P:(q % 2 + 1) * P],
                                   th[b][r:r + CI, :], start=True, stop=True)
                Z["F"].done(ins)
            if z.live(1):
                b = (t + 1) % 2
                z.wait(e, "xc", 1)
                e.wait_ge(s_ct[b], 16 * ((t + 1) // 2 + 1) if z.i is None else z.i * 16 + 16 * ((t + 1) // 2 + 1))
                z.wait(e, "pe")
                z.wait(e, "ge")
                e.matmul(ps[0:2 * CI, 0, 0:D], col("wth", 0, 2 * CI), xc[b], start=True, stop=True)
                e.matmul(ps[0:2 * CI, 0, D:2 * D], col("wph", 0, 2 * CI), cx[b], start=True, stop=True)
                for q in range(2):
                    ins = e.matmul(ps[:, 1, q * 2 * CI:(q + 1) * 2 * CI], xc[b][:, q * P:(q + 1) * P],
                                   col("wg", 0, 2 * CI), start=True, stop=True)
                Z["pj"].done(ins)
            if z.live(-1):
                b = (t - 1) % 2
                z.wait(e, "nrm", -1)
                z.wait(e, "pt", -2)
                for a in range(2):
                    for jh in range(2):
                        for ih in range(2):
                            at = (2 * jh + ih) * P
                            ins = e.transpose(ps[:, 4 + a, at:at + P], ff[b][:, 2 * a + ih, jh * P:(jh + 1) * P], ident)
                Z["T"].done(ins)
                z.wait(e, "pt", -1)
                z.wait(e, "ye", -2)
                for a in range(2):
                    for jh in range(2):
                        ins = e.matmul(ps[a * CI:(a + 1) * CI, 6, 0:D], gx[b][:, jh, a * CI:(a + 1) * CI],
                                       fT[:, (2 * a + jh) * D:(2 * a + jh + 1) * D], start=jh == 0, stop=jh == 1)
                Z["Y"].done(ins)
                z.wait(e, "ye", -1)
                z.wait(e, "we", -2)
                Z["wy"].done(e.matmul(ps[:, 7, 0:D], col("wz", 0, P)[0:2 * CI, :], yT[b][0:2 * CI, :], start=True, stop=True))

        def z_act(e, z):
            t = z.t
            if z.live(0):
                z.wait(e, "sub")
                Z["exp"].done(e.activation(ff[t % 2], ff[t % 2], ACT.Exp))
            if z.live(1):
                b = (t + 1) % 2
                z.wait(e, "pj", 1)
                z.wait(e, "F", -1)
                e.activation(th[b][0:2 * CI, :], ps[0:2 * CI, 0, 0:D], ACT.Identity, bias=col("bth")[0:2 * CI, :])
                Z["pe"].done(e.activation(ph[b][0:2 * CI, :], ps[0:2 * CI, 0, D:2 * D], ACT.Identity, bias=col("bph")[0:2 * CI, :]))
            if z.live(-1):
                z.wait(e, "T", -1)
                z.wait(e, "Y", -2)
                Z["pt"].done(e.activation(cut(fT, 2), ps[:, 4:6, :], ACT.Copy))
                z.wait(e, "Y", -1)
                z.wait(e, "wy", -3)
                Z["ye"].done(e.activation(yT[(t - 1) % 2][0:2 * CI, :], ps[0:2 * CI, 6, 0:D], ACT.Copy))

        def z_dve(e, z):
            t = z.t
            if z.live(0):
                b = t % 2
                f4 = ps[:, 2:4, :].rearrange("p b (q n) -> p (b q) n", n=D)
                z.wait(e, "F")
                Z["mx"].done(e.tensor_reduce(zmx[b], f4, axis=AX.X, op=ALU.max))
                z.wait(e, "mx")
                z.wait(e, "T", -2)
                Z["sub"].done(e.tensor_tensor(ff[b], f4, many(zmx[b], D), ALU.subtract))
            if z.live(1):
                b = (t + 1) % 2
                z.wait(e, "pj", 1)
                z.wait(e, "Y", -1)
                Z["ge"].done(e.tensor_tensor(gx[b], cut(ps[:, 1, 0:4 * CI], 2), each(row("bg")[:, 0:2 * CI], 2), ALU.add))
            if z.live(0):
                b = t % 2
                z.wait(e, "exp")
                Z["sum"].done(e.tensor_reduce(zsum[b], ff[b], axis=AX.X, op=ALU.add))
                z.wait(e, "sum")
                z.wait(e, "nrm", -2)
                Z["rec"].done(e.reciprocal(zrec[b], zsum[b]))
            if z.live(-1):
                z.wait(e, "wy", -1)
                dst = wy[:, bass.ds(z.n(-1), 1), :].rearrange("p a d -> p (a d)")
                Z["we"].done(e.tensor_scalar(dst, ps[:, 7, 0:D], col("bz"), None, ALU.add))
                z.wait(e, "we", -1)
                Z["st"].done(e.bn_stats(bst[:, bass.ds(z.n(-1), 1), :].rearrange("p a d -> p (a d)"), dst))

        def z_pool(e, z):
            t = z.t
            if z.live(1):
                b = (t + 1) % 2
                z.wait(e, "pj", -1)
                settled(e)
                Z["xc"].done(e.tensor_copy(xc[b], x_sb[:, bass.ds(z.n(1), 1), :].rearrange("p a d -> p (a d)")))
            if z.live(0):
                b = t % 2
                z.wait(e, "rec")
                Z["nrm"].done(e.tensor_tensor(ff[b], ff[b], many(zrec[b], D), ALU.mult))

        def run_tiles(e, step):
            lead, drain = 3, 2
            trips = (TILES - 1 - lead) // 2
            for t in range(-1, lead):
                step(e, Tile(t, None))
            with e.Fori(0, trips) as i:
                for t in range(lead, lead + 2):
                    step(e, Tile(t, i))
            for t in range(lead + 2 * trips, TILES + drain - 1):
                step(e, Tile(t, None))

        @on("sp")
        def _(e):
            mlp2["res"].wait(e, NCH - 1)
            with e.Fori(0, TILES // 2) as i:
                for b in range(2):
                    Z["pj"].wait(e, i * 2 + (b - 2))
                    e.dma_start(cx[b], ctx_tok[bass.ds(i * 2 + b, 1), :, :].rearrange("a p d -> (a p) d")).then_inc(s_ct[b], 16)

        @on("pe")
        def _(e):
            run_tiles(e, z_pe)

        @on("act")
        def _(e):
            mlp2["res"].wait(e, NCH - 1)
            run_tiles(e, z_act)

        @on("pool")
        def _(e):
            mlp2["res"].wait(e, NCH - 1)
            run_tiles(e, z_pool)
            z_c.wait(e, 2)
            z_p.done(e.tensor_tensor(zs[3][0:SEQ, :], zs[2][0:SEQ, :], minus_half[0:SEQ, 0:1], ALU.pow))

        @on("dve")
        def _(e):
            run_tiles(e, z_dve)
            lower = slice(0, SEQ)
            count = [0]

            def then(ins):
                z_c.done(ins)
                z_c.wait(e, count[0])
                count[0] += 1

            Z["st"].wait(e, TILES - 1)
            then(e.tensor_copy(bst[lower, TILES:2 * TILES, :], bst[SEQ:P, 0:TILES, :]))
            then(e.bn_aggr(zs2, bst[lower, :, :].rearrange("p t s -> p (t s)")))
            then(e.tensor_scalar(zs[2][lower, :], zs2[:, 1:2], 1e-5, None, ALU.add))
            z_p.wait(e, 0)
            then(e.tensor_tensor(zs[4][lower, :], zs[3][lower, :], zs[3][lower, :], ALU.mult))
            then(e.tensor_tensor(zs[5][lower, :], zs[4][lower, :], zs[2][lower, :], ALU.mult))
            then(e.tensor_scalar(zs[6][lower, :], zs[5][lower, :], -0.5, 1.5, ALU.mult, ALU.add))
            then(e.tensor_tensor(zs[7][lower, :], zs[3][lower, :], zs[6][lower, :], ALU.mult))
            e.tensor_copy(zs[8][lower, :], zs2[:, 0:1])
            e.tensor_copy(zs[8][SEQ:P, :], zs2[:, 0:1])
            e.tensor_copy(zs[9][lower, :], zs[7][lower, :])
            then(e.tensor_copy(zs[9][SEQ:P, :], zs[7][lower, :]))
            then(e.tensor_tensor(zs[10], zs[9], col("gam"), ALU.mult))
            for c in range(NCH):
                w = wy[:, c * TPC:(c + 1) * TPC, :]
                then(e.tensor_scalar(w, w, zs[8], zs[10], ALU.subtract, ALU.mult))
                z_o.done(e.scalar_tensor_tensor(x_sb[:, c * TPC:(c + 1) * TPC, :], w, col("bet"),
                                                x_sb[:, c * TPC:(c + 1) * TPC, :], ALU.add, ALU.add))

        zs2 = small[0:SEQ, 232:234]

        @on("sp")
        def _(e):
            to = out.rearrange("(t p) d -> p t d", p=P)
            for c in range(NCH):
                z_o.wait(e, c)
                e.dma_start(to[:, c * TPC:(c + 1) * TPC, :], x_sb[:, c * TPC:(c + 1) * TPC, :]).then_inc(s_out, 16)
            e.wait_ge(s_out, 16 * NCH)
            e.wait_ge(s_spill, 16)

        block = ctx.enter_context(nc.Block())

        def program(name):
            def run(e):
                for s in owned.get(name, ()):
                    e.sem_inc(s.sem, s.ahead)
                for f in todo[name]:
                    f(e)
            return run

        block.sync(program("sp"))
        block.scalar(program("act"))
        block.vector(program("dve"))
        block.gpsimd(program("pool"))
        block.tensor(program("pe"))


def kernel(**inputs):
    import concourse.bacc as bacc
    from concourse.bass_utils import run_bass_kernel_spmd

    v = {k: np.asarray(a) for k, a in inputs.items()}
    f0, f1, f2, f3 = (f"L{i}_xattn_" for i in range(4))

    def rows_on_partitions(w):
        return w.reshape(-1, P, w.shape[1]).transpose(1, 0, 2).reshape(P, -1)

    packs, pairs = [], []
    zero8 = np.zeros((P, 8), np.float32)
    for a in (1, 2):
        g = {n: v[f"{f0}{n}{a}"] for n in ("wq", "wk", "wv", "wo", "bq", "bk", "bv", "bias_k", "bias_v")}
        for w in range(NHP):
            c = slice(w * 2 * DH0, (w + 1) * 2 * DH0)
            bias = [g[n].reshape(-1)[c].reshape(2, DH0).T for n in ("bq", "bk", "bias_k", "bias_v")]
            packs.append([rows_on_partitions(g["wq"][:, c]), rows_on_partitions(g["wk"][:, c]),
                          rows_on_partitions(g["wv"][:, c]), rows_on_partitions(g["wo"][c, :]), *bias])
            pairs.append([g["bv"][c], g["bias_v"].reshape(-1)[c]])
    kv = v[f1 + "kv_w"].reshape(D, D, 2)
    kvb = v[f1 + "kv_b"].reshape(D, 2)
    packs += [[rows_on_partitions(v[f0 + "w_fc1"]), zero8], [rows_on_partitions(v[f0 + "w_fc2"]), zero8],
              [*(rows_on_partitions(w) for w in (v[f1 + "q_w"], kv[:, :, 0], kv[:, :, 1], v[f1 + "out_w"])), zero8],
              [rows_on_partitions(v[f1 + "mlp_w1"]), zero8], [rows_on_partitions(v[f1 + "mlp_w2"]), zero8],
              [*(rows_on_partitions(v[f2 + n]) for n in ("q_w", "k_w", "v_w", "cproj_w")), zero8],
              [rows_on_partitions(v[f2 + "fc_w"]), zero8], [rows_on_partitions(v[f2 + "proj_w"]), zero8]]
    wpack = np.stack([np.concatenate(p, axis=1) for p in packs])
    pairs += [[np.zeros(2 * DH0, np.float32)] * 2] * 2
    vb = np.stack([np.concatenate(p) for p in pairs])

    consts = np.zeros((P, NCOL), np.float32)

    def put(name, *vectors):
        blocks = [a.reshape(-1, P).T if a.ndim == 1 else a for a in vectors]
        block = np.concatenate(blocks, axis=1)
        consts[:block.shape[0], COLS[name][0]:COLS[name][0] + block.shape[1]] = block

    one, nil = np.ones(D, np.float32), np.zeros(D, np.float32)
    put("ln1", v[f0 + "ln1_scale"], v[f0 + "ln1_offset"])
    put("ln2", v[f0 + "ln2_scale"], v[f0 + "ln2_offset"])
    put("lnm", v[f0 + "ln_mlp_scale"], v[f0 + "ln_mlp_offset"])
    put("l1q", v[f1 + "q_b"])
    put("l1k", kvb[:, 0])
    put("rms", v[f1 + "postnorm_w"], nil)
    put("l2n", v[f2 + "ln1_w"], v[f2 + "ln1_b"])
    put("l2q", v[f2 + "q_b"])
    put("l2k", v[f2 + "k_b"])
    put("l2m", v[f2 + "ln2_w"], v[f2 + "ln2_b"])
    put("fb0", v[f0 + "b_fc1"])
    put("fb1", v[f1 + "mlp_b1"])
    put("fb2", v[f2 + "fc_b"])
    put("one", one, nil)
    for name, w in (("bth", "btheta"), ("bph", "bphi"), ("bz", "bz"), ("gam", "gamma"), ("bet", "beta")):
        put(name, np.tile(v[f3 + w], 2)[:, None])
    p = np.arange(P)
    put("hmask", (p[:, None] // DH1 == np.arange(HPT)).astype(np.float32))
    put("even", (p // DH1 % 2 == 0).astype(np.float32)[:, None])
    put("odd", (p // DH1 % 2 == 1).astype(np.float32)[:, None])
    put("ident", np.eye(P, dtype=np.float32))

    def twice(w):
        z = np.zeros((2 * w.shape[0], 2 * w.shape[1]), np.float32)
        z[:w.shape[0], :w.shape[1]] = z[w.shape[0]:, w.shape[1]:] = w
        return z

    put("wth", twice(v[f3 + "Wtheta"].T))
    put("wph", twice(v[f3 + "Wphi"].T))
    put("wg", twice(v[f3 + "Wg"].T))
    put("wz", twice(v[f3 + "Wz"].T))

    bg = np.concatenate([v[f3 + "bg"], v[f3 + "bg"], np.zeros(D - 2 * CI, np.float32)])
    rows = np.concatenate([v[f0 + "bo1"], v[f0 + "bo2"], v[f0 + "b_fc2"], v[f1 + "out_b"], v[f1 + "mlp_b2"],
                           v[f2 + "cproj_b"], v[f2 + "proj_b"], kvb[:, 1], v[f2 + "v_b"], bg])
    ctx_tok = v["ctx_2048"].reshape(TILES, P, D)
    arrays = {
        "wpack": wpack, "ctxT": v["ctx_2048"].reshape(TOK, D).T, "ctx_tok": ctx_tok, "x_in": v["x"].reshape(TOK, D),
        "mask1": v["mask_BxS2_ik0"], "mask2": v["mask_BxS2_bf1"].view(np.uint8), "cols_in": consts,
        "rows_in": rows, "vb_in": vb,
    }
    arrays = {k: np.ascontiguousarray(a) for k, a in arrays.items()}
    nc = bacc.Bacc("TRN2", target_bir_lowering=False, num_devices=1)
    aps = {k: nc.dram_tensor(k, a.shape, mybir.dt.from_np(a.dtype), kind="ExternalInput").ap() for k, a in arrays.items()}
    out = nc.dram_tensor("out", (TOK, D), F32, kind="ExternalOutput").ap()
    spill = nc.dram_tensor("spill", (TOK, D), F32, kind="Internal").ap()
    build(nc, **aps, out=out, spill=spill)
    got = run_bass_kernel_spmd(nc, [arrays], core_ids=[0])
    return got.results[0]["out"].reshape(NB, SEQ, D)
```

```python
import math
from contextlib import ExitStack

import numpy as np

import concourse.bass as bass
from concourse import mybir
from concourse.alu_op_type import AluOpType as ALU

F32 = mybir.dt.float32
F32R = mybir.dt.float32r
I32 = mybir.dt.int32
U8 = mybir.dt.uint8
BF16 = mybir.dt.bfloat16
ACT = mybir.ActivationFunctionType
AX = mybir.AxisListType

P = 128
NB, SEQ, D = 32, 64, 256
TOK = NB * SEQ
TILES = TOK // P
KT = D // P
FF = 4 * D
FT = FF // P
CH = 512
NCH = TOK // CH
TPC = CH // P
BPC = CH // SEQ
H0, DH0 = 16, 128
H1, DH1 = 16, 16
HPT = P // DH1
NHP = H0 // 2
UPP = 2 * NCH
UNITS = NHP * UPP
KEYS0 = SEQ + 1
CI = 32
PACK = 2048
PCOLS = PACK + 8
NPACK = 2 * NHP + 8
NEG = -3.3895313892515355e38

COLS = {}


def _col(name, n):
    COLS[name] = (sum(k for _, k in COLS.values()), n)


for _name, _n in (("ln1", 4), ("ln2", 4), ("lnm", 4), ("l1q", 2), ("l1k", 2), ("rms", 4), ("l2n", 4),
                  ("l2q", 2), ("l2k", 2), ("l2m", 4), ("fb0", FT), ("fb1", FT), ("fb2", FT),
                  ("one", 4), ("bth", 1), ("bph", 1), ("bz", 1), ("gam", 1), ("bet", 1),
                  ("hmask", HPT), ("even", 1), ("odd", 1),
                  ("wth", 2 * CI), ("wph", 2 * CI), ("wg", 2 * CI), ("wz", P), ("ident", P)):
    _col(_name, _n)
NCOL = sum(k for _, k in COLS.values())
ARENA = 12432
PJB = (0, 1, 2, 3)
ROWS = ("bo1", "bo2", "b_fc2", "out_b", "mlp_b2", "cproj_b", "proj_b", "l1v", "l2v", "bg")



class Steps:

    def __init__(self, sem, base):
        self.sem, self.base = sem, base

    def done(self, ins):
        ins.then_inc(self.sem, 1)

    def wait(self, eng, n):
        eng.wait_ge(self.sem, n + (self.base + 1))


class Stage:

    def __init__(self, sem, ahead):
        self.sem, self.total, self.ahead = sem, ahead, ahead

    def phase(self, steps):
        got = Steps(self.sem, self.total)
        self.total += steps
        return got


def build(nc, wpack, ctxT, ctx_tok, x_in, mask1, mask2, cols_in, rows_in, vb_in, out, spill):
    ctx = ExitStack()
    with ctx:
        def sb(name, cols, dt=F32):
            return ctx.enter_context(nc.sbuf_tensor(name, [P, cols], dt))

        def semaphore(name):
            return ctx.enter_context(nc.semaphore(name))

        owned = {e: [] for e in ("pe", "act", "dve", "pool")}

        def stages(owner, ahead, names):
            got = []
            for name in names.split():
                s = Stage(semaphore(name), ahead)
                if ahead:
                    owned[owner].append(s)
                got.append(s)
            return got

        def cut(t, k):
            return t.rearrange("p (k n) -> p k n", k=k)

        def many(t, n):
            return t.rearrange("p (k a) -> p k a", a=1).to_broadcast([P, t.shape[1], n])

        def each(t, k):
            return t.rearrange("p (a n) -> p a n", a=1).to_broadcast([P, k, t.shape[1]])

        x_sb = cut(sb("x_sb", TILES * D)[:, :], TILES)
        cT = [cut(sb(f"cT{i}", KT * TOK, F32R)[:, :], KT) for i in range(2)]
        hT = [cut(sb(f"hT{i}", KT * TOK, F32R)[:, :], KT) for i in range(2)]
        W = [[sb(f"W{b}{i}", PACK, F32R)[:, :] for i in range(2)] for b in range(2)]
        raw = sb("raw", PCOLS)
        hbias = [sb(f"hbias{b}", 8)[:, :] for b in range(2)]
        cols = sb("cols", NCOL)
        rows = cut(sb("rows", len(ROWS) * D)[:, :], len(ROWS))
        split_arena = sb("split_arena", 4096, F32R)
        norm_arena = sb("norm_arena", KT * CH + TPC * D)
        arena = sb("arena", ARENA)
        small = sb("small", 256)
        ps = ctx.enter_context(nc.psum_tensor("ps", [P, 8, 512], F32))

        def carve(tensor, sizes):
            at, got = 0, []
            for n in sizes:
                got.append(tensor[:, at:at + n])
                at += n
            assert at <= tensor.shape[1], (at, tensor.shape)
            return got

        def col(name, j=0, n=1):
            a = COLS[name][0] + j
            return cols[:, a:a + n]

        def row(name):
            return rows[:, ROWS.index(name), :]

        ident = col("ident", 0, P)

        s_cols, s_rows, s_ctx, s_raw, s_vb, s_mask, s_spill, s_back, s_out = (
            semaphore("s_" + s) for s in "cols rows ctx raw vb mask spill back out".split())
        s_x = [semaphore(f"s_x{c}") for c in range(NCH)]

        todo = {e: [] for e in ("pe", "act", "dve", "pool", "sp")}

        def on(engine):
            def keep(f):
                todo[engine].append(f)
                return f
            return keep

        def settled(e):
            e.sem_inc(s_turn, 1)

        s_turn = semaphore("s_turn")

        def split3(e, dst, lhs, rhs, start, stop):
            for n, (a, b) in enumerate(((0, 0), (0, 1), (1, 0))):
                last = e.matmul(dst, lhs[a], rhs[b], start=start and n == 0, stop=stop and n == 2,
                                skip_group_check=True)
            return last

        (w_used,) = stages("pe", 2, "w_used")
        (w_lo,) = stages("pool", 2, "w_lo")
        (v_diff,) = stages("pool", 2, "v_diff")
        w_used, w_lo, v_diff = (s.phase(NPACK) for s in (w_used, w_lo, v_diff))
        NPAIR = 2 * NHP + 1

        F_PIECES = 4
        (p_hi,) = (s.phase(NPACK) for s in stages("", 0, "p_hi"))
        (f_hi,) = (s.phase(NPACK * F_PIECES) for s in stages("", 0, "f_hi"))
        vraw = arena[:, ARENA - 4 * D:ARENA - 2 * D]
        vdiff = [arena[:, ARENA - (2 - b) * D:ARENA - (1 - b) * D] for b in range(2)]

        def pair_bias(e, n, b):
            e.wait_ge(s_vb, n * 16 + 16)
            w_used.wait(e, n - 2)
            v_diff.done(e.tensor_tensor(vdiff[b], vraw[:, 0:D], vraw[:, D:2 * D], ALU.subtract))

        def split_pool(e, n, b, nth, pair):
            if pair:
                pair_bias(e, n, b)
            e.wait_ge(s_raw, n * 16 + 16)
            w_used.wait(e, n - 2)
            settled(e)
            if pair:
                e.tensor_copy(hbias[b], raw[:, PACK:PCOLS])
            p_hi.done(e.tensor_copy(W[b][0], raw[:, 0:PACK]))
            p_hi.wait(e, nth)
            w_lo.done(e.tensor_tensor(W[b][1], raw[:, 0:PACK], W[b][0].bitcast(F32), ALU.subtract))

        def split_act(e, n, b, nth, pair):
            e.wait_ge(s_raw, n * 16 + 16)
            w_used.wait(e, n - 2)
            if pair:
                e.activation(hbias[b], raw[:, PACK:PCOLS], ACT.Copy)
            for k in range(F_PIECES):
                a = slice(k * PACK // F_PIECES, (k + 1) * PACK // F_PIECES)
                f_hi.done(e.activation(W[b][0][:, a], raw[:, a], ACT.Copy))

        def split_dve(e, n, b, nth, pair=False):
            if pair:
                pair_bias(e, n, b)
            w_lo.wait(e, n - 1)
            for k in range(F_PIECES):
                a = slice(k * PACK // F_PIECES, (k + 1) * PACK // F_PIECES)
                f_hi.wait(e, nth * F_PIECES + k)
                ins = e.tensor_tensor(W[b][1][:, a], raw[:, a], W[b][0][:, a].bitcast(F32), ALU.subtract)
            w_lo.done(ins)

        @on("sp")
        def _(e):
            e.dma_start(cols[:, :], cols_in[:, :]).then_inc(s_cols, 16)
            x_tiles = x_in.rearrange("(t p) d -> p t d", p=P)
            for c in range(NCH):
                tiles = slice(c * TPC, (c + 1) * TPC)
                e.dma_start(x_sb[:, tiles, :], x_tiles[:, tiles, :]).then_inc(s_x[c], 16)
                if c == 0:
                    w_lo.wait(e, -1)
                    e.dma_start(raw[:, :], wpack[0, :, :]).then_inc(s_raw, 16)
                    e.dma_start(vraw, vb_in[0, :].partition_broadcast(P)).then_inc(s_vb, 16)
                    e.dma_start(ctxraw, ctxT.rearrange("(k p) n -> p k n", p=P)).then_inc(s_ctx, 16)
                    e.dma_start(rows.rearrange("p r d -> p (r d)"), rows_in[:].partition_broadcast(P)).then_inc(s_rows, 16)
            with e.Fori(1, NPAIR) as n:
                w_lo.wait(e, n - 1)
                e.dma_start(raw[:, :], wpack[bass.ds(n, 1), :, :].rearrange("a p n -> (a p) n")).then_inc(s_raw, 16)
                v_diff.wait(e, n - 1)
                e.dma_start(vraw, vb_in[bass.ds(n, 1), :].rearrange("a d -> (a d)").partition_broadcast(P)).then_inc(s_vb, 16)
            with e.Fori(NPAIR, NPACK) as n:
                w_lo.wait(e, n - 1)
                e.dma_start(raw[:, :], wpack[bass.ds(n, 1), :, :].rearrange("a p n -> (a p) n")).then_inc(s_raw, 16)

        ctxraw = cut(arena[:, 0:KT * TOK], KT)
        c_hi, c_lo = (s.phase(KT) for s in stages("", 0, "c_hi c_lo"))

        def context_act(e):
            e.wait_ge(s_ctx, 16)
            for k in range(KT):
                c_hi.done(e.activation(cT[0][:, k, :], ctxraw[:, k, :], ACT.Copy))

        def context_dve(e):
            for k in range(KT):
                c_hi.wait(e, k)
                c_lo.done(e.tensor_tensor(cT[1][:, k, :], ctxraw[:, k, :], cT[0][:, k, :].bitcast(F32), ALU.subtract))

        N = dict(zip("st ag var sq r1 r2 r3 r4 x lo".split(),
                     stages("dve", 2, "n_st n_ag n_var n_sq n_r1 n_r2 n_r3 n_r4 n_x n_lo")))
        N |= zip(["pow"], stages("pool", 2, "n_pow"))
        N |= zip(["T"], stages("pe", 2, "n_T"))
        N |= zip(["ev", "hi"], stages("act", 2, "n_ev n_hi"))
        tn, xn = carve(norm_arena, [KT * CH, TPC * D])
        tn, xn = cut(tn, KT), cut(xn, TPC)
        st6 = cut(small[:, 0:TPC * 6], TPC)
        mv = cut(small[:, 32:32 + TPC * 2], TPC)
        vare, r0, ra, rb, rc, rstd, minus_half = (small[:, 40 + 4 * i:44 + 4 * i] for i in range(7))
        (s_small,) = (s.phase(1) for s in stages("", 0, "s_small"))

        (x_plus,) = stages("pool", 2, "x_plus")

        class Norm:

            def __init__(self, kind, eps, affine, times=1, row=None):
                self.kind, self.eps, self.affine = kind, float(eps), affine
                names = "x T ev hi lo".split()
                if kind != "none":
                    names += "st ag var pow r1 r2 r3 r4".split()
                if kind == "rms":
                    names.append("sq")
                self.s = {k: N[k].phase(times * NCH * (KT if k in ("ev", "hi", "lo") else 1)) for k in names}
                self.row = row
                self.x_plus = x_plus.phase(times * NCH) if row is not None or times > 1 else None

            def split(self, e, c, l=0):
                self.s["lo"].wait(e, l * (NCH * KT) + c * KT + (KT - 1))

            def dve(self, e, c, l=0):
                self.dve_stats(e, c, l)
                self.dve_x(e, c, l)

            def dve_stats(self, e, c, l=0):
                s, kind, g = self.s, self.kind, l * NCH + c
                if kind != "none":
                    s["x"].wait(e, g - 1)
                    settled(e)
                    for j in range(TPC):
                        ins = e.bn_stats(st6[:, j, :], x_sb[:, bass.ds(c * TPC + j, 1), :].rearrange("p a d -> p (a d)"))
                    s["st"].done(ins)
                    s["st"].wait(e, g)
                    settled(e)
                    for j in range(TPC):
                        ins = e.bn_aggr(mv[:, j, :], st6[:, j, :])
                    s["ag"].done(ins)
                    s["ag"].wait(e, g)
                    if kind == "rms":
                        s["sq"].done(e.tensor_tensor(ra, mv[:, :, 0], mv[:, :, 0], ALU.mult))
                        s["sq"].wait(e, g)
                        s["var"].done(e.scalar_tensor_tensor(vare, ra, self.eps, mv[:, :, 1], ALU.add, ALU.add))
                    else:
                        s["var"].done(e.tensor_scalar(vare, mv[:, :, 1], self.eps, None, ALU.add))

            def dve_x(self, e, c, l=0):
                s, kind, g = self.s, self.kind, l * NCH + c
                if kind != "none":
                    s["var"].wait(e, g)
                    s["pow"].wait(e, g)
                    s["r1"].done(e.tensor_tensor(ra, r0, r0, ALU.mult))
                    s["r1"].wait(e, g)
                    s["r2"].done(e.tensor_tensor(rb, ra, vare, ALU.mult))
                    s["r2"].wait(e, g)
                    s["r3"].done(e.tensor_scalar(rc, rb, -0.5, 1.5, ALU.mult, ALU.add))
                    s["r3"].wait(e, g)
                    s["r4"].done(e.tensor_tensor(rstd, r0, rc, ALU.mult))
                    s["r4"].wait(e, g)
                s["T"].wait(e, g - 1)
                settled(e)
                for j in range(TPC):
                    xt = x_sb[:, bass.ds(c * TPC + j, 1), :].rearrange("p a d -> p (a d)")
                    if kind == "layer":
                        ins = e.tensor_scalar(xn[:, j, :], xt, mv[:, j, 0:1], rstd[:, j:j + 1], ALU.subtract, ALU.mult)
                    elif kind == "rms":
                        ins = e.tensor_scalar(xn[:, j, :], xt, rstd[:, j:j + 1], None, ALU.mult)
                    else:
                        ins = e.tensor_copy(xn[:, j, :], xt)
                s["x"].done(ins)

            def dve_lo(self, e, c, l=0):
                for k in range(KT):
                    self.s["hi"].wait(e, (l * NCH + c) * KT + k)
                    self.s["lo"].done(e.tensor_tensor(hT[1][:, k, bass.ds(c * CH, CH)], tn[:, k, :],
                                                      hT[0][:, k, bass.ds(c * CH, CH)].bitcast(F32), ALU.subtract))

            def pool(self, e, c, row=None, l=0):
                g = l * NCH + c
                if self.kind != "none":
                    self.s["var"].wait(e, g)
                    self.s["pow"].done(e.tensor_tensor(r0, vare, minus_half, ALU.pow))
                if row is not None:
                    self.s["x"].wait(e, g)
                    settled(e)
                    xs = x_sb[:, bass.ds(c * TPC, TPC), :]
                    self.x_plus.done(e.tensor_tensor(xs, xs, each(row, TPC), ALU.add))

            def pe(self, e, c, banks, l=0):
                g = l * NCH + c
                self.s["x"].wait(e, g)
                self.s["ev"].wait(e, g * KT - 1)
                for k in range(KT):
                    for j in range(TPC):
                        ins = e.transpose(ps[:, banks[k], j * P:(j + 1) * P], xn[:, j, k * P:(k + 1) * P], ident)
                self.s["T"].done(ins)

            def act(self, e, c, banks, l=0):
                for part in range(2 * KT):
                    self.act_part(e, c, banks, part, l)

            def act_part(self, e, c, banks, part, l=0):
                s, g, k = self.s, l * NCH + c, part % KT
                if part < KT:
                    s["T"].wait(e, g)
                    s["lo"].wait(e, g * KT - 1)
                    settled(e)
                    s["ev"].done(e.activation(tn[:, k, :], ps[:, banks[k], :], ACT.Identity,
                                              bias=self.affine(l, KT + k), scale=self.affine(l, k)))
                else:
                    s["ev"].wait(e, g * KT + k)
                    s["hi"].done(e.activation(hT[0][:, k, bass.ds(c * CH, CH)], tn[:, k, :], ACT.Copy))

        def static_affine(name):
            return lambda l, j: col(name, j)

        got = carve(arena, [CH] * 2 + [BPC * KEYS0] * 2 + [TPC * D] * 2 + [TPC * KEYS0] * 2 + [TPC * P] * 2)
        qs, ks, vs, sm, pts = got[0:2], *([cut(g, k) for g in got[a:a + 2]] for a, k in ((2, BPC), (4, TPC), (6, TPC), (8, TPC)))
        oT = [[split_arena[:, (2 * b + i) * CH:(2 * b + i + 1) * CH] for i in range(2)] for b in range(4)]
        amax, asum, arec = ([small[:, 80 + 16 * i + 8 * b:84 + 16 * i + 8 * b] for b in range(2)] for i in range(3))
        A = {k: s.phase(2 * UNITS) for k, s in zip(
            "kb q k V qe ke ve S mx sub exp sum rec nrm T pt O oh ol wo acc".split(),
            stages("", 0, "a_kb a_q a_k a_V a_qe a_ke a_ve a_S a_mx a_sub a_exp a_sum a_rec a_nrm a_T a_pt a_O a_oh a_ol a_wo a_acc"))}
        (pt_zero,) = (s.phase(1) for s in stages("", 0, "pt_zero"))
        BQ, BK, BV, BS, BT, BO, BW = 0, 1, 2, (3, 4), 5, 6, 7
        norm0 = Norm("layer", 1e-5, lambda l, j: cols[:, bass.ds(l * 2 * KT + (COLS["ln1"][0] + j), 1)], times=3)
        NB0, NB0_HEAD = (BQ, BK), (BT, BW)
        NORM_STEP = {0: 1, 1: 2, 3: 3}

        def head_col(u, what):
            return hbias[u // UPP % 2][:, 2 * what + u % 2:2 * what + u % 2 + 1]

        class Step:

            def __init__(self, t, i, l):
                self.t, self.i, self.l = t, i, l

            def live(self, d):
                return self.i is not None or 0 <= self.t + d < UNITS

            def wait(self, e, name, d=0):
                if self.i is None and self.t + d < 0:
                    return
                n = self.l * UNITS + (self.t + d)
                A[name].wait(e, n if self.i is None else self.i * (2 * UPP) + n)

            def wait_pack(self, e, w):
                n = self.l * NHP + w
                w_lo.wait(e, n if self.i is None else self.i * 2 + n)

        def pe_step(e, z):
            t = z.t
            if z.live(0):
                b = t % 2
                z.wait(e, "qe")
                z.wait(e, "ke")
                z.wait(e, "kb")
                z.wait(e, "sub", -2)
                for n in range(BPC):
                    h = n % 2 * SEQ
                    ins = e.matmul(ps[h:h + SEQ, BS[b], n // 2 * KEYS0:(n // 2 + 1) * KEYS0],
                                   qs[b][:, n * SEQ:(n + 1) * SEQ], ks[b][:, n, :], start=True, stop=True)
                A["S"].done(ins)
            if z.i is None and t in NORM_STEP:
                z.wait(e, "pt", -2)
                norm0.pe(e, NORM_STEP[t], NB0_HEAD, z.l)
            if z.live(1):
                u = t + 1
                w, c, hd = u // UPP, u % UPP // 2, u % 2
                if u % UPP == 0:
                    z.wait_pack(e, w)
                if z.i is None and u in (0, 2, 4, 5):
                    norm0.split(e, (u + 1) // 2, z.l)
                if z.i is None and u == 0:
                    c_lo.wait(e, KT - 1)
                    norm0.s["ev"].wait(e, (z.l * NCH + 1) * KT - 1)
                for off, src, bank, name, read in ((0, hT, BQ, "q", "qe"), (2 * D, cT, BK, "k", "ke")):
                    z.wait(e, read)
                    for k in range(KT):
                        a = off + k * D + hd * DH0
                        ins = split3(e, ps[:, bank, :], [x[:, a:a + DH0] for x in W[w % 2]],
                                     [x[:, k, c * CH:(c + 1) * CH] for x in src], k == 0, k == KT - 1)
                    A[name].done(ins)
            if z.live(-1):
                b = (t - 1) % 2
                z.wait(e, "nrm", -1)
                z.wait(e, "pt", -2)
                if z.i is None and t in NORM_STEP:
                    norm0.s["ev"].wait(e, (z.l * NCH + NORM_STEP[t] + 1) * KT - 1)
                settled(e)
                for n in range(TPC):
                    ins = e.transpose(ps[0:SEQ, BT, n * P:(n + 1) * P], sm[b][:, n, 0:SEQ], ident)
                A["T"].done(ins)
            if z.live(1):
                u = t + 1
                w, c, hf = u // UPP, u % UPP // 2, u % 2
                z.wait(e, "ve")
                for j in range(2):
                    a = (c * TPC + hf * 2 + j) * P
                    for k in range(KT):
                        ins = split3(e, ps[:, BV, j * D:(j + 1) * D], [x[:, k, a:a + P] for x in cT],
                                     [x[:, (4 + k) * D:(5 + k) * D] for x in W[w % 2]],
                                     j == 0 and k == 0, k == KT - 1)
                A["V"].done(ins)
            if z.live(-1):
                u = t - 1
                z.wait(e, "pt", -1)
                z.wait(e, "ve", -1 if u % 2 else 0)
                z.wait(e, "ol", -2)
                for n in range(TPC):
                    ins = e.matmul(ps[:, BO, n * P:(n + 1) * P], vs[u // 2 % 2][:, n, u % 2 * DH0:(u % 2 + 1) * DH0],
                                   pts[u % 2][:, n, :], start=True, stop=True)
                A["O"].done(ins)
            if z.live(-3):
                v = t - 3
                z.wait(e, "ol", -3 if v % 2 else -2)
                z.wait(e, "acc", -4)
                if z.i is None and t in NORM_STEP:
                    norm0.s["ev"].wait(e, (z.l * NCH + NORM_STEP[t] + 1) * KT - 1)
                for j in range(2):
                    a = (v % 2 * 2 + j) * P
                    for hd in range(2):
                        ins = split3(e, ps[:, BW, j * D:(j + 1) * D], [x[:, a:a + P] for x in oT[(v // 2 * 2 + hd) % 4]],
                                     [x[:, (6 + hd) * D:(7 + hd) * D] for x in W[v // UPP % 2]],
                                     j == 0 and hd == 0, hd == 1)
                A["wo"].done(ins)
            if z.live(-4) and (t - 4) % UPP == UPP - 1:
                z.wait(e, "wo", -4)
                e.sem_inc(w_used.sem, 1)

        def act_step(e, z):
            t = z.t
            head = z.i is None and t in NORM_STEP
            if head:
                for k in range(KT):
                    norm0.act_part(e, NORM_STEP[t], NB0_HEAD, k, z.l)
            if z.live(0):
                z.wait(e, "sub")
                A["exp"].done(e.activation(sm[t % 2], sm[t % 2], ACT.Exp, scale=1.0 / math.sqrt(DH0)))
            if z.live(1):
                u = t + 1
                b = u % 2
                if u % UPP == 0:
                    z.wait_pack(e, u // UPP)
                z.wait(e, "S", -1)
                z.wait(e, "q", 1)
                A["qe"].done(e.activation(qs[b], ps[:, BQ, :], ACT.Identity, bias=head_col(u, 0)))
                z.wait(e, "k", 1)
                A["ke"].done(e.activation(ks[b][:, :, 0:SEQ], cut(ps[:, BK, :], BPC), ACT.Identity, bias=head_col(u, 1)))
            if z.live(-1):
                u = t - 1
                z.wait(e, "T", -1)
                z.wait(e, "O", -3)
                src = cut(ps[0:SEQ, BT, :], TPC)
                e.activation(pts[u % 2][0:SEQ, :, 0:SEQ], src[:, :, 0:SEQ], ACT.Copy)
                A["pt"].done(e.activation(pts[u % 2][SEQ:P, :, SEQ:P], src[:, :, SEQ:P], ACT.Copy))
                z.wait(e, "O", -1)
                z.wait(e, "wo", -5 if u % 2 else -4)
                A["oh"].done(e.activation(oT[u % 4][0], ps[:, BO, :], ACT.Identity, bias=head_col(u, 3)))
            if head:
                for k in range(KT):
                    norm0.act_part(e, NORM_STEP[t], NB0_HEAD, KT + k, z.l)

        def dve_step(e, z):
            t = z.t
            if z.live(1):
                u = t + 1
                if u % UPP == 0:
                    z.wait_pack(e, u // UPP)
                z.wait(e, "S", -1)
                A["kb"].done(e.tensor_copy(ks[u % 2][:, :, SEQ:KEYS0], each(head_col(u, 2), BPC)))
            if z.live(0):
                b = t % 2
                s3 = cut(ps[:, BS[b], 0:TPC * KEYS0], TPC)
                z.wait(e, "S")
                A["mx"].done(e.tensor_reduce(amax[b], s3, axis=AX.X, op=ALU.max))
                z.wait(e, "mx")
                z.wait(e, "T", -2)
                A["sub"].done(e.tensor_tensor(sm[b], s3, many(amax[b], KEYS0), ALU.subtract))
            if z.live(-4):
                v = t - 4
                z.wait(e, "wo", -4)
                if z.i is None and v == 0:
                    norm0.x_plus.wait(e, z.l * NCH + (NCH - 1))
                xs = x_sb[:, v % UPP * 2:v % UPP * 2 + 2, :]
                z.wait(e, "acc", -5)
                A["acc"].done(e.tensor_tensor(xs, cut(ps[:, BW, :], 2), xs, ALU.add))
            if z.live(0):
                b = t % 2
                z.wait(e, "exp")
                A["sum"].done(e.tensor_reduce(asum[b], sm[b], axis=AX.X, op=ALU.add))
                z.wait(e, "sum")
                A["rec"].done(e.reciprocal(arec[b], asum[b]))
                z.wait(e, "rec")
                A["nrm"].done(e.tensor_tensor(sm[b][:, :, 0:SEQ], sm[b][:, :, 0:SEQ], many(arec[b], SEQ), ALU.mult))
            if z.live(1):
                u = t + 1
                hf = u % 2
                z.wait(e, "V", 1)
                z.wait(e, "O", -2 - hf)
                A["ve"].done(e.tensor_tensor(vs[u // 2 % 2][:, 2 * hf:2 * hf + 2, :], cut(ps[:, BV, :], 2),
                                             each(vdiff[u // UPP % 2], 2), ALU.add))
            if z.live(-1):
                u = t - 1
                z.wait(e, "oh", -1)
                A["ol"].done(e.scalar_tensor_tensor(oT[u % 4][1], ps[:, BO, :], head_col(u, 3),
                                                    oT[u % 4][0].bitcast(F32), ALU.add, ALU.subtract))

        def run_units(e, step, l, head, tail):
            lead, turn, drain = 5, 2 * UPP, 4
            trips = (UNITS - 1 - lead) // turn
            for t in range(-1, lead):
                step(e, Step(t, None, l))
                head(e, t)
            with e.Fori(0, trips) as i:
                for t in range(lead, lead + turn):
                    step(e, Step(t, i, l))
            for t in range(lead + trips * turn, UNITS + drain):
                step(e, Step(t, None, l))
                tail(e, t - (UNITS - UPP))

        @on("dve")
        def _(e):
            s_small.done(e.memset(minus_half, -0.5))
            s_small.wait(e, 0)
            e.wait_ge(s_cols, 16)
            e.wait_ge(s_x[0], 16)
            norm0.dve(e, 0)
            split_dve(e, 0, 0, 0, True)
            norm0.dve_lo(e, 0)
            context_dve(e)
            c_lo.wait(e, KT - 1)
            e.memset(pts[0], 0.0)
            pt_zero.done(e.memset(pts[1], 0.0))
            for c in range(1, NCH):
                e.wait_ge(s_x[c], 16)
            with e.Fori(0, 2) as l:
                def head(e, t):
                    for c, at in ((1, -2), (2, -1), (3, 1)):
                        if t == at:
                            norm0.dve_stats(e, c, l)
                        if t == (-2, 0, 2)[c - 1]:
                            norm0.dve_x(e, c, l)
                    if t in NORM_STEP:
                        norm0.dve_lo(e, NORM_STEP[t], l)
                    if t == 4:
                        split_dve(e, l * NHP + 1, 1, l + 1, True)

                def tail(e, k):
                    if k == 5:
                        A["acc"].wait(e, l * UNITS + (UNITS - UPP + 1))
                        norm0.dve_stats(e, 0, l + 1)
                    if k == 6:
                        norm0.dve_x(e, 0, l + 1)
                    if k == 9:
                        norm0.dve_lo(e, 0, l + 1)

                head(e, -2)
                run_units(e, dve_step, l, head, tail)

        def nothing(e, t=None):
            return None

        @on("act")
        def _(e):
            e.wait_ge(s_cols, 16)
            norm0.act(e, 0, NB0)
            split_act(e, 0, 0, 0, True)
            context_act(e)
            pt_zero.wait(e, 0)
            with e.Fori(0, 2) as l:
                def head(e, t):
                    if t == 4:
                        split_act(e, l * NHP + 1, 1, l + 1, True)

                def tail(e, k):
                    if k == 8:
                        norm0.act(e, 0, NB0, l + 1)

                run_units(e, act_step, l, head, tail)

        @on("pe")
        def _(e):
            e.wait_ge(s_cols, 16)
            norm0.pe(e, 0, NB0)
            with e.Fori(0, 2) as l:
                def tail(e, k):
                    if k == 8:
                        norm0.pe(e, 0, NB0, l + 1)

                run_units(e, pe_step, l, nothing, tail)

        def out_row(l):
            return rows[:, bass.ds(l, 1), :].rearrange("p a d -> p (a d)")

        @on("pool")
        def _(e):
            s_small.wait(e, 0)
            norm0.pool(e, 0)
            e.wait_ge(s_rows, 16)
            xs = x_sb[:, 0:TPC, :]
            norm0.s["x"].wait(e, 0)
            norm0.x_plus.done(e.tensor_tensor(xs, xs, each(row("bo1"), TPC), ALU.add))
            with e.Fori(0, 2) as l:
                for c in range(1, NCH):
                    norm0.pool(e, c, out_row(l), l)
                with e.Fori(0, NHP // 2 - 1) as i:
                    for b in range(2):
                        split_pool(e, l * NHP + i * 2 + (2 + b), b, l * (NHP - 1) + i * 2 + b, True)
                split_pool(e, l * NHP + NHP, 0, l * (NHP - 1) + (NHP - 2), True)
                norm0.pool(e, 0, out_row(l + 1), l + 1)

        FAST = iter(range(4, NPACK))
        POOLED = iter(range(2 * (NHP - 1), NPACK))

        def by_chunks(chunk):
            def run(e):
                chunk(e, 0, True, False)
                with e.Fori(1, NCH - 1) as c:
                    chunk(e, c, False, False)
                chunk(e, NCH - 1, False, True)
            return run

        M = dict(zip("W1 W2".split(), stages("pe", 2, "m_W1 m_W2")))
        M |= zip("gel gh".split(), stages("act", 2, "m_gel m_gh"))
        M |= zip("gl res".split(), stages("dve", 2, "m_gl m_res"))
        gelu, resid = arena[:, 0:2 * CH], cut(arena[:, 2 * CH:2 * CH + TILES * D], TILES)
        gelu = cut(gelu, 2)
        gsp = [[split_arena[:, (2 * b + i) * CH:(2 * b + i + 1) * CH] for i in range(2)] for b in range(2)]

        (r_plus,) = stages("pool", 2, "r_plus")

        def mlp(which, func, norm, nxt, out_row, residual, before, seam):
            s = {k: v.phase(NCH * (1 if k == "res" else FT)) for k, v in M.items()}
            xr, x0 = (r_plus.phase(NCH), 0) if residual is not None else (norm.x_plus, 2 * NCH if which == 0 else 0)
            l = 2 if which == 0 else 0
            pack = (2 * NHP, 2 * NHP + 3, 2 * NHP + 6)[which]
            w1, w2 = [cut(w, KT) for w in W[pack % 2]], [cut(w, FT) for w in W[(pack + 1) % 2]]
            base = x_sb if residual is None else residual
            nth = None if seam is None else next(FAST)
            banks = (6, 7)

            def norm_work(engine, f, c, first):
                if first and which == 0:
                    table = {"dve": {0: [("stats", 1)], 1: [("x", 1)], 2: [("stats", 2)], 3: [("x", 2)],
                                     4: [("lo", 1), ("stats", 3)], 5: [("x", 3)], 6: [("lo", 2)], 7: [("lo", 3)]},
                             "pe": {1: [("T", 1)], 3: [("T", 2)], 5: [("T", 3)]},
                             "act": {f: [(2 * (f % 2) + k, f // 2) for k in range(2)] for f in range(2, FT)}}
                    return [(norm, part, m, l) for part, m in table[engine].get(f, ())]
                n, m = (norm, NCH - 1) if first else (nxt, c - 1)
                if n is None:
                    return []
                table = {"dve": {1: "stats", 2: "x", FT - 1: "lo"}, "pe": {3: "T"}, "act": {4 + i: i for i in range(2 * KT)}}
                return [(n, table[engine][f], m, 0)] if f in table[engine] else []

            @by_chunks
            def dve(e, c, first, last):
                if first and which == 0:
                    split_dve(e, pack + 1, (pack + 1) % 2, 3)
                for f in range(FT):
                    g = c * FT + f
                    s["gh"].wait(e, g)
                    s["W2"].wait(e, g - 2)
                    s["gl"].done(e.tensor_tensor(gsp[f % 2][1], gelu[:, f % 2, :], gsp[f % 2][0].bitcast(F32), ALU.subtract))
                    for n, part, m, turn in norm_work("dve", f, c, first):
                        if part == "stats" and not first:
                            s["res"].wait(e, m)
                        {"stats": n.dve_stats, "x": n.dve_x, "lo": n.dve_lo}[part](e, m, turn)
                s["W2"].wait(e, c * FT + (FT - 1))
                xr.wait(e, c + x0)
                rt = base[:, bass.ds(c * TPC, TPC), :]
                s["res"].done(e.tensor_tensor(x_sb[:, bass.ds(c * TPC, TPC), :],
                                              ps[:, 2:4, :].rearrange("p b (t d) -> p (b t) d", d=D), rt, ALU.add))
                if last and seam is not None:
                    split_dve(e, seam, seam % 2, nth)

            @by_chunks
            def act(e, c, first, last):
                if first and which == 0:
                    split_act(e, pack + 1, (pack + 1) % 2, 3, False)
                for f in range(FT):
                    g = c * FT + f
                    s["W1"].wait(e, g)
                    s["gl"].wait(e, g - 2)
                    s["gel"].done(e.activation(gelu[:, f % 2, :], ps[:, f % 2, :], func, bias=col(f"fb{which}", f)))
                    s["gel"].wait(e, g)
                    s["W2"].wait(e, g - 2)
                    s["gh"].done(e.activation(gsp[f % 2][0], gelu[:, f % 2, :], ACT.Copy))
                    for n, part, m, turn in norm_work("act", f, c, first):
                        n.act_part(e, m, banks, part, turn)
                if last and seam is not None:
                    split_act(e, seam, seam % 2, nth, False)

            @by_chunks
            def pool(e, c, first, last):
                if first and which == 0:
                    for j in range(1, NCH):
                        norm.pool(e, j, row(out_row), l)
                if residual is not None:
                    rt = base[:, bass.ds(c * TPC, TPC), :]
                    settled(e)
                    xr.done(e.tensor_tensor(rt, rt, each(row(out_row), TPC), ALU.add))
                if not (first and which == 0):
                    n, m = (norm, NCH - 1) if first else (nxt, c - 1)
                    if n is not None:
                        n.pool(e, m, n.row)

            def up(e, c, f):
                s["gel"].wait(e, c * FT + (f - 2))
                for k in range(KT):
                    ins = split3(e, ps[:, f % 2, :], [w[:, k, f * P:(f + 1) * P] for w in w1],
                                 [x[:, k, bass.ds(c * CH, CH)] for x in hT], k == 0, k == KT - 1)
                s["W1"].done(ins)

            @by_chunks
            def pe(e, c, first, last):
                if first:
                    before["pe"](e)
                    norm.split(e, 0, l)
                    w_lo.wait(e, pack)
                    up(e, 0, 0)
                for f in range(FT):
                    if f + 1 < FT:
                        up(e, c, f + 1)
                    elif not last:
                        norm.split(e, c + 1, l)
                        up(e, c + 1, 0)
                    if first and f == 0:
                        w_lo.wait(e, pack + 1)
                    s["gl"].wait(e, c * FT + f)
                    if f == 0:
                        s["res"].wait(e, c - 1)
                    for j in range(TPC):
                        ins = split3(e, ps[:, 2 + j // 2, j % 2 * D:(j % 2 + 1) * D],
                                     [g[:, j * P:(j + 1) * P] for g in gsp[f % 2]],
                                     [w[:, f, :] for w in w2], f == 0 and j % 2 == 0, f == FT - 1)
                    s["W2"].done(ins)
                    for n, _, m, turn in norm_work("pe", f, c, first):
                        n.pe(e, m, banks, turn)
                    if last and f == FT - 2:
                        s["W1"].wait(e, NCH * FT - 1)
                        e.sem_inc(w_used.sem, 1)

            todo["dve"].append(dve)
            todo["act"] += [before["act"], act]
            todo["pool"] += [before["pool"], pool]
            todo["pe"].append(pe)

            @on("pe")
            def _(e):
                s["W2"].wait(e, NCH * FT - 1)
                e.sem_inc(w_used.sem, 1)

            return s

        H = dict(zip("pj S T PV out".split(), stages("pe", 2, "h_pj h_S h_T h_PV h_out")))
        H |= zip("c ea exp pt ah".split(), stages("act", 2, "h_c h_ea h_exp h_pt h_ah"))
        H |= zip("cl ev m mx neg rec a1 a2 al res".split(),
                 stages("dve", 2, "h_cl h_ev h_m h_mx h_neg h_rec h_a1 h_a2 h_al h_res"))
        H |= zip(["nrm"], stages("pool", 2, "h_nrm"))
        (mask_ready,) = stages("", 0, "mask_ready")
        G = H1 // 2
        PW = 2 * DH1

        def narrow(layer, nk, norm, nxt, qb, kb, vb, out_row, mask, before):
            own = nk > SEQ
            nsrc = nk // SEQ
            pack = 2 * NHP + 2 + 3 * (layer - 1)
            wb = W[pack % 2]
            nth_pack, nth_pool = next(FAST), next(POOLED)
            scale = 1.0 / (DH1 if own else math.sqrt(DH1))
            NQK, NV = KT + KT * nsrc, BPC // 2
            NPJ = NQK + NV
            bank_of = [0, 1, 2, 3, 0, 1][:NQK] + [4, 5, 6, 7]
            LAG = 3
            SPT = P // nk
            fill = {BPC: (0, 1), BPC + 1: (2, 3) if own else (), BPC + 2: range(4 if own else 2, NQK)}
            OUT = (2, 3)
            banks = (4, 5)
            per = {"pj": NPJ, "ea": NQK, "ev": NV, "c": 1, "cl": 1, "ah": 1, "al": 1, "out": 2, "res": 2}
            s = {k: v.phase(NCH * per.get(k, BPC)) for k, v in H.items()}
            xr = r_plus.phase(NCH) if out_row else norm.x_plus
            mask_ok = mask_ready.phase(2)
            NT = 3
            mraw, qz, v_sb, pt, aT, tmp, maskb, kT = carve(
                arena, [NT * G * P, KT * BPC * P, BPC * (D if own else P), G * nk, KT * CH, KT * SEQ, NB * SEQ // 2, KT * BPC * nk])
            maskb = maskb.bitcast(BF16)
            tt = [cut(mraw[:, b * G * P:b * G * P + G * nk], G) for b in range(NT)]
            qz = qz.rearrange("p (k u h n) -> p k u h n", k=KT, u=BPC, h=2)
            kT = kT.rearrange("p (k u n) -> p k u n", k=KT, u=BPC)
            v_sb, pt, aT, tmp = cut(v_sb, BPC), cut(pt, G // SPT), cut(aT, KT), cut(tmp, KT)
            mx, neg, sums, recs = ([small[:, 128 + 16 * i + 8 * b:136 + 16 * i + 8 * b] for b in range(2)] for i in range(4))
            qzb = cut(small[:, 72:72 + 2 * KT], 2)
            kv = [cut(split_arena[:, 2048 * i:2048 * i + KT * BPC * nk], KT) for i in range(2)]
            at = 2048 - KT * CH if not own else 0
            asp = [cut(split_arena[:, 2048 * i + at:2048 * i + at + KT * CH], KT) for i in range(2)]

            def kv_parts(i, c):
                for k in range(KT):
                    dst = cut(kv[i][:, k, :], BPC)
                    yield dst[:, :, 0:SEQ], cut(cT[i][:, k, bass.ds(c * CH, CH)], BPC)
                    if own:
                        yield dst[:, :, SEQ:nk], cut(hT[i][:, k, bass.ds(c * CH, CH)], BPC)

            def kv_free(e, c):
                s["pj"].wait(e, c * NPJ - 1)
                if own:
                    s["out"].wait(e, c * 2 - 1)
                norm.split(e, c)

            def kv_act(e, c):
                kv_free(e, c)
                settled(e)
                for dst, src in kv_parts(0, c):
                    ins = e.activation(dst, src.bitcast(F32), ACT.Copy)
                s["c"].done(ins)

            def kv_dve(e, c):
                kv_free(e, c)
                settled(e)
                for dst, src in kv_parts(1, c):
                    ins = e.tensor_copy(dst, src.bitcast(F32))
                s["cl"].done(ins)

            def behind(c, first):
                return (norm, NCH - 1) if first else (nxt, c - 1)

            def project(e, c, i):
                bank = ps[:, bank_of[i], :]
                if i < 4:
                    s["m"].wait(e, c * BPC - 1)
                    if i == 0:
                        norm.split(e, c)
                elif i < NQK:
                    s["ea"].wait(e, c * NQK + (i - 4))
                else:
                    s["a2"].wait(e, c * BPC - 1)
                if i < NQK:
                    m, src = (i, 0) if i < KT else ((i - KT) // nsrc, (i - KT) % nsrc)
                    w0 = 0 if i < KT else 2 * D
                    rhs = hT if i < KT or src else cT
                    for k in range(KT):
                        ins = split3(e, bank, [w[:, w0 + k * D + m * P:w0 + k * D + (m + 1) * P] for w in wb],
                                     [x[:, k, bass.ds(c * CH, CH)] for x in rhs], k == 0, k == KT - 1)
                else:
                    j = i - NQK
                    if j == 0:
                        s["c"].wait(e, c)
                        s["cl"].wait(e, c)
                    for m in range(nsrc):
                        a = (nsrc * j + m) * P
                        for k in range(KT):
                            ins = split3(e, bank[:, m * D:(m + 1) * D], [x[:, k, a:a + P] for x in kv],
                                         [w[:, (4 + k) * D:(5 + k) * D] for w in wb], m == 0 and k == 0, k == KT - 1)
                s["pj"].done(ins)

            def output(e, c):
                s["al"].wait(e, c)
                s["ea"].wait(e, c * NQK + (NQK - 1))
                for i in range(2):
                    for j in range(2):
                        a = (2 * i + j) * P
                        for k in range(KT):
                            ins = split3(e, ps[:, OUT[i], j * D:(j + 1) * D], [x[:, k, a:a + P] for x in asp],
                                         [w[:, (6 + k) * D:(7 + k) * D] for w in wb], j == 0 and k == 0, k == KT - 1)
                    s["out"].done(ins)

            @by_chunks
            def pe(e, c, first, last):
                if first:
                    before["pe"](e)
                    w_lo.wait(e, pack)
                    for i in range(NQK):
                        project(e, c, i)
                    norm.s["ev"].wait(e, (NCH - 1) * KT - 1)
                else:
                    s["ea"].wait(e, c * NQK + 3 if own else c * NQK + (NQK - 1))
                    output(e, c - 1)
                s["ea"].wait(e, c * NQK + (NQK - 1))
                s["res"].wait(e, c * 2 - 1)
                for u in range(BPC + LAG):
                    g = c * BPC + u
                    h, b = g - LAG, (u - LAG) % 2
                    if u >= LAG:
                        s["nrm"].wait(e, h)
                        s["pt"].wait(e, h - 1)
                        if u == LAG:
                            s["ev"].wait(e, c * NV + (NV - 1))
                        if u == 5:
                            n, m = behind(c, first)
                            n.s["ev"].wait(e, m * KT + (KT - 1))
                        settled(e)
                        t = tt[(u - LAG) % NT]
                        for n in range(G // SPT):
                            ins = e.transpose(ps[:, banks[n // 4], n % 4 * P:(n % 4 + 1) * P],
                                              t[:, n * SPT:(n + 1) * SPT, :].rearrange("p a n -> p (a n)"), ident)
                        s["T"].done(ins)
                    if u < BPC:
                        s["m"].wait(e, g - 1)
                        for k in range(KT):
                            for j in range(G // KT):
                                r = j * PW
                                ins = e.matmul(ps[:, j, k * nk:(k + 1) * nk],
                                               qz[r:r + PW, k, u, :, :].rearrange("p h n -> p (h n)"),
                                               kT[r:r + PW, k, u, :], start=True, stop=True)
                        s["S"].done(ins)
                        for i in range(NQK + 2 * u, min(NQK + 2 * u + 2, NPJ)):
                            project(e, c, i)
                    elif not last and u < BPC + 2:
                        for i in fill[u]:
                            project(e, c + 1, i)
                    if u >= LAG:
                        s["pt"].wait(e, h)
                        s["a2"].wait(e, h - (2 if own else 1))
                        settled(e)
                        for i in range(G):
                            j, k = i % (G // KT), i // (G // KT)
                            if own:
                                ins = e.matmul(ps[j * PW:(j + 1) * PW, 6 + b, k * P:(k + 1) * P],
                                               v_sb[:, u - LAG, k * P + j * PW:k * P + (j + 1) * PW],
                                               pt[:, j * KT + k, :], start=True, stop=True)
                            else:
                                rows_k = slice(k * SEQ, (k + 1) * SEQ)
                                ins = e.matmul(ps[j * PW:(j + 1) * PW, 6 + k, 0:P],
                                               v_sb[rows_k, u - LAG, j * PW:(j + 1) * PW],
                                               pt[rows_k, j, :], start=True, stop=True)
                        s["PV"].done(ins)
                    if u == 4:
                        n, m = behind(c, first)
                        s["pt"].wait(e, h)
                        n.pe(e, m, banks)
                    if not last and u == BPC + 2:
                        for i in fill[u]:
                            project(e, c + 1, i)
                if last:
                    output(e, c)
                    s["out"].wait(e, 2 * NCH - 1)
                    e.sem_inc(w_used.sem, 1)

            def evacuate(e, c, i):
                bank = ps[:, bank_of[i], :]
                s["pj"].wait(e, c * NPJ + i)
                if i < KT:
                    for h, part in enumerate(("even", "odd")):
                        ins = e.activation(qz[:, i, :, h, :], cut(bank, BPC), ACT.Identity,
                                           bias=qzb[:, h, i:i + 1], scale=col(part))
                else:
                    m, src = (i - KT) // nsrc, (i - KT) % nsrc
                    ins = e.activation(kT[:, m, :, src * SEQ:(src + 1) * SEQ], cut(bank, BPC), ACT.Identity, bias=col(kb, m))
                s["ea"].done(ins)

            @by_chunks
            def act(e, c, first, last):
                if first:
                    before["act"](e)
                    raw_mask = mraw[:, 0:NB * SEQ].bitcast(I32) if own else mraw.bitcast(U8)[:, 0:NB * SEQ]
                    e.dma_start(raw_mask, mask.rearrange("b s -> (b s)").partition_broadcast(P)).then_inc(s_mask, 16)
                    mask_ok.wait(e, 0)
                    for i in range(KT):
                        evacuate(e, c, i)
                    kv_act(e, c)
                    for i in range(KT, NQK):
                        evacuate(e, c, i)
                else:
                    s["a2"].wait(e, c * BPC - 1)
                    s["out"].wait(e, (c - 1) * 2 - 1)
                    s["ah"].done(e.activation(asp[0], aT, ACT.Copy))
                    for i in fill[BPC + 2]:
                        evacuate(e, c, i)
                if own and not first:
                    kv_act(e, c)
                for u in range(BPC + LAG):
                    g = c * BPC + u
                    if u >= LAG:
                        h, b = g - LAG, (u - LAG) % 2
                        s["T"].wait(e, h)
                        s["PV"].wait(e, h - 1)
                        src = ps[:, banks[0]:banks[0] + 2 // SPT, :].rearrange("p b (t n) -> p (b t) n", n=P)
                        s["pt"].done(e.activation(pt, src, ACT.Copy))
                    n, m = behind(c, first)
                    if u in (4, 5):
                        for part in range(KT):
                            n.act_part(e, m, banks, (u - 4) * KT + part)
                    if 1 <= u <= BPC:
                        s["neg"].wait(e, g - 1)
                        s["rec"].wait(e, g - 3)
                        b = (u - 1) % 2
                        for n in range(G):
                            t = tt[(u - 1) % NT][:, n, :]
                            ins = e.activation(t, t, ACT.Exp, scale=scale, bias=neg[b][:, n:n + 1],
                                               accum_out=sums[b][:, n:n + 1])
                        s["exp"].done(ins)
                    if u >= BPC and not last:
                        if u == BPC + 1 and not own:
                            kv_act(e, c + 1)
                        if u < BPC + 2:
                            for i in fill[u]:
                                evacuate(e, c + 1, i)
                if last:
                    s["a2"].wait(e, (c + 1) * BPC - 1)
                    s["out"].wait(e, c * 2 - 1)
                    s["ah"].done(e.activation(asp[0], aT, ACT.Copy))
                    if pack + 2 < NPACK:
                        split_act(e, pack + 2, pack % 2, nth_pack, False)

            def split_output(e, c):
                s["ah"].wait(e, c)
                s["al"].done(e.tensor_tensor(asp[1], aT, asp[0].bitcast(F32), ALU.subtract))

            def residual(e, c):
                xr.wait(e, c)
                for i in range(2):
                    s["out"].wait(e, c * 2 + i)
                    xs = x_sb[:, bass.ds(c * TPC + 2 * i, 2), :]
                    s["res"].done(e.tensor_tensor(xs, cut(ps[:, OUT[i], :], 2), xs, ALU.add))

            @by_chunks
            def dve(e, c, first, last):
                if first:
                    for h, part in enumerate(("even", "odd")):
                        ins = e.tensor_scalar(qzb[:, h, :], col(qb, 0, KT), col(part), None, ALU.mult)
                    mask_ok.done(ins)
                    kv_dve(e, c)
                    e.wait_ge(s_mask, 16 * layer)
                    src = mraw[:, 0:NB * SEQ].bitcast(I32) if own else mraw.bitcast(U8)[:, 0:NB * SEQ]
                    mask_ok.done(e.tensor_scalar(maskb, src, 0.0, NEG, ALU.is_equal, ALU.mult))
                else:
                    split_output(e, c - 1)
                    residual(e, c - 1)
                    if own:
                        kv_dve(e, c)
                for u in range(BPC + LAG):
                    g = c * BPC + u
                    if u < BPC:
                        b = u % 2
                        t = tt[u % NT]
                        sps = ps[:, 0:G // KT, 0:KT * nk].rearrange("p b (t n) -> p b t n", n=nk)
                        t4 = t.rearrange("p (b t) n -> p b t n", t=KT)
                        mk = each(maskb[:, bass.ds(g * SEQ, SEQ)], G).rearrange("p (b t) n -> p b t n", t=KT)
                        s["S"].wait(e, g)
                        s["T"].wait(e, g - NT)
                        if first and u == 0:
                            mask_ok.wait(e, 1)
                        ins = e.tensor_tensor(t4[:, :, :, 0:SEQ], sps[:, :, :, 0:SEQ], mk, ALU.add)
                        if own:
                            ins = e.tensor_copy(t4[:, :, :, SEQ:nk], sps[:, :, :, SEQ:nk])
                        s["m"].done(ins)
                        s["m"].wait(e, g)
                        s["mx"].done(e.tensor_reduce(mx[b], t, axis=AX.X, op=ALU.max))
                        s["mx"].wait(e, g)
                        s["exp"].wait(e, g - 2)
                        s["neg"].done(e.tensor_scalar(neg[b], mx[b], -scale, None, ALU.mult))
                    if 1 <= u <= BPC:
                        s["exp"].wait(e, g - 1)
                        s["nrm"].wait(e, g - 3)
                        s["rec"].done(e.reciprocal(recs[(u - 1) % 2], sums[(u - 1) % 2]))
                    for i in range(2 * u, min(2 * u + 2, NV)):
                        s["pj"].wait(e, c * NPJ + (NQK + i))
                        s["PV"].wait(e, c * BPC - 1)
                        bank = ps[:, bank_of[NQK + i], :]
                        if own:
                            ins = e.tensor_tensor(v_sb[:, 2 * i:2 * i + 2, :], cut(bank, 2), each(row(vb), 2), ALU.add)
                        else:
                            for m in range(2):
                                frm = slice(m * SEQ, (m + 1) * SEQ)
                                for k in range(KT):
                                    a = slice(k * P, (k + 1) * P)
                                    ins = e.tensor_tensor(v_sb[k * SEQ:(k + 1) * SEQ, 2 * i + m, :],
                                                          bank[frm, a], row(vb)[frm, a], ALU.add)
                        s["ev"].done(ins)
                    if u >= LAG:
                        h = g - LAG
                        s["PV"].wait(e, h)
                        xv = cut(ps[:, 6 + (u - LAG) % 2, 0:KT * P], KT) if own else ps[:, 6:8, 0:P]
                        s["a2"].wait(e, h - 1)
                        s["a1"].done(e.tensor_scalar(tmp, xv[:, :, SEQ:P], col("odd"), None, ALU.mult))
                        s["a1"].wait(e, h)
                        if u == LAG:
                            s["al"].wait(e, c - 1)
                        s["a2"].done(e.scalar_tensor_tensor(aT[:, :, (u - LAG) * SEQ:(u - LAG + 1) * SEQ], xv[:, :, 0:SEQ],
                                                            col("even"), tmp, ALU.mult, ALU.add))
                    if u in (2, 3):
                        n, m = behind(c, first)
                        (n.dve_stats, n.dve_x)[u - 2](e, m)
                    if u == 6:
                        n, m = behind(c, first)
                        n.dve_lo(e, m)
                    if u == BPC + 1 and not own and not last:
                        kv_dve(e, c + 1)
                if last:
                    split_output(e, c)
                    residual(e, c)
                    if pack + 2 < NPACK:
                        split_dve(e, pack + 2, pack % 2, nth_pack)

            @by_chunks
            def pool(e, c, first, last):
                if first:
                    split_pool(e, pack + 1, (pack + 1) % 2, nth_pool, False)
                for u in range(1, BPC + 1):
                    h = c * BPC + (u - 1)
                    s["rec"].wait(e, h)
                    t = tt[(u - 1) % NT]
                    s["nrm"].done(e.tensor_tensor(t, t, many(recs[(u - 1) % 2], nk), ALU.mult))
                    if u == 2:
                        n, m = behind(c, first)
                        n.pool(e, m, n.row)
                    if u == 5 and out_row:
                        if first:
                            before["pool"](e)
                        norm.s["x"].wait(e, c)
                        settled(e)
                        xs = x_sb[:, bass.ds(c * TPC, TPC), :]
                        xr.done(e.tensor_tensor(xs, xs, each(row(out_row), TPC), ALU.add))

            for name, part in (("pe", pe), ("act", act), ("dve", dve), ("pool", pool)):
                todo[name].append(part)
            return s


        def after(steps, n):
            return lambda e: steps.wait(e, n)

        def last_of(steps, n=NCH - 1):
            return {e: after(steps, n) for e in ("pe", "act")} | {"pool": nothing}

        norm1 = Norm("none", 0.0, static_affine("one"))
        mlp0 = mlp(0, ACT.Gelu, norm0, norm1, "b_fc2", None,
                   {"pe": after(norm0.s["ev"], (2 * NCH + 1) * KT - 1), "act": nothing, "pool": nothing}, 2 * NHP + 2)

        def spill_tokens(e):
            mlp0["res"].wait(e, NCH - 1)
            e.dma_start(spill.rearrange("(t p) d -> p t d", p=P), x_sb).then_inc(s_spill, 16)

        rms1 = Norm("rms", 1e-6, static_affine("rms"))
        narrow1 = narrow(1, 2 * SEQ, norm1, rms1, "l1q", "l1k", "l1v", "out_b", mask1,
                         last_of(mlp0["res"]) | {"act": spill_tokens, "pool": lambda e: e.wait_ge(s_spill, 16)})

        def fetch_tokens(e):
            narrow1["res"].wait(e, 2 * NCH - 1)
            e.dma_start(resid, spill.rearrange("(t p) d -> p t d", p=P)).then_inc(s_back, 16)

        norm2 = Norm("layer", 1e-5, static_affine("l2n"), row=row("cproj_b"))
        mlp1 = mlp(1, ACT.Gelu_apprx_tanh, rms1, norm2, "mlp_b2", resid,
                   last_of(narrow1["res"], 2 * NCH - 1) | {"act": fetch_tokens, "pool": lambda e: e.wait_ge(s_back, 16)},
                   2 * NHP + 5)
        norm2m = Norm("layer", 1e-5, static_affine("l2m"), row=row("proj_b"))
        narrow2 = narrow(2, SEQ, norm2, norm2m, "l2q", "l2k", "l2v", None, mask2, last_of(mlp1["res"]))
        mlp2 = mlp(2, ACT.Gelu_apprx_tanh, norm2m, None, None, None, last_of(narrow2["res"], 2 * NCH - 1), None)

        Z = {k: v.phase(TILES) for k, v in zip("F pj T Y wy".split(), stages("pe", 4, "z_F z_pj z_T z_Y z_wy"))}
        Z |= {k: v.phase(TILES) for k, v in zip("exp pt ye".split(), stages("act", 4, "z_exp z_pt z_ye"))}
        Z |= {k: v.phase(TILES) for k, v in zip("mx neg pe rec ge we st".split(),
                                                 stages("dve", 4, "z_mx z_neg z_pe z_rec z_ge z_we z_st"))}
        Z |= {k: v.phase(TILES) for k, v in zip("xc nrm".split(), stages("pool", 4, "z_xc z_nrm"))}
        (z_c,) = (s.phase(16) for s in stages("", 0, "z_c"))
        (z_o,) = (s.phase(NCH) for s in stages("", 0, "z_o"))
        (z_p,) = (s.phase(1) for s in stages("", 0, "z_p"))
        (z_w,) = (s.phase(NCH // 2) for s in stages("", 0, "z_w"))
        NZ = 4
        s_ct = [semaphore(f"s_ct{b}") for b in range(2)]
        got = carve(arena, [D] * 4 + [D] * 6 + [2 * 2 * CI] * 4 + [4 * D] * 2 + [4 * D] + [D] * 2 + [TILES * D])
        xc, cx, th, ph = got[0:4], got[4:6], got[6:8], got[8:10]
        gx = [cut(g, 2) for g in got[10:14]]
        ff = [cut(g, 4) for g in got[14:16]]
        fT, yT, wy = got[16], got[17:19], cut(got[19], TILES)
        bst = cut(norm_arena[:, 0:2 * TILES * 6], 2 * TILES)
        zmx, zneg, zsum, zrec = ([small[:, 184 + 8 * i + 4 * b:188 + 8 * i + 4 * b] for b in range(2)] for i in range(4))
        zs = [small[:, 216 + i:217 + i] for i in range(12)]

        class Tile:

            def __init__(self, t, i):
                self.t, self.i = t, i

            def live(self, d):
                return self.i is not None or 0 <= self.t + d < TILES

            def n(self, d=0):
                return self.t + d if self.i is None else self.i * NZ + (self.t + d)

            def wait(self, e, name, d=0):
                Z[name].wait(e, self.n(d))

        def z_pe(e, z):
            t = z.t
            if z.live(-2):
                b = t % 2
                z.wait(e, "nrm", -2)
                z.wait(e, "pt", -3)
                for a in range(2):
                    for jh in range(2):
                        for ih in range(2):
                            at = (2 * jh + ih) * P
                            ins = e.transpose(ps[:, 4 + a, at:at + P], ff[b][:, 2 * a + ih, jh * P:(jh + 1) * P], ident)
                Z["T"].done(ins)
            if z.live(0):
                b = t % 2
                z.wait(e, "pe")
                z.wait(e, "exp", -1)
                for ih in range(2):
                    for a in range(2):
                        r = a * CI
                        ins = e.matmul(ps[:, 2 + a, ih * D:(ih + 1) * D], ph[b][r:r + CI, ih * P:(ih + 1) * P],
                                       th[b][r:r + CI, :], start=True, stop=True)
                Z["F"].done(ins)
            if z.live(-3):
                z.wait(e, "ye", -3)
                z.wait(e, "we", -4)
                Z["wy"].done(e.matmul(ps[:, 7, 0:D], col("wz", 0, P)[0:2 * CI, :], yT[(t - 3) % 2][0:2 * CI, :], start=True, stop=True))
            if z.live(1):
                b = (t + 1) % 2
                z.wait(e, "xc", 1)
                turns = 16 * ((t + 1) // 2 + 1)
                e.wait_ge(s_ct[b], turns if z.i is None else z.i * (16 * NZ // 2) + turns)
                z.wait(e, "pe")
                z.wait(e, "ge")
                e.matmul(ps[0:2 * CI, 0, 0:D], col("wth", 0, 2 * CI), xc[(t + 1) % 4], start=True, stop=True)
                e.matmul(ps[0:2 * CI, 0, D:2 * D], col("wph", 0, 2 * CI), cx[b], start=True, stop=True)
                for q in range(2):
                    ins = e.matmul(ps[:, 1, q * 2 * CI:(q + 1) * 2 * CI], xc[(t + 1) % 4][:, q * P:(q + 1) * P],
                                   col("wg", 0, 2 * CI), start=True, stop=True)
                Z["pj"].done(ins)
            if z.live(-2):
                z.wait(e, "pt", -2)
                z.wait(e, "ye", -3)
                for jh in range(2):
                    for a in range(2):
                        ins = e.matmul(ps[a * CI:(a + 1) * CI, 6, 0:D], gx[(t - 2) % 4][:, jh, a * CI:(a + 1) * CI],
                                       fT[:, (2 * a + jh) * D:(2 * a + jh + 1) * D], start=jh == 0, stop=jh == 1,
                                       skip_group_check=True)
                Z["Y"].done(ins)

        def z_act(e, z):
            t = z.t
            if z.live(-2):
                z.wait(e, "T", -2)
                z.wait(e, "Y", -3)
                Z["pt"].done(e.activation(cut(fT, 2), ps[:, 4:6, :], ACT.Copy))
            if z.live(0):
                b = t % 2
                z.wait(e, "neg")
                z.wait(e, "T", -2)
                z.wait(e, "rec", -2)
                for q in range(4):
                    ins = e.activation(ff[b][:, q, :], ps[:, 2 + q // 2, q % 2 * D:(q % 2 + 1) * D], ACT.Exp,
                                       bias=zneg[b][:, q:q + 1], accum_out=zsum[b][:, q:q + 1])
                Z["exp"].done(ins)
            if z.live(-2):
                z.wait(e, "Y", -2)
                z.wait(e, "wy", -4)
                Z["ye"].done(e.activation(yT[(t - 2) % 2][0:2 * CI, :], ps[0:2 * CI, 6, 0:D], ACT.Copy))

        def z_dve(e, z):
            t = z.t
            if z.live(0):
                b = t % 2
                f4 = ps[:, 2:4, :].rearrange("p b (q n) -> p (b q) n", n=D)
                z.wait(e, "F")
                Z["mx"].done(e.tensor_reduce(zmx[b], f4, axis=AX.X, op=ALU.max))
                z.wait(e, "mx")
                z.wait(e, "exp", -2)
                Z["neg"].done(e.tensor_scalar(zneg[b], zmx[b], -1.0, None, ALU.mult))
            if z.live(1):
                b = (t + 1) % 2
                z.wait(e, "pj", 1)
                z.wait(e, "F", -1)
                e.tensor_scalar(th[b][0:2 * CI, :], ps[0:2 * CI, 0, 0:D], col("bth")[0:2 * CI, :], None, ALU.add)
                Z["pe"].done(e.tensor_scalar(ph[b][0:2 * CI, :], ps[0:2 * CI, 0, D:2 * D], col("bph")[0:2 * CI, :], None, ALU.add))
                z.wait(e, "Y", -3)
                Z["ge"].done(e.tensor_tensor(gx[(t + 1) % 4], cut(ps[:, 1, 0:4 * CI], 2), each(row("bg")[:, 0:2 * CI], 2), ALU.add))
            if z.live(-3):
                z.wait(e, "wy", -3)
                dst = wy[:, bass.ds(z.n(-3), 1), :].rearrange("p a d -> p (a d)")
                Z["we"].done(e.tensor_scalar(dst, ps[:, 7, 0:D], col("bz"), None, ALU.add))
                z.wait(e, "we", -3)
                settled(e)
                Z["st"].done(e.bn_stats(bst[:, bass.ds(z.n(-3), 1), :].rearrange("p a d -> p (a d)"), dst))
            if z.live(0):
                b = t % 2
                z.wait(e, "exp")
                z.wait(e, "nrm", -2)
                Z["rec"].done(e.reciprocal(zrec[b], zsum[b]))

        def z_pool(e, z):
            t = z.t
            if z.live(0):
                b = t % 2
                z.wait(e, "rec")
                Z["nrm"].done(e.tensor_tensor(ff[b], ff[b], many(zrec[b], D), ALU.mult))
            if z.live(2):
                z.wait(e, "pj", -2)
                settled(e)
                Z["xc"].done(e.tensor_copy(xc[(t + 2) % 4], x_sb[:, bass.ds(z.n(2), 1), :].rearrange("p a d -> p (a d)")))

        def run_tiles(e, step):
            lead, drain = 4, 3
            trips = (TILES - 2 - lead) // NZ
            for t in range(-2, lead):
                step(e, Tile(t, None))
            with e.Fori(0, trips) as i:
                for t in range(lead, lead + NZ):
                    step(e, Tile(t, i))
            for t in range(lead + NZ * trips, TILES + drain):
                step(e, Tile(t, None))

        @on("sp")
        def _(e):
            mlp2["res"].wait(e, NCH - 1)
            with e.Fori(0, TILES // 2) as i:
                for b in range(2):
                    Z["pj"].wait(e, i * 2 + (b - 2))
                    e.dma_start(cx[b], ctx_tok[bass.ds(i * 2 + b, 1), :, :].rearrange("a p d -> (a p) d")).then_inc(s_ct[b], 16)

        @on("pe")
        def _(e):
            run_tiles(e, z_pe)

        @on("act")
        def _(e):
            mlp2["res"].wait(e, NCH - 1)
            run_tiles(e, z_act)
            z_c.wait(e, 10)
            for c in range(1, NCH, 2):
                w = wy[:, c * TPC:(c + 1) * TPC, :]
                z_w.done(e.activation(w, w, ACT.Identity, bias=zs[1], scale=zs[10]))

        @on("pool")
        def _(e):
            mlp2["res"].wait(e, NCH - 1)
            run_tiles(e, z_pool)
            z_c.wait(e, 2)
            z_p.done(e.tensor_tensor(zs[3][0:SEQ, :], zs[2][0:SEQ, :], minus_half[0:SEQ, 0:1], ALU.pow))

        @on("dve")
        def _(e):
            run_tiles(e, z_dve)
            lower = slice(0, SEQ)
            count = [0]

            def then(ins):
                z_c.done(ins)
                z_c.wait(e, count[0])
                count[0] += 1

            Z["st"].wait(e, TILES - 1)
            then(e.tensor_copy(bst[lower, TILES:2 * TILES, :], bst[SEQ:P, 0:TILES, :]))
            then(e.bn_aggr(zs2, bst[lower, :, :].rearrange("p t s -> p (t s)")))
            then(e.tensor_scalar(zs[2][lower, :], zs2[:, 1:2], 1e-5, None, ALU.add))
            z_p.wait(e, 0)
            then(e.tensor_tensor(zs[4][lower, :], zs[3][lower, :], zs[3][lower, :], ALU.mult))
            then(e.tensor_tensor(zs[5][lower, :], zs[4][lower, :], zs[2][lower, :], ALU.mult))
            then(e.tensor_scalar(zs[6][lower, :], zs[5][lower, :], -0.5, 1.5, ALU.mult, ALU.add))
            then(e.tensor_tensor(zs[7][lower, :], zs[3][lower, :], zs[6][lower, :], ALU.mult))
            e.tensor_copy(zs[8][lower, :], zs2[:, 0:1])
            e.tensor_copy(zs[8][SEQ:P, :], zs2[:, 0:1])
            e.tensor_copy(zs[9][lower, :], zs[7][lower, :])
            then(e.tensor_copy(zs[9][SEQ:P, :], zs[7][lower, :]))
            then(e.tensor_tensor(zs[10], zs[9], col("gam"), ALU.mult))
            then(e.tensor_tensor(zs[0], zs[8], zs[10], ALU.mult))
            then(e.tensor_tensor(zs[1], col("bet"), zs[0], ALU.subtract))
            for c in range(NCH):
                w, x = wy[:, c * TPC:(c + 1) * TPC, :], x_sb[:, c * TPC:(c + 1) * TPC, :]
                if c % 2 == 0:
                    then(e.tensor_scalar(w, w, zs[8], zs[10], ALU.subtract, ALU.mult))
                    z_o.done(e.scalar_tensor_tensor(x, w, col("bet"), x, ALU.add, ALU.add))
                else:
                    z_w.wait(e, c // 2)
                    z_o.done(e.tensor_tensor(x, w, x, ALU.add))

        zs2 = small[0:SEQ, 232:234]

        @on("sp")
        def _(e):
            to = out.rearrange("(t p) d -> p t d", p=P)
            for c in range(NCH):
                z_o.wait(e, c)
                e.dma_start(to[:, c * TPC:(c + 1) * TPC, :], x_sb[:, c * TPC:(c + 1) * TPC, :]).then_inc(s_out, 16)
            e.wait_ge(s_out, 16 * NCH)
            e.wait_ge(s_spill, 16)

        block = ctx.enter_context(nc.Block())

        def program(name):
            def run(e):
                for s in owned.get(name, ()):
                    e.sem_inc(s.sem, s.ahead)
                for f in todo[name]:
                    f(e)
            return run

        block.sync(program("sp"))
        block.scalar(program("act"))
        block.vector(program("dve"))
        block.gpsimd(program("pool"))
        block.tensor(program("pe"))


def kernel(**inputs):
    import concourse.bacc as bacc
    from concourse.bass_utils import run_bass_kernel_spmd

    v = {k: np.asarray(a) for k, a in inputs.items()}
    f0, f1, f2, f3 = (f"L{i}_xattn_" for i in range(4))

    def rows_on_partitions(w):
        return w.reshape(-1, P, w.shape[1]).transpose(1, 0, 2).reshape(P, -1)

    packs, pairs = [], []
    zero8 = np.zeros((P, 8), np.float32)
    for a in (1, 2):
        g = {n: v[f"{f0}{n}{a}"] for n in ("wq", "wk", "wv", "wo", "bq", "bk", "bv", "bias_k", "bias_v")}
        for w in range(NHP):
            c = slice(w * 2 * DH0, (w + 1) * 2 * DH0)
            bias = [g[n].reshape(-1)[c].reshape(2, DH0).T for n in ("bq", "bk", "bias_k", "bias_v")]
            packs.append([rows_on_partitions(g["wq"][:, c]), rows_on_partitions(g["wk"][:, c]),
                          rows_on_partitions(g["wv"][:, c]), rows_on_partitions(g["wo"][c, :]), *bias])
            pairs.append([g["bv"][c], g["bias_v"].reshape(-1)[c]])
    kv = v[f1 + "kv_w"].reshape(D, D, 2)
    kvb = v[f1 + "kv_b"].reshape(D, 2)
    packs += [[rows_on_partitions(v[f0 + "w_fc1"]), zero8], [rows_on_partitions(v[f0 + "w_fc2"]), zero8],
              [*(rows_on_partitions(w) for w in (v[f1 + "q_w"], kv[:, :, 0], kv[:, :, 1], v[f1 + "out_w"])), zero8],
              [rows_on_partitions(v[f1 + "mlp_w1"]), zero8], [rows_on_partitions(v[f1 + "mlp_w2"]), zero8],
              [*(rows_on_partitions(v[f2 + n]) for n in ("q_w", "k_w", "v_w", "cproj_w")), zero8],
              [rows_on_partitions(v[f2 + "fc_w"]), zero8], [rows_on_partitions(v[f2 + "proj_w"]), zero8]]
    wpack = np.stack([np.concatenate(p, axis=1) for p in packs])
    pairs.append([np.zeros(2 * DH0, np.float32)] * 2)
    vb = np.stack([np.concatenate(p) for p in pairs])

    consts = np.zeros((P, NCOL), np.float32)

    def put(name, *vectors):
        blocks = [a.reshape(-1, P).T if a.ndim == 1 else a for a in vectors]
        block = np.concatenate(blocks, axis=1)
        consts[:block.shape[0], COLS[name][0]:COLS[name][0] + block.shape[1]] = block

    one, nil = np.ones(D, np.float32), np.zeros(D, np.float32)
    put("ln1", v[f0 + "ln1_scale"], v[f0 + "ln1_offset"])
    put("ln2", v[f0 + "ln2_scale"], v[f0 + "ln2_offset"])
    put("lnm", v[f0 + "ln_mlp_scale"], v[f0 + "ln_mlp_offset"])
    put("l1q", v[f1 + "q_b"])
    put("l1k", kvb[:, 0])
    put("rms", v[f1 + "postnorm_w"], nil)
    put("l2n", v[f2 + "ln1_w"], v[f2 + "ln1_b"])
    put("l2q", v[f2 + "q_b"])
    put("l2k", v[f2 + "k_b"])
    put("l2m", v[f2 + "ln2_w"], v[f2 + "ln2_b"])
    put("fb0", v[f0 + "b_fc1"])
    put("fb1", v[f1 + "mlp_b1"])
    put("fb2", v[f2 + "fc_b"])
    put("one", one, nil)
    for name, w in (("bth", "btheta"), ("bph", "bphi"), ("bz", "bz"), ("gam", "gamma"), ("bet", "beta")):
        put(name, np.tile(v[f3 + w], 2)[:, None])
    p = np.arange(P)
    put("hmask", (p[:, None] // DH1 == np.arange(HPT)).astype(np.float32))
    put("even", (p // DH1 % 2 == 0).astype(np.float32)[:, None])
    put("odd", (p // DH1 % 2 == 1).astype(np.float32)[:, None])
    put("ident", np.eye(P, dtype=np.float32))

    def twice(w):
        z = np.zeros((2 * w.shape[0], 2 * w.shape[1]), np.float32)
        z[:w.shape[0], :w.shape[1]] = z[w.shape[0]:, w.shape[1]:] = w
        return z

    put("wth", twice(v[f3 + "Wtheta"].T))
    put("wph", twice(v[f3 + "Wphi"].T))
    put("wg", twice(v[f3 + "Wg"].T))
    put("wz", twice(v[f3 + "Wz"].T))

    bg = np.concatenate([v[f3 + "bg"], v[f3 + "bg"], np.zeros(D - 2 * CI, np.float32)])
    rows = np.concatenate([v[f0 + "bo1"], v[f0 + "bo2"], v[f0 + "b_fc2"], v[f1 + "out_b"], v[f1 + "mlp_b2"],
                           v[f2 + "cproj_b"], v[f2 + "proj_b"], kvb[:, 1], v[f2 + "v_b"], bg])
    ctx_tok = v["ctx_2048"].reshape(TILES, P, D)
    arrays = {
        "wpack": wpack, "ctxT": v["ctx_2048"].reshape(TOK, D).T, "ctx_tok": ctx_tok, "x_in": v["x"].reshape(TOK, D),
        "mask1": v["mask_BxS2_ik0"], "mask2": v["mask_BxS2_bf1"].view(np.uint8), "cols_in": consts,
        "rows_in": rows, "vb_in": vb,
    }
    arrays = {k: np.ascontiguousarray(a) for k, a in arrays.items()}
    nc = bacc.Bacc("TRN2", target_bir_lowering=False, num_devices=1)
    aps = {k: nc.dram_tensor(k, a.shape, mybir.dt.from_np(a.dtype), kind="ExternalInput").ap() for k, a in arrays.items()}
    out = nc.dram_tensor("out", (TOK, D), F32, kind="ExternalOutput").ap()
    spill = nc.dram_tensor("spill", (TOK, D), F32, kind="Internal").ap()
    build(nc, **aps, out=out, spill=spill)
    got = run_bass_kernel_spmd(nc, [arrays], core_ids=[0])
    return got.results[0]["out"].reshape(NB, SEQ, D)
```
